# Optimizing a Trainium2 kernel written in Bass

```python
import numpy as np
import jax
import jax.numpy as jnp

def _softmax(x, axis=-1):
    return jax.nn.softmax(x, axis=axis)

def _gelu(x):
    return jax.nn.gelu(x, approximate=True)

def _silu(x):
    return jax.nn.silu(x)

def _sigmoid(x):
    return jax.nn.sigmoid(x)

def _layernorm(x, axis=-1, eps=1e-05):
    m = jnp.mean(x, axis=axis, keepdims=True)
    v = jnp.var(x, axis=axis, keepdims=True)
    return (x - m) / jnp.sqrt(v + eps)

def _scatter_add(tgt, idx, src, axis=0):
    return tgt.at[idx].add(src)

def _segment_sum(src, seg, n):
    return jax.ops.segment_sum(src, seg, n)
kernel_name = 'mk_adj_ffn_d2_adj_r2_75583d'

def setup_inputs(seed: int=0):
    np.random.seed(seed)
    _w = jnp.asarray

    def _rec_inputs():
        import jax
        import jax.numpy as jnp
        _gk = jax.random.key(seed)
        x = -8.015e-05 + 0.9999 * jax.random.normal(jax.random.fold_in(_gk, 1), (128, 128, 128), jnp.float32)
        _a = jax.random.bernoulli(jax.random.fold_in(_gk, 2), 0.125, (128, 128, 128))
        _a = jnp.logical_or(_a, jnp.swapaxes(_a, -1, -2))
        _a = jnp.logical_or(_a, jnp.eye(128, dtype=bool))
        _af = _a.astype(jnp.float32)
        _af = _af * jax.random.uniform(jax.random.fold_in(_gk, 3), (128, 128, 128), jnp.float32, 0.05, 0.999837)
        adj = _af
        _nm = jnp.ones((128, 128), dtype=bool)
        nodemask = jnp.where(_nm, 1.0, 0.0).astype(jnp.float32)
        return (x, adj, nodemask)
    x, adj, nodemask = _rec_inputs()

    def _L0_gnn_setup():
        import jax, jax.numpy as jnp
        import numpy as np
        GROUPS = [list(range(25)), [0, 1, 2, 3, 4, 5, 6, 7, 8], [0, 9, 10, 11, 12, 13, 14], [6, 7, 8, 12, 13, 14], [3, 4, 5, 9, 10, 11]]
        B, N, D_IN, D_HID = (4096, 25, 128, 256)

        def _graph_conv(x, adj, W, b):
            n = adj.shape[-1]
            A = adj + jnp.eye(n, dtype=adj.dtype)
            deg = jnp.sum(A, axis=-1)
            deg_safe = jnp.where(deg == 0, 1.0, deg)
            dinv = jnp.where(deg == 0, 0.0, deg_safe ** (-0.5))
            norm_adj = dinv[:, :, None] * A * dinv[:, None, :]
            support = jnp.einsum('bnd,de->bne', x, W)
            out = jnp.einsum('bnm,bme->bne', norm_adj, support) + b
            return jax.nn.relu(out)
        key = jax.random.key(seed)
        ks = jax.random.split(key, 7)
        s1 = float(np.sqrt(6.0 / (D_IN + D_HID)))
        s2 = float(np.sqrt(6.0 / (D_HID + D_IN)))
        return {'x': jax.random.normal(ks[0], (B, N, D_IN), dtype=jnp.float32), 'adj': jax.random.uniform(ks[1], (B, N, N), dtype=jnp.float32), 'W1': jax.random.uniform(ks[2], (5, D_IN, D_HID), jnp.float32, -s1, s1), 'b1': jnp.zeros((5, D_HID), dtype=jnp.float32), 'W2': jax.random.uniform(ks[3], (5, D_HID, D_IN), jnp.float32, -s2, s2), 'b2': jnp.zeros((5, D_IN), dtype=jnp.float32), 'fusion_w': jnp.ones((5,), dtype=jnp.float32)}
    _L0_gnn_all = _L0_gnn_setup()
    _L0_gnn_in = {k: v for k, v in _L0_gnn_all.items() if k in ('W1', 'b1', 'W2', 'b2', 'fusion_w')}
    del _L0_gnn_all

    def _L0_ffn_setup():
        import jax, jax.numpy as jnp
        import numpy as np
        B, S, D, H, E, K = (8, 4096, 128, 512, 8, 2)
        key = jax.random.key(seed)
        ks = jax.random.split(key, 7)
        s_in = 1.0 / np.sqrt(D)
        s_hid = 1.0 / np.sqrt(H)
        return {'x': jax.random.normal(ks[0], (B, S, D), dtype=jnp.float32), 'Wg': jax.random.uniform(ks[1], (E, D), jnp.float32, -s_in, s_in), 'bg': jax.random.uniform(ks[2], (E,), jnp.float32, -s_in, s_in), 'W1': jax.random.uniform(ks[3], (E, H, D), jnp.float32, -s_in, s_in), 'b1': jax.random.uniform(ks[4], (E, H), jnp.float32, -s_in, s_in), 'W2': jax.random.uniform(ks[5], (E, D, H), jnp.float32, -s_hid, s_hid), 'b2': jax.random.uniform(ks[6], (E, D), jnp.float32, -s_hid, s_hid)}
    _L0_ffn_all = _L0_ffn_setup()
    _L0_ffn_in = {k: v for k, v in _L0_ffn_all.items() if k in ('Wg', 'bg', 'W1', 'b1', 'W2', 'b2')}
    del _L0_ffn_all

    def _L1_gnn_setup():
        import jax, jax.numpy as jnp
        import numpy as np
        EPS = 1e-08
        key = jax.random.key(seed)
        kH, kA, kW = jax.random.split(key, 3)
        B, N, IN, OUT = (32, 256, 128, 128)
        H = jax.random.normal(kH, (B, N, IN), dtype=jnp.float32)
        A = jax.random.uniform(kA, (B, N, N), dtype=jnp.float32)
        mask = jnp.ones((B, N), dtype=jnp.float32)
        W = jax.random.normal(kW, (OUT, IN), dtype=jnp.float32) * (1.0 / np.sqrt(IN))
        b = jnp.zeros((OUT,), dtype=jnp.float32)
        return {'H': H, 'A': A, 'mask': mask, 'W': W, 'b': b}
    _L1_gnn_all = _L1_gnn_setup()
    _L1_gnn_in = {k: v for k, v in _L1_gnn_all.items() if k in ('W', 'b')}
    del _L1_gnn_all

    def _L1_ffn_setup():
        import jax, jax.numpy as jnp
        import numpy as np
        B, A = (2048, 8)
        IN, OUT = (128, 128)
        SH1, SH2 = (128, 128)
        EH1, EH2 = (128, 64)
        E, TOPK = (4, 2)

        def _shared_mlp(x, W1, b1, W2, b2, W3, b3):
            h = jax.nn.relu(x @ W1 + b1)
            h = jax.nn.relu(h @ W2 + b2)
            return h @ W3 + b3

        def _experts_mlp(x, eW1, eb1, eW2, eb2, eW3, eb3):
            h = jax.nn.relu(jnp.einsum('baf,efh->ebah', x, eW1) + eb1[:, None, None, :])
            h = jax.nn.relu(jnp.einsum('ebah,ehg->ebag', h, eW2) + eb2[:, None, None, :])
            o = jnp.einsum('ebag,ego->ebao', h, eW3) + eb3[:, None, None, :]
            return jnp.moveaxis(o, 0, -1)
        key = jax.random.key(seed)
        ks = jax.random.split(key, 16)
        s = 0.05
        return {'x': jax.random.normal(ks[0], (B, A, IN), jnp.float32), 'sW1': jax.random.normal(ks[1], (IN, SH1), jnp.float32) * s, 'sb1': jnp.zeros((SH1,), jnp.float32), 'sW2': jax.random.normal(ks[2], (SH1, SH2), jnp.float32) * s, 'sb2': jnp.zeros((SH2,), jnp.float32), 'sW3': jax.random.normal(ks[3], (SH2, OUT), jnp.float32) * s, 'sb3': jnp.zeros((OUT,), jnp.float32), 'eW1': jax.random.normal(ks[4], (E, IN, EH1), jnp.float32) * s, 'eb1': jnp.zeros((E, EH1), jnp.float32), 'eW2': jax.random.normal(ks[5], (E, EH1, EH2), jnp.float32) * s, 'eb2': jnp.zeros((E, EH2), jnp.float32), 'eW3': jax.random.normal(ks[6], (E, EH2, OUT), jnp.float32) * s, 'eb3': jnp.zeros((E, OUT), jnp.float32), 'gW': jax.random.normal(ks[7], (IN, E), jnp.float32) * s, 'gb': jnp.zeros((E,), jnp.float32)}
    _L1_ffn_all = _L1_ffn_setup()
    _L1_ffn_in = {k: v for k, v in _L1_ffn_all.items() if k in ('sW1', 'sb1', 'sW2', 'sb2', 'sW3', 'sb3', 'eW1', 'eb1', 'eW2', 'eb2', 'eW3', 'eb3', 'gW', 'gb')}
    del _L1_ffn_all
    return {'x': x, 'adj': adj, 'nodemask': nodemask, 'L0_gnn_W1': _L0_gnn_in['W1'], 'L0_gnn_b1': _L0_gnn_in['b1'], 'L0_gnn_W2': _L0_gnn_in['W2'], 'L0_gnn_b2': _L0_gnn_in['b2'], 'L0_gnn_fusion_w': _L0_gnn_in['fusion_w'], 'L0_ffn_Wg': _L0_ffn_in['Wg'], 'L0_ffn_bg': _L0_ffn_in['bg'], 'L0_ffn_W1': _L0_ffn_in['W1'], 'L0_ffn_b1': _L0_ffn_in['b1'], 'L0_ffn_W2': _L0_ffn_in['W2'], 'L0_ffn_b2': _L0_ffn_in['b2'], 'L1_gnn_W': _L1_gnn_in['W'], 'L1_gnn_b': _L1_gnn_in['b'], 'L1_ffn_sW1': _L1_ffn_in['sW1'], 'L1_ffn_sb1': _L1_ffn_in['sb1'], 'L1_ffn_sW2': _L1_ffn_in['sW2'], 'L1_ffn_sb2': _L1_ffn_in['sb2'], 'L1_ffn_sW3': _L1_ffn_in['sW3'], 'L1_ffn_sb3': _L1_ffn_in['sb3'], 'L1_ffn_eW1': _L1_ffn_in['eW1'], 'L1_ffn_eb1': _L1_ffn_in['eb1'], 'L1_ffn_eW2': _L1_ffn_in['eW2'], 'L1_ffn_eb2': _L1_ffn_in['eb2'], 'L1_ffn_eW3': _L1_ffn_in['eW3'], 'L1_ffn_eb3': _L1_ffn_in['eb3'], 'L1_ffn_gW': _L1_ffn_in['gW'], 'L1_ffn_gb': _L1_ffn_in['gb']}

def reference(x, adj, nodemask, L0_gnn_W1, L0_gnn_b1, L0_gnn_W2, L0_gnn_b2, L0_gnn_fusion_w, L0_ffn_Wg, L0_ffn_bg, L0_ffn_W1, L0_ffn_b1, L0_ffn_W2, L0_ffn_b2, L1_gnn_W, L1_gnn_b, L1_ffn_sW1, L1_ffn_sb1, L1_ffn_sW2, L1_ffn_sb2, L1_ffn_sW3, L1_ffn_sb3, L1_ffn_eW1, L1_ffn_eb1, L1_ffn_eW2, L1_ffn_eb2, L1_ffn_eW3, L1_ffn_eb3, L1_ffn_gW, L1_ffn_gb):
    import jax
    import jax.numpy as jnp

    def _L0_gnn_ref(x, adj, W1, b1, W2, b2, fusion_w):
        import jax, jax.numpy as jnp
        import numpy as np
        GROUPS = [list(range(25)), [0, 1, 2, 3, 4, 5, 6, 7, 8], [0, 9, 10, 11, 12, 13, 14], [6, 7, 8, 12, 13, 14], [3, 4, 5, 9, 10, 11]]
        B, N, D_IN, D_HID = (4096, 25, 128, 256)

        def _graph_conv(x, adj, W, b):
            n = adj.shape[-1]
            A = adj + jnp.eye(n, dtype=adj.dtype)
            deg = jnp.sum(A, axis=-1)
            deg_safe = jnp.where(deg == 0, 1.0, deg)
            dinv = jnp.where(deg == 0, 0.0, deg_safe ** (-0.5))
            norm_adj = dinv[:, :, None] * A * dinv[:, None, :]
            support = jnp.einsum('bnd,de->bne', x, W)
            out = jnp.einsum('bnm,bme->bne', norm_adj, support) + b
            return jax.nn.relu(out)
        norm_w = jax.nn.softmax(fusion_w)
        fused = jnp.zeros_like(x)
        for g, idx_list in enumerate(GROUPS):
            idx = jnp.asarray(idx_list)
            x_g = x[:, idx, :]
            adj_g = adj[:, idx][:, :, idx]
            h = _graph_conv(x_g, adj_g, W1[g], b1[g])
            out_g = _graph_conv(h, adj_g, W2[g], b2[g])
            fused = fused.at[:, idx, :].add(norm_w[g] * out_g)
        return fused

    def _L0_ffn_ref(x, Wg, bg, W1, b1, W2, b2):
        import jax, jax.numpy as jnp
        import numpy as np
        B, S, D, H, E, K = (8, 4096, 128, 512, 8, 2)
        gate_scores = jnp.einsum('bsd,ed->bse', x, Wg) + bg
        topk_scores, topk_idx = jax.lax.top_k(gate_scores, K)
        topk_probs = jax.nn.softmax(topk_scores, axis=-1)
        combine = jnp.sum(topk_probs[..., None] * jax.nn.one_hot(topk_idx, E, dtype=x.dtype), axis=-2)
        out = jnp.zeros_like(x)
        for e in range(E):
            h = jax.nn.relu(jnp.einsum('bsd,hd->bsh', x, W1[e]) + b1[e])
            y = jnp.einsum('bsh,dh->bsd', h, W2[e]) + b2[e]
            out = out + combine[..., e:e + 1] * y
        return out

    def _L1_gnn_ref(H, A, mask, W, b):
        import jax, jax.numpy as jnp
        import numpy as np
        EPS = 1e-08
        N = A.shape[-1]
        A_hat = A + jnp.eye(N, dtype=A.dtype)
        deg = A_hat.sum(axis=-1)
        dis = (deg + EPS) ** (-0.5)
        A_norm = dis[:, :, None] * A_hat * dis[:, None, :]
        H_lin = jnp.einsum('bni,oi->bno', H, W) + b
        out = jnp.einsum('bnm,bmo->bno', A_norm, H_lin)
        out = out * mask[:, :, None]
        return jax.nn.relu(out)

    def _L1_ffn_ref(x, sW1, sb1, sW2, sb2, sW3, sb3, eW1, eb1, eW2, eb2, eW3, eb3, gW, gb):
        import jax, jax.numpy as jnp
        import numpy as np
        B, A = (2048, 8)
        IN, OUT = (128, 128)
        SH1, SH2 = (128, 128)
        EH1, EH2 = (128, 64)
        E, TOPK = (4, 2)

        def _shared_mlp(x, W1, b1, W2, b2, W3, b3):
            h = jax.nn.relu(x @ W1 + b1)
            h = jax.nn.relu(h @ W2 + b2)
            return h @ W3 + b3

        def _experts_mlp(x, eW1, eb1, eW2, eb2, eW3, eb3):
            h = jax.nn.relu(jnp.einsum('baf,efh->ebah', x, eW1) + eb1[:, None, None, :])
            h = jax.nn.relu(jnp.einsum('ebah,ehg->ebag', h, eW2) + eb2[:, None, None, :])
            o = jnp.einsum('ebag,ego->ebao', h, eW3) + eb3[:, None, None, :]
            return jnp.moveaxis(o, 0, -1)
        all_out = _experts_mlp(x, eW1, eb1, eW2, eb2, eW3, eb3)
        shared = _shared_mlp(x, sW1, sb1, sW2, sb2, sW3, sb3)
        gates = jax.nn.softmax(x @ gW + gb, axis=-1)
        topv, topi = jax.lax.top_k(gates, TOPK)
        topw = jax.nn.softmax(topv, axis=-1)
        sel = jnp.take_along_axis(all_out, topi[:, :, None, :], axis=-1)
        gated = jnp.sum(sel * topw[:, :, None, :], axis=-1)
        return shared + gated
    x = x + _L0_gnn_ref(_layernorm(x, axis=-1), adj, L0_gnn_W1, L0_gnn_b1, L0_gnn_W2, L0_gnn_b2, L0_gnn_fusion_w)
    x = x + _L0_ffn_ref(_layernorm(x, axis=-1), L0_ffn_Wg, L0_ffn_bg, L0_ffn_W1, L0_ffn_b1, L0_ffn_W2, L0_ffn_b2)
    x = x + _L1_gnn_ref(_layernorm(x, axis=-1), adj, nodemask, L1_gnn_W, L1_gnn_b)
    x = x + _L1_ffn_ref(_layernorm(x, axis=-1), L1_ffn_sW1, L1_ffn_sb1, L1_ffn_sW2, L1_ffn_sb2, L1_ffn_sW3, L1_ffn_sb3, L1_ffn_eW1, L1_ffn_eb1, L1_ffn_eW2, L1_ffn_eb2, L1_ffn_eW3, L1_ffn_eb3, L1_ffn_gW, L1_ffn_gb)
    return x

_drawn_inputs = setup_inputs


def setup_inputs(seed=0):
    import zlib

    import numpy as np

    out = dict(_drawn_inputs(seed))
    spreads = {'L0_gnn_b1': (0.0, 0.78),
     'L0_gnn_b2': (0.0, 0.595),
     'L0_gnn_fusion_w': (1.0, 0.6),
     'L1_gnn_b': (0.0, 0.1),
     'L1_ffn_sb1': (0.0, 0.583),
     'L1_ffn_sb2': (0.0, 0.1),
     'L1_ffn_sb3': (0.0, 0.1),
     'L1_ffn_eb1': (0.0, 0.8),
     'L1_ffn_eb2': (0.0, 0.469),
     'L1_ffn_eb3': (0.0, 0.1),
     'L1_ffn_gb': (0.0, 0.351)}
    factors = {'L0_ffn_b1': 3.538, 'L0_ffn_b2': 2.67}
    for name, (base, spread) in spreads.items():
        noise = np.random.default_rng([zlib.crc32(name.encode()), seed]).standard_normal(out[name].shape)
        drawn = base * np.exp(spread * noise) if base else spread * noise
        out[name] = jnp.asarray(drawn.astype(out[name].dtype))
    for name, factor in factors.items():
        out[name] = (out[name] * factor).astype(out[name].dtype)
    return out
```

```python
import numpy as np
import concourse.bass as bass
from concourse import mybir
from contextlib import ExitStack

F32 = mybir.dt.float32
F16 = mybir.dt.float16
I32 = mybir.dt.int32
ALU = mybir.AluOpType
ACT = mybir.ActivationFunctionType
AX = mybir.AxisListType

P = 128
B = 128
N = P
D = P
R = 4
W = R * P
GROUPS = [list(range(25)), [0, 1, 2, 3, 4, 5, 6, 7, 8], [0, 9, 10, 11, 12, 13, 14], [6, 7, 8, 12, 13, 14],
          [3, 4, 5, 9, 10, 11]]
GN = [len(g) for g in GROUPS]
GPT = [P // n for n in GN]
GB = [-(-(-(-B // k)) // R) for k in GPT]
GOFF = [sum(GN[:g]) for g in range(len(GROUPS))]
GR = sum(GN)
NGB = sum(GB)
GHID = 256
E0 = 8
H0 = 512
HC = H0 // P
TILE = 512
NT = (2 * B * N + E0 * (TILE - 1)) // TILE
NTP = NT + NT % 2
NCOL = NTP * R
EW = HC * P + HC * D + HC + 2
E1 = 4
GWID = GHID + 2 * D + 2 + D
BIG = -3.0e38


def consts():
    i = np.arange(P)
    ident = np.eye(P, dtype=np.float32)
    sel = np.zeros((GR, P), np.float32)
    for g, nodes in enumerate(GROUPS):
        for n, node in enumerate(nodes):
            sel[GOFF[g] + n, node] = 1
    before = (i[:, None] < i[None, :]).astype(np.float32)
    b8 = (np.arange(E0)[None, :] < np.arange(E0)[:, None]).astype(np.float32)
    cf = np.concatenate([
        ident,
        np.broadcast_to(np.arange(E0, 0, -1, dtype=np.float32), (P, E0)),
        np.broadcast_to(b8.reshape(1, -1), (P, E0 * E0)),
        np.broadcast_to(np.arange(P, dtype=np.float32), (P, P)),
        i[:, None].astype(np.float32),
        np.broadcast_to(np.arange(NTP, dtype=np.float32), (P, NTP)),
    ], axis=1)
    ch = np.concatenate([
        before, np.ones((P, P), np.float32),
        np.broadcast_to(np.arange(P, dtype=np.float32), (P, P)),
        np.broadcast_to(np.arange(NCOL, dtype=np.float32), (P, NCOL)),
    ], axis=1).astype(np.float16)
    selp = np.zeros((R * E1, R, 2, P), np.float32)
    for k in range(R):
        for e in range(E1):
            selp[k * E1 + e, k, e // 2, (e % 2) * 64:(e % 2) * 64 + 64] = 1
    return cf, ch, sel, selp


CF_ID, CF_PRI, CF_B8, CF_T, CF_P, CF_J = 0, P, P + E0, P + E0 + E0 * E0, 2 * P + E0 + E0 * E0, 2 * P + E0 + E0 * E0 + 1
CF_W = CF_J + NTP
CH_U, CH_1, CH_I, CH_H = 0, P, 2 * P, 3 * P
CH_W = 3 * P + NCOL


def build(nc, x_tok, x_grp, a_grp, w_grp, fus, wg, bg, w_exp, a_t, w_gcn, b_gcn, mask_t,
          w_s, b_s, e_w1, e_w2, e_w3, b_e, b_out, gw, gb, cf_d, ch_d, sel_d, selp_d, out):
    xln_d = nc.dram_tensor("xln_scratch", (B * N, D), F32, kind="Internal").ap()
    y_d = nc.dram_tensor("expert_rows_scratch", (NTP * TILE, D), F32, kind="Internal").ap()
    c_d = [nc.dram_tensor(f"group_rows_scratch{g}", (GB[g] * R * GPT[g] * GN[g], D), F32, kind="Internal").ap()
           for g in range(len(GROUPS))]

    top = ExitStack()
    with top:
        def alloc(ctx, name, shape, dt=F32):
            return ctx.enter_context(nc.sbuf_tensor(name, shape, dt))

        def bank(ctx, name, shape, dt=F32):
            return ctx.enter_context(nc.psum_tensor(name, shape, dt))

        def sem(name):
            return top.enter_context(nc.semaphore(name))

        def pair(name):
            return [sem(name + "_even"), sem(name + "_odd")]

        def turns(eng, n, body):
            body(0, 0, True, False)
            body(0, 1, True, True)
            with eng.Fori(2, n - 1, 2) as i:
                body(i, 0, True, True)
                body(i, 1, True, True)
            body(n, 0, False, True)

        xtok = alloc(top, "xtok", [P, B, D])
        cf = alloc(top, "cf", [P, CF_W])
        ch = alloc(top, "ch", [P, CH_W], F16)
        mhalf = alloc(top, "mhalf", [P, 2 * R])
        ident = cf[:, CF_ID:CF_ID + P]
        pos_i = alloc(top, "pos_i", [P, 2, B], I32)
        prob = alloc(top, "prob", [P, 2, B])
        ids = alloc(top, "ids", [P, NCOL], I32)
        texp = alloc(top, "texp", [P, NTP], I32)

        x_loaded = sem("x_loaded")
        half_set = sem("half_set")
        passed = sem("passed")

        with ExitStack() as ctx:
            xg = [alloc(ctx, f"xg{p}", [P, R, D]) for p in range(2)]
            ag = [alloc(ctx, f"ag{p}", [P, R, P]) for p in range(2)]
            wj = [alloc(ctx, f"wj{p}", [P, GWID]) for p in range(2)]
            ones = alloc(ctx, "ones", [P, 1])
            fw = alloc(ctx, "fw", [P, 5])
            fe = alloc(ctx, "fe", [P, 5])
            fm = alloc(ctx, "fm", [P, 4])
            wb = alloc(ctx, "wb", [P, NGB])
            st = [alloc(ctx, f"st{p}", [P, R, 6]) for p in range(2)]
            mv = [alloc(ctx, f"mv{p}", [P, R, 2]) for p in range(2)]
            pre = [alloc(ctx, f"pre{p}", [P, 2 * R]) for p in range(2)]
            root = [alloc(ctx, f"root{p}", [P, 2 * R]) for p in range(2)]
            nz = [alloc(ctx, f"nz{p}", [P, R]) for p in range(2)]
            dinv = [alloc(ctx, f"dinv{p}", [P, R]) for p in range(2)]
            dsc = [alloc(ctx, f"dsc{p}", [P, R]) for p in range(2)]
            wdi = [alloc(ctx, f"wdi{p}", [P, R]) for p in range(2)]
            xs = [alloc(ctx, f"xs{p}", [P, R, D]) for p in range(2)]
            ys = [alloc(ctx, f"ys{p}", [P, R, D]) for p in range(2)]
            yt = [alloc(ctx, f"yt{p}", [P, W]) for p in range(2)]
            ht = [alloc(ctx, f"ht{p}", [P, 2, W]) for p in range(2)]
            zs = [alloc(ctx, f"zs{p}", [P, R, D]) for p in range(2)]
            b2w = [alloc(ctx, f"b2w{p}", [P, D]) for p in range(2)]
            os_ = [alloc(ctx, f"os{p}", [P, R, D]) for p in range(2)]
            orl = [alloc(ctx, f"orl{p}", [P, R, D]) for p in range(2)]
            p_deg = bank(ctx, "p_deg", [P, 512])
            p_y = bank(ctx, "p_y", [P, R, D])
            p_t = bank(ctx, "p_t", [P, R, D])
            p_h = [bank(ctx, f"p_h{c}", [P, W]) for c in range(2)]
            p_z = bank(ctx, "p_z", [P, R, D])
            p_o = bank(ctx, "p_o", [P, R, D])

            c_loaded = sem("g_consts_loaded")
            loaded = pair("g_loaded")
            set_ = sem("g_set")
            fus_exp = sem("g_fus_exp")
            fus_s = sem("g_fus_steps")
            a_ready = sem("g_a_ready")
            deg_done = sem("g_deg_done")
            stat_s = sem("g_stat_s")
            mv_s = sem("g_mv_s")
            pre_s = sem("g_pre_s")
            pre_ready = sem("g_pre_ready")
            root_done = sem("g_root_done")
            dinv_s = sem("g_dinv_s")
            xs_ready = sem("g_xs_ready")
            y_done = sem("g_y_done")
            ys_ready = sem("g_ys_ready")
            t_done = sem("g_t_done")
            yt_ready = sem("g_yt_ready")
            h_done = sem("g_h_done")
            ht_ready = sem("g_ht_ready")
            z_done = sem("g_z_done")
            zs_ready = sem("g_zs_ready")
            o_done = sem("g_o_done")
            os_s = sem("g_os_s")
            os_ready = sem("g_os_ready")
            orl_ready = sem("g_orl_ready")
            stored = pair("g_stored")

            batch_of = [(g, b) for g in range(len(GROUPS)) for b in range(GB[g])]

            with nc.Block() as block:
                @block.sync
                def _(sp):
                    sp.dma_start(cf[:, :], cf_d).then_inc(c_loaded, 16)
                    sp.dma_start(ch[:, :], ch_d).then_inc(c_loaded, 16)
                    sp.dma_start(fw[:, :], fus).then_inc(c_loaded, 16)

                    def load(j):
                        sp.dma_start(xg[j % 2][:, :, :], x_grp[j]).then_inc(loaded[j % 2], 16)
                        sp.dma_start(ag[j % 2][:, :, :], a_grp[j]).then_inc(loaded[j % 2], 16)
                        sp.dma_start(wj[j % 2][:, :], w_grp[j]).then_inc(loaded[j % 2], 16)

                    load(0)
                    load(1)
                    for j, (g, b) in enumerate(batch_of):
                        if j % 2 == 0:
                            n = B * j // NGB, B * (j + 2) // NGB
                            sp.dma_start(xtok[:, n[0]:n[1], :], x_tok[:, n[0]:n[1], :]).then_inc(x_loaded, 16)
                        if j >= 1:
                            sp.wait_ge(orl_ready, j)
                            pg, pb = batch_of[j - 1]
                            rows = GPT[pg] * GN[pg]
                            dst = c_d[pg][pb * R * rows:(pb + 1) * R * rows, :].rearrange("(k r) d -> r k d", r=rows)
                            sp.dma_start(dst, orl[(j - 1) % 2][0:rows, :, :]).then_inc(stored[(j - 1) % 2], 16)
                            if j + 1 < NGB:
                                sp.wait_ge(o_done, j)
                                load(j + 1)
                    sp.wait_ge(orl_ready, NGB)
                    pg, pb = batch_of[-1]
                    rows = GPT[pg] * GN[pg]
                    dst = c_d[pg][pb * R * rows:(pb + 1) * R * rows, :].rearrange("(k r) d -> r k d", r=rows)
                    sp.dma_start(dst, orl[(NGB - 1) % 2][0:rows, :, :]).then_inc(stored[(NGB - 1) % 2], 16)
                    sp.wait_ge(stored[0], 16 * (NGB // 2) + 1)
                    sp.wait_ge(stored[1], 16 * (NGB // 2) + 1)
                    sp.wait_ge(x_loaded, 16 * (NGB // 2))

                @block.gpsimd
                def _(pool):
                    nc.gpsimd.memset(mhalf[:, :], -0.5).then_inc(half_set, 1)
                    pool.wait_ge(half_set, 1)
                    with pool.Fori(0, NGB - 1, 2) as i:
                        for p in range(2):
                            pool.wait_ge(pre_ready, i + p + 1)
                            nc.gpsimd.tensor_tensor(root[p][:, :], pre[p][:, :], mhalf[:, :], ALU.pow)\
                              .then_inc(root_done, 1)

                @block.scalar
                def _(act):
                    act.sem_inc(stored[0], 1)
                    act.sem_inc(stored[1], 1)
                    act.wait_ge(fus_s, 2)
                    nc.scalar.activation(fe[:, :], fe[:, :], ACT.Exp).then_inc(fus_exp, 1)

                    def body(i, p, front, back):
                        j = i + p
                        q = 1 - p
                        if back:
                            for c in range(2):
                                act.wait_ge(h_done, 2 * j + c - 1)
                                nc.scalar.activation(ht[q][:, c, :], p_h[c][:, :], ACT.Relu,
                                                     bias=wj[q][:, GHID + 2 * D + c:GHID + 2 * D + c + 1])\
                                  .then_inc(ht_ready, 1)
                        if front:
                            act.wait_ge(t_done, j + 1)
                            nc.scalar.activation(yt[p][:, :], p_t[:, :, :].rearrange("p r d -> p (r d)"), ACT.Copy)\
                              .then_inc(yt_ready, 1)
                        if back:
                            act.wait_ge(os_ready, j)
                            act.wait_ge(stored[q], 8 * i + 1 if p else 8 * i - 15)
                            nc.scalar.activation(orl[q][:, :, :], os_[q][:, :, :], ACT.Relu).then_inc(orl_ready, 1)

                    turns(act, NGB, body)

                @block.tensor
                def _(pe):
                    def body(i, p, front, back):
                        j = i + p
                        q = 1 - p
                        if front:
                            pe.wait_ge(a_ready, j + 1)
                            for k in range(R):
                                last = nc.tensor.matmul(p_deg[:, k:k + 1], ag[p][:, k, :], ones[:, :],
                                                        start=True, stop=True)
                            last.then_inc(deg_done, 1)
                        if back:
                            pe.wait_ge(yt_ready, j)
                            for c in range(2):
                                nc.tensor.matmul(p_h[c][:, :], wj[q][:, c * P:(c + 1) * P], yt[q][:, :],
                                                 start=True, stop=True).then_inc(h_done, 1)
                        if front:
                            pe.wait_ge(xs_ready, j + 1)
                            for k in range(R):
                                last = nc.tensor.matmul(p_y[:, k, :], ag[p][:, k, :], xs[p][:, k, :],
                                                        start=True, stop=True)
                            last.then_inc(y_done, 1)
                        if back:
                            pe.wait_ge(ht_ready, 2 * j)
                            for k in range(R):
                                for c in range(2):
                                    last = nc.tensor.matmul(p_z[:, k, :], ht[q][:, c, k * P:(k + 1) * P],
                                                            wj[q][:, GHID + c * D:GHID + (c + 1) * D],
                                                            start=(c == 0), stop=(c == 1))
                            last.then_inc(z_done, 1)
                        if front:
                            pe.wait_ge(ys_ready, j + 1)
                            for k in range(R):
                                last = nc.tensor.transpose(p_t[:, k, :], ys[p][:, k, :], ident)
                            last.then_inc(t_done, 1)
                        if back:
                            pe.wait_ge(zs_ready, j)
                            if not (isinstance(j, int) and j < 2):
                                pe.wait_ge(os_s, j - 1)
                            for k in range(R):
                                last = nc.tensor.matmul(p_o[:, k, :], ag[q][:, k, :], zs[q][:, k, :],
                                                        start=True, stop=True)
                            last.then_inc(o_done, 1)

                    pe.wait_ge(set_, 1)
                    pe.wait_ge(c_loaded, 48)
                    turns(pe, NGB, body)

                @block.vector
                def _(dve):
                    nc.vector.memset(ones[:, :], 1.0).then_inc(set_, 1)
                    dve.wait_ge(c_loaded, 48)
                    nc.vector.reduce_max(fm[:, 0:1], fw[:, :], AX.X).then_inc(fus_s, 1)
                    dve.wait_ge(fus_s, 1)
                    nc.vector.tensor_scalar(fe[:, :], fw[:, :], fm[:, 0:1], None, ALU.subtract).then_inc(fus_s, 1)
                    dve.wait_ge(fus_exp, 1)
                    nc.vector.reduce_sum(fm[:, 1:2], fe[:, :], AX.X).then_inc(fus_s, 1)
                    dve.wait_ge(fus_s, 3)
                    nc.vector.reciprocal(fm[:, 2:3], fm[:, 1:2]).then_inc(fus_s, 1)
                    dve.wait_ge(fus_s, 4)
                    nc.vector.tensor_scalar(fw[:, :], fe[:, :], fm[:, 2:3], None, ALU.mult).then_inc(fus_s, 1)
                    dve.wait_ge(fus_s, 5)
                    for g in range(len(GROUPS)):
                        a = sum(GB[:g])
                        last = nc.vector.tensor_copy(wb[:, a:a + GB[g]], fw[:, g:g + 1].to_broadcast([P, GB[g]]))
                    last.then_inc(fus_s, 1)
                    dve.wait_ge(fus_s, 6)

                    def body(i, p, front, back):
                        j = i + p
                        q = 1 - p
                        if front:
                            dve.wait_ge(loaded[p], 24 * i + 48)
                            nc.vector.tensor_tensor(ag[p][:, :, :], ag[p][:, :, :],
                                                    ident.unsqueeze(1).to_broadcast([P, R, P]), ALU.add)\
                              .then_inc(a_ready, 1)
                            for k in range(R):
                                last = nc.vector.bn_stats(st[p][:, k, :], xg[p][:, k, :])
                            last.then_inc(stat_s, 1)
                            dve.wait_ge(stat_s, j + 1)
                            dve.sem_inc(passed, 1)
                            for k in range(R):
                                last = nc.vector.bn_aggr(mv[p][:, k, :], st[p][:, k, :])
                            last.then_inc(mv_s, 1)
                            dve.wait_ge(mv_s, j + 1)
                            nc.vector.tensor_scalar(pre[p][:, 0:R], mv[p][:, :, 1], 1e-5, None, ALU.add)
                            dve.wait_ge(deg_done, j + 1)
                            nc.vector.tensor_scalar(nz[p][:, :], p_deg[:, 0:R], 0.0, None, ALU.is_equal)\
                              .then_inc(pre_s, 1)
                            dve.wait_ge(pre_s, j + 1)
                            nc.vector.tensor_tensor(pre[p][:, R:2 * R], p_deg[:, 0:R], nz[p][:, :], ALU.add)\
                              .then_inc(pre_ready, 1)
                        if front:
                            nc.vector.tensor_scalar(nz[p][:, :], nz[p][:, :], -1.0, 1.0, ALU.mult, ALU.add)\
                              .then_inc(dinv_s, 1)
                            dve.wait_ge(dinv_s, 4 * j + 1)
                            dve.wait_ge(root_done, j + 1)
                            nc.vector.tensor_tensor(dinv[p][:, :], nz[p][:, :], root[p][:, R:2 * R], ALU.mult)\
                              .then_inc(dinv_s, 1)
                            dve.wait_ge(dinv_s, 4 * j + 2)
                            nc.vector.tensor_tensor(dsc[p][:, :], dinv[p][:, :], root[p][:, 0:R], ALU.mult)\
                              .then_inc(dinv_s, 1)
                            nc.vector.tensor_scalar(wdi[p][:, :], dinv[p][:, :], wb[:, bass.ds(j, 1)], None, ALU.mult)
                            nc.vector.tensor_scalar(b2w[p][:, :], wj[p][:, GWID - D:GWID], wb[:, bass.ds(j, 1)],
                                                    None, ALU.mult).then_inc(dinv_s, 1)
                            dve.wait_ge(dinv_s, 4 * j + 4)
                            for k in range(R):
                                last = nc.vector.tensor_scalar(xs[p][:, k, :], xg[p][:, k, :], mv[p][:, k, 0:1],
                                                               dsc[p][:, k:k + 1], ALU.subtract, ALU.mult)
                            last.then_inc(xs_ready, 1)
                        if back:
                            dve.wait_ge(z_done, j)
                            nc.vector.tensor_tensor(zs[q][:, :, :], p_z[:, :, :],
                                                    dinv[q][:, :].unsqueeze(2).to_broadcast([P, R, D]), ALU.mult)\
                              .then_inc(zs_ready, 1)
                        if front:
                            dve.wait_ge(y_done, j + 1)
                            nc.vector.tensor_tensor(ys[p][:, :, :], p_y[:, :, :],
                                                    dinv[p][:, :].unsqueeze(2).to_broadcast([P, R, D]), ALU.mult)\
                              .then_inc(ys_ready, 1)
                        if back:
                            dve.wait_ge(o_done, j)
                            nc.vector.tensor_tensor(os_[q][:, :, :], p_o[:, :, :],
                                                    wdi[q][:, :].unsqueeze(2).to_broadcast([P, R, D]), ALU.mult)\
                              .then_inc(os_s, 1)
                            dve.wait_ge(os_s, j)
                            nc.vector.tensor_tensor(os_[q][:, :, :], os_[q][:, :, :],
                                                    b2w[q][:, :].unsqueeze(1).to_broadcast([P, R, D]), ALU.add)\
                              .then_inc(os_ready, 1)

                    turns(dve, NGB, body)

        lgp = top.enter_context(ExitStack())
        p_lg = bank(lgp, "p_lg", [P, B * E0])
        with ExitStack() as ctx:
            ct = [alloc(ctx, f"ct{p}", [GR, R, D]) for p in range(2)]
            sel = alloc(ctx, "sel", [GR, P])
            wgt = alloc(ctx, "wgt", [P, E0])
            st = [alloc(ctx, f"gst{p}", [P, R, 6]) for p in range(2)]
            mv = [alloc(ctx, f"gmv{p}", [P, R, 2]) for p in range(2)]
            pre = [alloc(ctx, f"gpre{p}", [P, R]) for p in range(2)]
            root = [alloc(ctx, f"groot{p}", [P, R]) for p in range(2)]
            xl = [alloc(ctx, f"xl{p}", [P, R, D]) for p in range(2)]
            xt = [alloc(ctx, f"gxt{p}", [P, W]) for p in range(2)]
            p_sel = [bank(ctx, f"p_sel{p}", [P, R, D]) for p in range(2)]
            p_t = bank(ctx, "p_gt", [P, R, D])
            NB = B // R
            c_loaded = sem("r_consts_loaded")
            loaded = pair("r_loaded")
            sel_done = sem("r_sel_done")
            x1_ready = sem("r_x1_ready")
            stat_s = sem("r_stat_s")
            mv_s = sem("r_mv_s")
            pre_ready = sem("r_pre_ready")
            root_done = sem("r_root_done")
            xl_ready = sem("r_xl_ready")
            t_done = sem("r_t_done")
            xt_ready = sem("r_xt_ready")
            stored = pair("r_stored")

            with nc.Block() as block:
                @block.sync
                def _(sp):
                    sp.dma_start(sel[:, :], sel_d).then_inc(c_loaded, 16)
                    sp.dma_start(wgt[:, :], wg).then_inc(c_loaded, 16)

                    def load(j, p):
                        for g in range(len(GROUPS)):
                            src = c_d[g][0:B * GN[g], :].rearrange("(b n) d -> n b d", n=GN[g])
                            sp.dma_start(ct[p][GOFF[g]:GOFF[g] + GN[g], :, :], src[:, bass.ds(R * j, R), :])\
                              .then_inc(loaded[p], 16)

                    def store(j, p):
                        sp.wait_ge(xl_ready, j + 1)
                        sp.dma_start(xln_d.rearrange("(b n) d -> n b d", n=N)[:, bass.ds(R * j, R), :],
                                     xl[p][:, :, :]).then_inc(stored[p], 16)

                    load(0, 0)
                    load(1, 1)
                    with sp.Fori(0, NB - 3, 2) as i:
                        for p in range(2):
                            sp.wait_ge(sel_done, i + p + 1)
                            load(i + p + 2, p)
                            store(i + p, p)
                    store(NB - 2, 0)
                    store(NB - 1, 1)
                    for p in range(2):
                        sp.wait_ge(stored[p], 8 * NB + 1)

                @block.gpsimd
                def _(pool):
                    with pool.Fori(0, NB - 1, 2) as i:
                        for p in range(2):
                            pool.wait_ge(pre_ready, i + p + 1)
                            nc.gpsimd.tensor_tensor(root[p][:, :], pre[p][:, :], mhalf[:, 0:R], ALU.pow)\
                              .then_inc(root_done, 1)

                @block.scalar
                def _(act):
                    def body(i, p, front, back):
                        j = i + p
                        if back:
                            act.wait_ge(t_done, j)
                            nc.scalar.activation(xt[1 - p][:, :], p_t[:, :, :].rearrange("p r d -> p (r d)"), ACT.Copy)\
                              .then_inc(xt_ready, 1)

                    turns(act, NB, body)

                @block.tensor
                def _(pe):
                    def body(i, p, front, back):
                        j = i + p
                        q = 1 - p
                        if front:
                            pe.wait_ge(loaded[p], 40 * i + 80)
                            if not (isinstance(j, int) and j < 2):
                                pe.wait_ge(x1_ready, j - 1)
                            nc.tensor.matmul(p_sel[p][:, :, :].rearrange("p r d -> p (r d)"), sel[:, :],
                                             ct[p][:, :, :].rearrange("p r d -> p (r d)"),
                                             start=True, stop=True).then_inc(sel_done, 1)
                        if back:
                            pe.wait_ge(xl_ready, j)
                            for k in range(R):
                                last = nc.tensor.transpose(p_t[:, k, :], xl[q][:, k, :], ident)
                            last.then_inc(t_done, 1)
                            pe.wait_ge(xt_ready, j)
                            for k in range(R):
                                nc.tensor.matmul(p_lg[:, bass.ds((j - 1) * (R * E0) + k * E0, E0)],
                                                 xt[q][:, k * P:(k + 1) * P], wgt[:, :],
                                                 start=True, stop=True)

                    pe.wait_ge(c_loaded, 32)
                    turns(pe, NB, body)

                @block.vector
                def _(dve):
                    dve.sem_inc(stored[0], 1)
                    dve.sem_inc(stored[1], 1)

                    def body(i, p, front, back):
                        j = i + p
                        q = 1 - p
                        if front:
                            rows = xtok[:, bass.ds(R * j, R), :]
                            dve.wait_ge(sel_done, j + 1)
                            nc.vector.tensor_tensor(rows, rows, p_sel[p][:, :, :], ALU.add).then_inc(x1_ready, 1)
                        if back:
                            dve.wait_ge(root_done, j)
                            dve.wait_ge(stored[q], 8 * i + 1 if p else 8 * i - 15)
                            for k in range(R):
                                last = nc.vector.tensor_scalar(xl[q][:, k, :], xtok[:, bass.ds(R * (j - 1) + k, 1), :],
                                                               mv[q][:, k, 0:1], root[q][:, k:k + 1],
                                                               ALU.subtract, ALU.mult)
                            last.then_inc(xl_ready, 1)
                        if front:
                            dve.wait_ge(x1_ready, j + 1)
                            dve.sem_inc(passed, 1)
                            for k in range(R):
                                last = nc.vector.bn_stats(st[p][:, k, :], xtok[:, bass.ds(R * j + k, 1), :])
                            last.then_inc(stat_s, 1)
                            dve.wait_ge(stat_s, j + 1)
                            dve.sem_inc(passed, 1)
                            for k in range(R):
                                last = nc.vector.bn_aggr(mv[p][:, k, :], st[p][:, k, :])
                            last.then_inc(mv_s, 1)
                            dve.wait_ge(mv_s, j + 1)
                            nc.vector.tensor_scalar(pre[p][:, :], mv[p][:, :, 1], 1e-5, None, ALU.add)\
                              .then_inc(pre_ready, 1)

                    turns(dve, NB, body)

        with ExitStack() as ctx:
            lg = alloc(ctx, "lg", [P, B, E0])
            bgs = alloc(ctx, "bgs", [P, E0])
            wide = alloc(ctx, "wide", [P, B, E0])
            mask = [alloc(ctx, f"mask{k}", [P, B, E0]) for k in range(2)]
            top_s = [alloc(ctx, f"top_s{k}", [P, B]) for k in range(2)]
            pm = alloc(ctx, "pm", [P, B])
            dif = alloc(ctx, "dif", [P, B])
            mb = alloc(ctx, "mb", [P, B, E0], F16)
            tot = alloc(ctx, "tot", [P, E0], F16)
            tu = alloc(ctx, "tu", [P, E0, B], F16)
            cnt_i = alloc(ctx, "cnt_i", [P, E0], I32)
            ntl = alloc(ctx, "ntl", [P, E0])
            b8 = alloc(ctx, "b8", [P, E0, E0])
            base = alloc(ctx, "base", [P, E0])
            end = alloc(ctx, "end", [P, E0])
            base_r = alloc(ctx, "base_r", [P, E0])
            posf = alloc(ctx, "posf", [P, E0, B])
            pos_f = alloc(ctx, "pos_f", [P, 2, B])
            lo_i = alloc(ctx, "lo_i", [P, 2, B], I32)
            hi_i = alloc(ctx, "hi_i", [P, 2, B], I32)
            lo_f = alloc(ctx, "lo_f", [P, 2, B])
            hi_f = alloc(ctx, "hi_f", [P, 2, B])
            tge = alloc(ctx, "tge", [P, NTP, E0])
            tex = alloc(ctx, "tex", [P, NTP])
            lp = [alloc(ctx, f"lp{k}", [P, P], F16) for k in range(4)]
            lt = [alloc(ctx, f"lt{k}", [P, P], F16) for k in range(4)]
            hh = [alloc(ctx, f"hh{k}", [P, NCOL], F16) for k in range(4)]
            zero = alloc(ctx, "zero", [P, NCOL], F16)
            idf = alloc(ctx, "idf", [P, NCOL])
            p_rank = bank(ctx, "p_rank", [P, E0, B])
            p_tot = bank(ctx, "p_tot", [P, 512])
            p_cnt = bank(ctx, "p_cnt", [P, 512])
            p_ip = bank(ctx, "p_ip", [P, 512])
            p_it = bank(ctx, "p_it", [P, 512])

            c_loaded = sem("s_consts_loaded")
            s = sem("s_steps")
            dif_ready = sem("s_dif_ready")
            exp_done = sem("s_exp_done")
            mb_ready = sem("s_mb_ready")
            tot_done = sem("s_tot_done")
            tot_ready = sem("s_tot_ready")
            tu_ready = sem("s_tu_ready")
            cnt_done = sem("s_cnt_done")
            rank_done = sem("s_rank_done")
            zero_set = sem("s_zero_set")
            hot_ready = sem("s_hot_ready")
            hot_used = sem("s_hot_used")
            ids_done = sem("s_ids_done")

            with nc.Block() as block:
                @block.sync
                def _(sp):
                    sp.dma_start(bgs[:, :], bg).then_inc(c_loaded, 16)

                @block.gpsimd
                def _(pool):
                    nc.gpsimd.memset(zero[:, :], 0.0).then_inc(zero_set, 1)

                @block.scalar
                def _(act):
                    act.wait_ge(dif_ready, 1)
                    nc.scalar.activation(dif[:, :], dif[:, :], ACT.Exp).then_inc(exp_done, 1)

                @block.tensor
                def _(pe):
                    ones16 = ch[:, CH_1:CH_1 + P]
                    pe.wait_ge(mb_ready, 1)
                    for e in range(E0):
                        last = nc.tensor.matmul(p_tot[:, e:e + 1], mb[:, :, e], ones16[:, 0:1], start=True, stop=True)
                    last.then_inc(tot_done, 1)
                    pe.wait_ge(tot_ready, 1)
                    nc.tensor.matmul(p_cnt[:, 0:E0], ones16, tot[:, :], start=True, stop=True).then_inc(cnt_done, 1)
                    pe.wait_ge(tu_ready, 1)
                    for h in range(2):
                        e = slice(h * E0 // 2, (h + 1) * E0 // 2)
                        nc.tensor.matmul(p_rank[:, e, :], ch[:, CH_U:CH_U + P],
                                         mb[:, :, e].rearrange("p b e -> p e b"), start=True, stop=False)
                        nc.tensor.matmul(p_rank[:, e, :], ones16, tu[:, e, :], start=False, stop=True)\
                          .then_inc(rank_done, 1)
                    pe.wait_ge(zero_set, 1)
                    for acc in (p_ip, p_it):
                        nc.tensor.matmul(acc[:, 0:NCOL], ch[:, CH_U:CH_U + P], zero[:, :], start=True, stop=False)
                    with pe.Fori(0, B - 1, 2) as i:
                        for p in range(2):
                            pe.wait_ge(hot_ready, i + p + 1)
                            for k in range(2):
                                nc.tensor.matmul(p_ip[:, 0:NCOL], lp[2 * p + k][:, :], hh[2 * p + k][:, :],
                                                 start=False, stop=False)
                                last = nc.tensor.matmul(p_it[:, 0:NCOL], lt[2 * p + k][:, :], hh[2 * p + k][:, :],
                                                        start=False, stop=False)
                            last.then_inc(hot_used, 1)
                    for acc in (p_ip, p_it):
                        nc.tensor.matmul(acc[:, 0:NCOL], ch[:, CH_U:CH_U + P], zero[:, :], start=False, stop=True)\
                          .then_inc(ids_done, 1)

                @block.vector
                def _(dve):
                    count = [0]

                    def step(ins):
                        count[0] += 1
                        ins.then_inc(s, 1)
                        dve.wait_ge(s, count[0])

                    pri = cf[:, CF_PRI:CF_PRI + E0].unsqueeze(1).to_broadcast([P, B, E0])
                    flat = lambda t: t[:, :, :].rearrange("p b e -> p (b e)")
                    dve.wait_ge(c_loaded, 16)
                    h = B // 2
                    nc.vector.tensor_tensor(lg[:, 0:h, :], p_lg[:, 0:h * E0].rearrange("p (b e) -> p b e", e=E0),
                                            bgs[:, :].unsqueeze(1).to_broadcast([P, h, E0]), ALU.add)
                    step(nc.vector.tensor_tensor(lg[:, h:B, :],
                                                 p_lg[:, h * E0:B * E0].rearrange("p (b e) -> p b e", e=E0),
                                                 bgs[:, :].unsqueeze(1).to_broadcast([P, h, E0]), ALU.add))
                    src = lg
                    for k in range(2):
                        step(nc.vector.tensor_reduce(top_s[k][:, :], src[:, :, :], AX.X, ALU.max))
                        step(nc.vector.tensor_tensor(wide[:, :, :], src[:, :, :],
                                                     top_s[k][:, :].unsqueeze(2).to_broadcast([P, B, E0]),
                                                     ALU.is_equal))
                        step(nc.vector.tensor_tensor(wide[:, :, :], wide[:, :, :], pri, ALU.mult))
                        step(nc.vector.tensor_reduce(pm[:, :], wide[:, :, :], AX.X, ALU.max))
                        step(nc.vector.tensor_tensor(mask[k][:, :, :], wide[:, :, :],
                                                     pm[:, :].unsqueeze(2).to_broadcast([P, B, E0]), ALU.is_equal))
                        if k == 0:
                            step(nc.vector.scalar_tensor_tensor(flat(lg), flat(mask[0]), BIG, flat(lg),
                                                                ALU.mult, ALU.add))
                    nc.vector.tensor_tensor(mb[:, :, :], mask[0][:, :, :], mask[1][:, :, :], ALU.add)\
                      .then_inc(mb_ready, 1)
                    nc.vector.tensor_tensor(dif[:, :], top_s[1][:, :], top_s[0][:, :], ALU.subtract)\
                      .then_inc(dif_ready, 1)
                    dve.wait_ge(tot_done, 1)
                    nc.vector.tensor_copy(tot[:, :], p_tot[:, 0:E0]).then_inc(tot_ready, 1)
                    nc.vector.tensor_tensor(tu[:, :, :], p_tot[:, 0:E0].unsqueeze(2).to_broadcast([P, E0, B]),
                                            ch[:, CH_U:CH_U + P].unsqueeze(1).to_broadcast([P, E0, B]), ALU.mult)\
                      .then_inc(tu_ready, 1)
                    dve.wait_ge(cnt_done, 1)
                    step(nc.vector.tensor_scalar(cnt_i[:, :], p_cnt[:, 0:E0], float(TILE - 1), None, ALU.add))
                    step(nc.vector.tensor_single_scalar(cnt_i[:, :], cnt_i[:, :], TILE.bit_length() - 1,
                                                        ALU.logical_shift_right))
                    step(nc.vector.tensor_copy(ntl[:, :], cnt_i[:, :]))
                    step(nc.vector.tensor_tensor(b8[:, :, :], ntl[:, :].unsqueeze(1).to_broadcast([P, E0, E0]),
                                                 cf[:, CF_B8:CF_B8 + E0 * E0].rearrange("p (a b) -> p a b", b=E0),
                                                 ALU.mult))
                    step(nc.vector.tensor_reduce(base[:, :], b8[:, :, :], AX.X, ALU.add))
                    nc.vector.tensor_tensor(end[:, :], base[:, :], ntl[:, :], ALU.add)
                    step(nc.vector.tensor_scalar(base_r[:, :], base[:, :], float(TILE), None, ALU.mult))
                    step(nc.vector.tensor_tensor(tge[:, :, :],
                                                 cf[:, CF_J:CF_J + NTP].unsqueeze(2).to_broadcast([P, NTP, E0]),
                                                 end[:, :].unsqueeze(1).to_broadcast([P, NTP, E0]), ALU.is_ge))
                    step(nc.vector.tensor_reduce(tex[:, :], tge[:, :, :], AX.X, ALU.add))
                    step(nc.vector.tensor_scalar(texp[:, :], tex[:, :], float(E0 - 1), None, ALU.min))
                    for hb in range(2):
                        dve.wait_ge(rank_done, hb + 1)
                        e = slice(hb * E0 // 2, (hb + 1) * E0 // 2)
                        step(nc.vector.tensor_tensor(posf[:, e, :], p_rank[:, e, :],
                                                     base_r[:, e].unsqueeze(2).to_broadcast([P, E0 // 2, B]), ALU.add))
                    for k in range(2):
                        step(nc.vector.tensor_tensor(wide[:, :, :], mask[k][:, :, :],
                                                     posf[:, :, :].rearrange("p e b -> p b e"), ALU.mult))
                        step(nc.vector.tensor_reduce(pos_f[:, k, :], wide[:, :, :], AX.X, ALU.add))
                    step(nc.vector.tensor_copy(pos_i[:, :, :], pos_f[:, :, :]))
                    nc.vector.tensor_single_scalar(lo_i[:, :, :], pos_i[:, :, :], P - 1, ALU.bitwise_and)
                    step(nc.vector.tensor_single_scalar(hi_i[:, :, :], pos_i[:, :, :], P.bit_length() - 1,
                                                        ALU.logical_shift_right))
                    nc.vector.tensor_copy(lo_f[:, :, :], lo_i[:, :, :])
                    step(nc.vector.tensor_copy(hi_f[:, :, :], hi_i[:, :, :]))
                    dve.wait_ge(exp_done, 1)
                    step(nc.vector.tensor_scalar(pm[:, :], dif[:, :], 1.0, None, ALU.add))
                    step(nc.vector.reciprocal(prob[:, 0, :], pm[:, :]))
                    step(nc.vector.tensor_tensor(prob[:, 1, :], dif[:, :], prob[:, 0, :], ALU.mult))

                    iota = ch[:, CH_I:CH_I + P]
                    iota_h = ch[:, CH_H:CH_H + NCOL]

                    def one_hots(j, p):
                        for k in range(2):
                            m = 2 * p + k
                            nc.vector.tensor_scalar(lp[m][:, :], iota, lo_f[:, k, bass.ds(j, 1)],
                                                    cf[:, CF_P:CF_P + 1], ALU.is_equal, ALU.mult)
                            nc.vector.tensor_scalar(lt[m][:, :], iota, lo_f[:, k, bass.ds(j, 1)],
                                                    cf[:, bass.ds(j + CF_T, 1)], ALU.is_equal, ALU.mult)
                            last = nc.vector.tensor_scalar(hh[m][:, :], iota_h, hi_f[:, k, bass.ds(j, 1)], None,
                                                           ALU.is_equal)
                        last.then_inc(hot_ready, 1)

                    one_hots(0, 0)
                    one_hots(1, 1)
                    with dve.Fori(2, B - 1, 2) as i:
                        for p in range(2):
                            dve.wait_ge(hot_used, i + p - 1)
                            one_hots(i + p, p)
                    dve.wait_ge(ids_done, 2)
                    step(nc.vector.tensor_scalar(idf[:, :], p_it[:, 0:NCOL], float(P), None, ALU.mult))
                    step(nc.vector.tensor_tensor(idf[:, :], idf[:, :], p_ip[:, 0:NCOL], ALU.add))
                    step(nc.vector.tensor_copy(ids[:, :], idf[:, :]))
        lgp.close()

        with ExitStack() as ctx:
            wall = alloc(ctx, "wall", [P, E0, EW])
            wc = [alloc(ctx, f"wc{p}", [P, EW]) for p in range(2)]
            xg = [alloc(ctx, f"exg{p}", [P, R, D]) for p in range(2)]
            xt = [alloc(ctx, f"ext{p}", [P, W]) for p in range(2)]
            ht = [alloc(ctx, f"eht{p}", [P, HC, W]) for p in range(2)]
            yt = [alloc(ctx, f"eyt{p}", [P, W]) for p in range(2)]
            yo = [alloc(ctx, f"eyo{p}", [P, R, D]) for p in range(2)]
            idx = [alloc(ctx, f"eidx{p}", [P, R], I32) for p in range(2)]
            p_x = bank(ctx, "p_ex", [P, R, D])
            p_h = [bank(ctx, f"p_eh{c}", [P, W]) for c in range(HC)]
            p_y = [bank(ctx, f"p_ey{p}", [P, W]) for p in range(2)]
            p_yo = bank(ctx, "p_eyo", [P, R, D])
            w1 = lambda p, c: wc[p][:, c * P:(c + 1) * P]
            w2 = lambda p, c: wc[p][:, H0 + c * D:H0 + (c + 1) * D]
            CB1 = H0 + HC * D

            w_loaded = sem("e_w_loaded")
            wc_ready = sem("e_wc_ready")
            gathered = pair("e_gathered")
            idx_ready = sem("e_idx_ready")
            x_done = sem("e_x_done")
            xt_ready = sem("e_xt_ready")
            h_done = sem("e_h_done")
            ht_ready = sem("e_ht_ready")
            y_done = sem("e_y_done")
            yt_ready = sem("e_yt_ready")
            yo_done = sem("e_yo_done")
            yo_ready = sem("e_yo_ready")
            stored = pair("e_stored")

            with nc.Block() as block:
                @block.sync
                def _(sp):
                    sp.dma_start(wall[:, :, :], w_exp).then_inc(w_loaded, 16)
                    dst = y_d.rearrange("(t p) d -> p t d", p=P)
                    with sp.Fori(0, NTP - 1, 2) as i:
                        for p in range(2):
                            sp.wait_ge(yo_ready, i + p + 1)
                            sp.dma_start(dst[:, bass.ds((i + p) * R, R), :], yo[p][:, :, :]).then_inc(stored[p], 16)
                    for p in range(2):
                        sp.wait_ge(stored[p], 8 * NTP + 1)

                @block.gpsimd
                def _(pool):
                    def gather(j, p):
                        nc.gpsimd.tensor_copy(idx[p][:, :], ids[:, bass.ds(j * R, R)]).then_inc(idx_ready, 1)
                        pool.wait_ge(idx_ready, j + 1)
                        pool.sem_inc(passed, 1)
                        for k in range(R):
                            pool.indirect_dma_start(
                                out=xg[p][:, k, :], out_offset=None, in_=xln_d,
                                in_offset=bass.IndirectOffsetOnAxis(ap=idx[p][:, k:k + 1], axis=0))\
                                .then_inc(gathered[p], 16)

                    gather(0, 0)
                    gather(1, 1)
                    with pool.Fori(2, NTP - 1, 2) as i:
                        for p in range(2):
                            pool.wait_ge(x_done, i + p - 1)
                            gather(i + p, p)

                @block.scalar
                def _(act):
                    def evacuate(j, p):
                        act.wait_ge(x_done, j + 1)
                        nc.scalar.activation(xt[p][:, :], p_x[:, :, :].rearrange("p r d -> p (r d)"), ACT.Copy)\
                          .then_inc(xt_ready, 1)

                    def hidden(j, p):
                        for c in range(HC):
                            act.wait_ge(h_done, HC * j + c + 1)
                            nc.scalar.activation(ht[p][:, c, :], p_h[c][:, :], ACT.Relu,
                                                 bias=wc[p][:, CB1 + c:CB1 + c + 1]).then_inc(ht_ready, 1)

                    evacuate(0, 0)
                    with act.Fori(0, NTP - 3, 2) as i:
                        for p in range(2):
                            hidden(i + p, p)
                            evacuate(i + p + 1, 1 - p)
                    hidden(NTP - 2, 0)
                    evacuate(NTP - 1, 1)
                    hidden(NTP - 1, 1)

                @block.tensor
                def _(pe):
                    def transpose_x(j, p, half):
                        pe.wait_ge(gathered[p], half * 16 * R + 16 * R)
                        for k in range(R):
                            last = nc.tensor.transpose(p_x[:, k, :], xg[p][:, k, :], ident)
                        last.then_inc(x_done, 1)

                    def up(j, p, c):
                        nc.tensor.matmul(p_h[c][:, :], w1(p, c), xt[p][:, :], start=True, stop=True).then_inc(h_done, 1)

                    def down(j, p, c):
                        pe.wait_ge(ht_ready, HC * j + c + 1)
                        last = nc.tensor.matmul(p_y[p][:, :], w2(p, c), ht[p][:, c, :], start=(c == 0),
                                                stop=(c == HC - 1))
                        if c == HC - 1:
                            last.then_inc(y_done, 1)

                    def transpose_y(j, p):
                        pe.wait_ge(yt_ready, j + 1)
                        for k in range(R):
                            last = nc.tensor.transpose(p_yo[:, k, :], yt[p][:, k * P:(k + 1) * P], ident)
                        last.then_inc(yo_done, 1)

                    def turn(i, p, after, before):
                        j = i + p
                        pe.wait_ge(wc_ready, j + 1)
                        pe.wait_ge(xt_ready, j + 1)
                        up(j, p, 0)
                        up(j, p, 1)
                        down(j, p, 0)
                        up(j, p, 2)
                        down(j, p, 1)
                        up(j, p, 3)
                        if after:
                            if isinstance(i, int):
                                transpose_x(j + 1, 1 - p, (j + 1) // 2)
                            else:
                                pe.wait_ge(gathered[1 - p], (i + 2 * p) * (8 * R) + 16 * R)
                                for k in range(R):
                                    last = nc.tensor.transpose(p_x[:, k, :], xg[1 - p][:, k, :], ident)
                                last.then_inc(x_done, 1)
                        down(j, p, 2)
                        if before:
                            transpose_y(j - 1, 1 - p)
                        down(j, p, 3)

                    transpose_x(0, 0, 0)
                    turn(0, 0, True, False)
                    turn(0, 1, True, True)
                    with pe.Fori(2, NTP - 3, 2) as i:
                        turn(i, 0, True, True)
                        turn(i, 1, True, True)
                    turn(NTP - 2, 0, True, True)
                    turn(NTP - 2, 1, False, True)
                    transpose_y(NTP - 1, 1)

                @block.vector
                def _(dve):
                    dve.sem_inc(stored[0], 1)
                    dve.sem_inc(stored[1], 1)

                    def take(j, p):
                        e = dve.value_load(texp[0:1, bass.ds(j, 1)], min_val=0, max_val=E0 - 1)
                        nc.vector.tensor_copy(wc[p][:, :], wall[:, bass.ds(e, 1), :].rearrange("p a w -> p (a w)"))\
                          .then_inc(wc_ready, 1)

                    def rows(i, p):
                        j = i + p
                        dve.wait_ge(y_done, j + 1)
                        nc.vector.tensor_scalar(yt[p][:, :], p_y[p][:, :], wc[p][:, CB1 + HC:CB1 + HC + 1], None,
                                                ALU.add).then_inc(yt_ready, 1)

                    def turned(i, p):
                        j = i + p
                        dve.wait_ge(yo_done, j + 1)
                        dve.wait_ge(stored[p], 8 * i + 1)
                        nc.vector.tensor_copy(yo[p][:, :, :], p_yo[:, :, :]).then_inc(yo_ready, 1)

                    dve.wait_ge(w_loaded, 16)
                    take(0, 0)
                    take(1, 1)
                    with dve.Fori(0, NTP - 3, 2) as i:
                        for p in range(2):
                            rows(i, p)
                            dve.wait_ge(yt_ready, i + p + 1)
                            take(i + p + 2, p)
                            turned(i, p)
                    for p in range(2):
                        rows(NTP - 2, p)
                        turned(NTP - 2, p)

        with ExitStack() as ctx:
            NB = B // R
            wgcn = alloc(ctx, "wgcn", [P, D])
            bgcn = alloc(ctx, "bgcn", [P, D])
            maskt = alloc(ctx, "maskt", [P, B])
            ws = alloc(ctx, "ws", [P, 3 * P])
            bs = alloc(ctx, "bs", [P, 2])
            w1 = alloc(ctx, "w1", [P, E1, P])
            w2 = alloc(ctx, "w2", [P, E1, P // 2])
            w3 = alloc(ctx, "w3", [P, 2, D])
            be = alloc(ctx, "be", [P, E1 + 2])
            bout = alloc(ctx, "bout", [R * E1 + 1, R, D])
            gws = alloc(ctx, "gws", [P, E1])
            gbs = alloc(ctx, "gbs", [P, E1])
            selp = alloc(ctx, "selp", [R * E1, R, 2, P])
            ones = alloc(ctx, "ones_l", [P, 1])
            at = [alloc(ctx, f"at{p}", [P, R, P]) for p in range(2)]
            yg = [alloc(ctx, f"yg{p}", [P, 2, R, D]) for p in range(2)]
            idx = [alloc(ctx, f"idx{p}", [P, 2, R], I32) for p in range(2)]
            st = alloc(ctx, "st_l", [P, R, 6])
            mv = alloc(ctx, "mv_l", [P, R, 2])
            pre = [alloc(ctx, f"pre_l{k}", [P, 2 * R]) for k in range(2)]
            root = [alloc(ctx, f"root_l{k}", [P, 2 * R]) for k in range(2)]
            rd = alloc(ctx, "rd", [P, R])
            dm = alloc(ctx, "dm", [P, R])
            xn = [alloc(ctx, f"xn{k}", [P, R, D]) for k in range(2)]
            x3t = alloc(ctx, "x3t", [P, W])
            x4t = alloc(ctx, "x4t", [P, W])
            gg = alloc(ctx, "gg", [P, R, D])
            gr = alloc(ctx, "gr", [P, R, D])
            hs = [alloc(ctx, f"hs{k}", [P, W]) for k in range(2)]
            he = [alloc(ctx, f"he{e}", [P, W]) for e in range(E1)]
            rp = [alloc(ctx, f"rp{k}", [P, W]) for k in range(2)]
            rc = [alloc(ctx, f"rc{k}", [P, W]) for k in range(2)]
            cw = alloc(ctx, "cw", [P, R, E1])
            cwt = alloc(ctx, "cwt", [R * E1 + 1, P])
            outx = [alloc(ctx, f"outx{p}", [P, R, D]) for p in range(2)]
            sm = [alloc(ctx, f"sm{k}", [P, R, E1]) for k in range(6)]
            sv = [alloc(ctx, f"sv{k}", [P, R]) for k in range(8)]
            p_h = [bank(ctx, f"p_lh{k}", [P, W]) for k in range(2)]
            p_t = bank(ctx, "p_lt", [P, R, D])
            p_hl = bank(ctx, "p_hl", [P, R, D])
            p_ag = bank(ctx, "p_ag", [P, R, D])
            p_sm = bank(ctx, "p_sm", [P, 512])
            p_cb = bank(ctx, "p_cb", [P, R, D])
            p_out = bank(ctx, "p_out", [P, R, D])
            LG, CT = 16, P
            flat = lambda t: t[:, :, :].rearrange("p r d -> p (r d)")

            c_loaded = sem("l_consts_loaded")
            set_ = sem("l_set")
            a_loaded = pair("l_a_loaded")
            gathered = pair("l_gathered")
            idx_ready = sem("l_idx_ready")
            a_ready = sem("l_a_ready")
            x2_ready = sem("l_x2_ready")
            deg_done = sem("l_deg_done")
            pre_ready = sem("l_pre_ready")
            root_done = sem("l_root_done")
            s = sem("l_steps")
            sx = sem("l_router_steps")
            xn_ready = sem("l_xn_ready")
            t_done = sem("l_t_done")
            x3t_ready = sem("l_x3t_ready")
            x4t_ready = sem("l_x4t_ready")
            hl_done = sem("l_hl_done")
            gg_ready = sem("l_gg_ready")
            ag_done = sem("l_ag_done")
            gr_ready = sem("l_gr_ready")
            lg_done = sem("l_lg_done")
            d_ready = sem("l_d_ready")
            exp_done = sem("l_exp_done")
            cw_ready = sem("l_cw_ready")
            ct_done = sem("l_ct_done")
            cwt_ready = sem("l_cwt_ready")
            cb_done = sem("l_cb_done")
            h_done = sem("l_h_done")
            h_ready = sem("l_h_ready")
            rc_ready = sem("l_rc_ready")
            out_done = sem("l_out_done")
            out_ready = sem("l_out_ready")
            stored = pair("l_stored")
            NC = 13

            with nc.Block() as block:
                @block.sync
                def _(sp):
                    src_a = a_t

                    def load(j, p):
                        sp.dma_start(at[p][:, :, :], src_a[:, bass.ds(R * j, R), :]).then_inc(a_loaded[p], 16)

                    def store(j, p):
                        sp.wait_ge(out_ready, j + 1)
                        sp.dma_start(out.rearrange("b n d -> n b d")[:, bass.ds(R * j, R), :], outx[p][:, :, :])\
                          .then_inc(stored[p], 16)

                    load(0, 0)
                    load(1, 1)
                    for dst, src in ((wgcn[:, :], w_gcn), (bgcn[:, :], b_gcn), (maskt[:, :], mask_t),
                                     (ws[:, :], w_s), (bs[:, :], b_s), (w1[:, :, :], e_w1), (w2[:, :, :], e_w2),
                                     (w3[:, :, :], e_w3), (be[:, :], b_e), (bout[:, :, :], b_out),
                                     (gws[:, :], gw), (gbs[:, :], gb), (selp[:, :, :, :], selp_d)):
                        sp.dma_start(dst, src).then_inc(c_loaded, 16)
                    with sp.Fori(0, NB - 3, 2) as i:
                        for p in range(2):
                            sp.wait_ge(ag_done, i + p + 1)
                            load(i + p + 2, p)
                            store(i + p, p)
                    store(NB - 2, 0)
                    store(NB - 1, 1)
                    for p in range(2):
                        sp.wait_ge(stored[p], 8 * NB + 1)

                @block.gpsimd
                def _(pool):
                    def take(j, p):
                        nc.gpsimd.tensor_copy(idx[p][:, :, :], pos_i[:, :, bass.ds(R * j, R)]).then_inc(idx_ready, 1)
                        pool.wait_ge(idx_ready, j + 1)
                        pool.sem_inc(passed, 1)

                    def gather(j, p, c):
                        for k in range(R):
                            pool.indirect_dma_start(
                                out=yg[p][:, c, k, :], out_offset=None, in_=y_d,
                                in_offset=bass.IndirectOffsetOnAxis(ap=idx[p][:, c, k:k + 1], axis=0))\
                                .then_inc(gathered[p], 16)

                    def roots(n, k):
                        pool.wait_ge(pre_ready, n)
                        w = (2 - k) * R
                        nc.gpsimd.tensor_tensor(root[k][:, 0:w], pre[k][:, 0:w], mhalf[:, 0:w], ALU.pow)\
                          .then_inc(root_done, 1)

                    take(0, 0)
                    gather(0, 0, 0)
                    gather(0, 0, 1)
                    take(1, 1)
                    gather(1, 1, 0)
                    gather(1, 1, 1)
                    with pool.Fori(0, NB - 3, 2) as i:
                        for p in range(2):
                            j = i + p
                            roots(2 * j + 1, 0)
                            pool.wait_ge(x2_ready, j + 1)
                            take(j + 2, p)
                            gather(j + 2, p, 0)
                            roots(2 * j + 2, 1)
                            gather(j + 2, p, 1)
                    for j in (NB - 2, NB - 1):
                        roots(2 * j + 1, 0)
                        roots(2 * j + 2, 1)

                @block.scalar
                def _(act):
                    act.sem_inc(stored[0], 1)
                    act.sem_inc(stored[1], 1)
                    act.wait_ge(c_loaded, 16 * NC)

                    def relu(b, u, dst, bias):
                        act.wait_ge(h_done, 8 * b + u + 1)
                        nc.scalar.activation(dst, p_h[u % 2][:, :], ACT.Relu, bias=bias).then_inc(h_ready, 1)

                    def body(i, p, front, back):
                        j = i + p
                        if back:
                            relu(j - 1, 0, hs[0][:, :], bs[:, 0:1])
                            for e in range(3):
                                relu(j - 1, 1 + e, he[e][:, :], be[:, e:e + 1])
                        if front:
                            act.wait_ge(t_done, 2 * j + 1)
                            nc.scalar.activation(x3t[:, :], flat(p_t), ACT.Copy).then_inc(x3t_ready, 1)
                        if back:
                            relu(j - 1, 4, he[3][:, :], be[:, 3:4])
                            relu(j - 1, 5, hs[1][:, :], bs[:, 1:2])
                            act.wait_ge(ct_done, j)
                            nc.scalar.activation(cwt[0:R * E1, :], p_sm[0:R * E1, CT:CT + P], ACT.Copy)\
                              .then_inc(cwt_ready, 1)
                        if front:
                            act.wait_ge(ag_done, j + 1)
                            for k in range(R):
                                last = nc.scalar.activation(gr[:, k, :], p_ag[:, k, :], ACT.Relu, scale=dm[:, k:k + 1])
                            last.then_inc(gr_ready, 1)
                        if back:
                            relu(j - 1, 6, rp[0][:, :], be[:, E1:E1 + 1])
                            relu(j - 1, 7, rp[1][:, :], be[:, E1 + 1:E1 + 2])
                        if front:
                            act.wait_ge(t_done, 2 * j + 2)
                            nc.scalar.activation(x4t[:, :], flat(p_t), ACT.Copy).then_inc(x4t_ready, 1)
                            act.wait_ge(d_ready, 2 * j + 1)
                            nc.scalar.activation(sm[1][:, :, :], sm[1][:, :, :], ACT.Exp).then_inc(exp_done, 1)
                            act.wait_ge(d_ready, 2 * j + 2)
                            nc.scalar.activation(sv[4][:, :], sv[4][:, :], ACT.Exp).then_inc(exp_done, 1)

                    turns(act, NB, body)

                @block.tensor
                def _(pe):
                    def product(b, u, mms):
                        if not (isinstance(b, int) and b == 0 and u < 2):
                            pe.wait_ge(h_ready, 8 * b + u - 1)
                        for dst, lhs, rhs in mms:
                            last = nc.tensor.matmul(dst, lhs, rhs, start=True, stop=True)
                        last.then_inc(h_done, 1)

                    def spread(dst, pair_):
                        for k in range(R):
                            last = nc.tensor.matmul(dst[:, k, :], selp[:, k, pair_, :], cwt[0:R * E1, :],
                                                    start=True, stop=True)
                        last.then_inc(cb_done, 1)

                    def second(b, pair_):
                        a = 2 * pair_
                        product(b, 6 + pair_, [(p_h[pair_][0:64, :], w2[:, a, :], he[a][:, :]),
                                               (p_h[pair_][64:128, :], w2[:, a + 1, :], he[a + 1][:, :])])

                    def body(i, p, front, back):
                        j = i + p
                        if back:
                            b = j - 1
                            pe.wait_ge(x4t_ready, j)
                            product(b, 0, [(p_h[0][:, :], ws[:, 0:P], x4t[:, :])])
                        if front:
                            pe.wait_ge(a_ready, j + 1)
                            for k in range(R):
                                last = nc.tensor.matmul(p_sm[:, k:k + 1], at[p][:, k, :], ones[:, :],
                                                        start=True, stop=True)
                            last.then_inc(deg_done, 1)
                        if back:
                            for e in range(3):
                                product(b, 1 + e, [(p_h[(1 + e) % 2][:, :], w1[:, e, :], x4t[:, :])])
                        if front:
                            pe.wait_ge(xn_ready, 2 * j + 1)
                            for k in range(R):
                                last = nc.tensor.transpose(p_t[:, k, :], xn[0][:, k, :], ident)
                            last.then_inc(t_done, 1)
                        if back:
                            product(b, 4, [(p_h[0][:, :], w1[:, 3, :], x4t[:, :])])
                        if front:
                            pe.wait_ge(x3t_ready, j + 1)
                            for k in range(R):
                                last = nc.tensor.matmul(p_hl[:, k, :], x3t[:, k * P:(k + 1) * P], wgcn[:, :],
                                                        start=True, stop=True)
                            last.then_inc(hl_done, 1)
                        if back:
                            product(b, 5, [(p_h[1][:, :], ws[:, P:2 * P], hs[0][:, :])])
                            pe.wait_ge(cw_ready, j)
                            nc.tensor.transpose(p_sm[0:R * E1, CT:CT + P], cw[:, :, :].rearrange("p r e -> p (r e)"),
                                                ident).then_inc(ct_done, 1)
                            pe.wait_ge(cwt_ready, j)
                            spread(p_cb, 0)
                        if front:
                            pe.wait_ge(gg_ready, j + 1)
                            for k in range(R):
                                last = nc.tensor.matmul(p_ag[:, k, :], at[p][:, k, :], gg[:, k, :],
                                                        start=True, stop=True)
                            last.then_inc(ag_done, 1)
                        if back:
                            spread(p_hl, 1)
                            second(b, 0)
                            second(b, 1)
                            pe.wait_ge(rc_ready, 2 * j)
                            pe.wait_ge(h_ready, 8 * b + 6)
                            if not (isinstance(b, int) and b == 0):
                                pe.wait_ge(out_ready, b)
                            for k in range(R):
                                tok = slice(k * P, (k + 1) * P)
                                nc.tensor.matmul(p_out[:, k, :], hs[1][:, tok], ws[:, 2 * P:3 * P],
                                                 start=True, stop=False)
                                nc.tensor.matmul(p_out[:, k, :], rc[0][:, tok], w3[:, 0, :], start=False, stop=False)
                                nc.tensor.matmul(p_out[:, k, :], rc[1][:, tok], w3[:, 1, :], start=False, stop=False)
                                last = nc.tensor.matmul(p_out[:, k, :], cwt[:, :], bout[:, k, :],
                                                        start=False, stop=True)
                            last.then_inc(out_done, 1)
                        if front:
                            pe.wait_ge(xn_ready, 2 * j + 2)
                            for k in range(R):
                                last = nc.tensor.transpose(p_t[:, k, :], xn[1][:, k, :], ident)
                            last.then_inc(t_done, 1)
                            pe.wait_ge(x4t_ready, j + 1)
                            for k in range(R):
                                last = nc.tensor.matmul(p_sm[:, LG + k * E1:LG + (k + 1) * E1],
                                                        x4t[:, k * P:(k + 1) * P], gws[:, :], start=True, stop=True)
                            last.then_inc(lg_done, 1)

                    pe.wait_ge(set_, 2)
                    pe.wait_ge(c_loaded, 16 * NC)
                    turns(pe, NB, body)

                @block.vector
                def _(dve):
                    nc.vector.memset(ones[:, :], 1.0).then_inc(set_, 1)
                    nc.vector.memset(cwt[:, :], 1.0).then_inc(set_, 1)
                    dve.wait_ge(c_loaded, 16 * NC)
                    S, SX = 7, 20
                    pri = cf[:, CF_PRI + E0 - E1:CF_PRI + E0].unsqueeze(1).to_broadcast([P, R, E1])
                    over = lambda v: v[:, :].unsqueeze(2).to_broadcast([P, R, E1])

                    def counted(sm_, start, n):
                        count = [0]

                        def step(ins):
                            count[0] += 1
                            assert count[0] <= n
                            ins.then_inc(sm_, 1)
                            dve.wait_ge(sm_, start + count[0])
                        return step

                    def layer_norm(step, rows, k):
                        for r in range(R):
                            last = nc.vector.bn_stats(st[:, r, :], rows(r))
                        step(last)
                        dve.sem_inc(passed, 1)
                        for r in range(R):
                            last = nc.vector.bn_aggr(mv[:, r, :], st[:, r, :])
                        step(last)

                    def first(step, dst, src, m):
                        step(nc.vector.tensor_reduce(dst[:, :], src[:, :, :], AX.X, ALU.max))
                        step(nc.vector.tensor_tensor(sm[4][:, :, :], src[:, :, :], over(dst), ALU.is_equal))
                        step(nc.vector.tensor_tensor(sm[4][:, :, :], sm[4][:, :, :], pri, ALU.mult))
                        step(nc.vector.tensor_reduce(sv[7][:, :], sm[4][:, :, :], AX.X, ALU.max))
                        step(nc.vector.tensor_tensor(sm[m][:, :, :], sm[4][:, :, :], over(sv[7]), ALU.is_equal))

                    def body(i, p, front, back):
                        j = i + p
                        if front:
                            step = counted(s, S * j, S)
                            rows = lambda r: xtok[:, bass.ds(R * j + r, 1), :].rearrange("p a d -> p (a d)")
                            batch = xtok[:, bass.ds(R * j, R), :]
                            dve.wait_ge(a_loaded[p], 8 * i + 16)
                            nc.vector.tensor_tensor(at[p][:, :, :], at[p][:, :, :],
                                                    ident.unsqueeze(1).to_broadcast([P, R, P]), ALU.add)\
                              .then_inc(a_ready, 1)
                            dve.wait_ge(gathered[p], 64 * i + 128)
                            for c in range(2):
                                for r in range(R):
                                    last = nc.vector.scalar_tensor_tensor(rows(r), yg[p][:, c, r, :],
                                                                          prob[:, c, bass.ds(R * j + r, 1)], rows(r),
                                                                          ALU.mult, ALU.add)
                                if c == 1:
                                    last.then_inc(x2_ready, 1)
                                    dve.wait_ge(x2_ready, j + 1)
                                    dve.sem_inc(passed, 1)
                                else:
                                    step(last)
                            layer_norm(step, rows, 0)
                            nc.vector.tensor_scalar(pre[0][:, 0:R], mv[:, :, 1], 1e-5, None, ALU.add)
                            dve.wait_ge(deg_done, j + 1)
                            nc.vector.tensor_scalar(pre[0][:, R:2 * R], p_sm[:, 0:R], 1e-8, None, ALU.add)\
                              .then_inc(pre_ready, 1)
                            dve.wait_ge(root_done, 2 * j + 1)
                            nc.vector.tensor_tensor(dm[:, :], root[0][:, R:2 * R], maskt[:, bass.ds(R * j, R)],
                                                    ALU.mult)
                            step(nc.vector.tensor_tensor(rd[:, :], root[0][:, 0:R], root[0][:, R:2 * R], ALU.mult))
                            for r in range(R):
                                last = nc.vector.tensor_scalar(xn[0][:, r, :], rows(r), mv[:, r, 0:1],
                                                               rd[:, r:r + 1], ALU.subtract, ALU.mult)
                            last.then_inc(xn_ready, 1)
                            dve.wait_ge(hl_done, j + 1)
                            for r in range(R):
                                last = nc.vector.scalar_tensor_tensor(gg[:, r, :], bgcn[:, :],
                                                                      root[0][:, R + r:R + r + 1], p_hl[:, r, :],
                                                                      ALU.mult, ALU.add)
                            last.then_inc(gg_ready, 1)
                            dve.wait_ge(gr_ready, j + 1)
                            step(nc.vector.tensor_tensor(batch, batch, gr[:, :, :], ALU.add))
                            dve.sem_inc(passed, 1)
                            layer_norm(step, rows, 1)
                            nc.vector.tensor_scalar(pre[1][:, 0:R], mv[:, :, 1], 1e-5, None, ALU.add)\
                              .then_inc(pre_ready, 1)
                        if back:
                            dve.wait_ge(h_ready, 8 * j - 1)
                            dve.wait_ge(cb_done, 2 * j)
                            nc.vector.tensor_tensor(rc[0][:, :], rp[0][:, :], flat(p_cb), ALU.mult)\
                              .then_inc(rc_ready, 1)
                        if front:
                            dve.wait_ge(root_done, 2 * j + 2)
                            for r in range(R):
                                last = nc.vector.tensor_scalar(xn[1][:, r, :], rows(r), mv[:, r, 0:1],
                                                               root[1][:, r:r + 1], ALU.subtract, ALU.mult)
                            last.then_inc(xn_ready, 1)
                        if back:
                            dve.wait_ge(h_ready, 8 * j)
                            nc.vector.tensor_tensor(rc[1][:, :], rp[1][:, :], flat(p_hl), ALU.mult)\
                              .then_inc(rc_ready, 1)
                            dve.wait_ge(out_done, j)
                            dve.wait_ge(stored[1 - p], 8 * i + 1 if p else 8 * i - 15)
                            nc.vector.tensor_tensor(outx[1 - p][:, :, :], xtok[:, bass.ds(R * (j - 1), R), :],
                                                    p_out[:, :, :], ALU.add).then_inc(out_ready, 1)
                        if front:
                            step = counted(sx, SX * j, SX)
                            dve.wait_ge(lg_done, j + 1)
                            step(nc.vector.tensor_tensor(sm[0][:, :, :],
                                                         p_sm[:, LG:LG + R * E1].rearrange("p (r e) -> p r e", e=E1),
                                                         gbs[:, :].unsqueeze(1).to_broadcast([P, R, E1]), ALU.add))
                            step(nc.vector.tensor_reduce(sv[0][:, :], sm[0][:, :, :], AX.X, ALU.max))
                            nc.vector.tensor_tensor(sm[1][:, :, :], sm[0][:, :, :], over(sv[0]), ALU.subtract)\
                              .then_inc(d_ready, 1)
                            dve.wait_ge(exp_done, 2 * j + 1)
                            step(nc.vector.tensor_reduce(sv[1][:, :], sm[1][:, :, :], AX.X, ALU.add))
                            step(nc.vector.reciprocal(sv[1][:, :], sv[1][:, :]))
                            step(nc.vector.tensor_tensor(sm[2][:, :, :], sm[1][:, :, :], over(sv[1]), ALU.mult))
                            first(step, sv[2], sm[2], 3)
                            step(nc.vector.scalar_tensor_tensor(flat(sm[2]), flat(sm[3]), BIG, flat(sm[2]),
                                                                ALU.mult, ALU.add))
                            first(step, sv[3], sm[2], 5)
                            nc.vector.tensor_tensor(sv[4][:, :], sv[3][:, :], sv[2][:, :], ALU.subtract)\
                              .then_inc(d_ready, 1)
                            dve.wait_ge(exp_done, 2 * j + 2)
                            step(nc.vector.tensor_scalar(sv[5][:, :], sv[4][:, :], 1.0, None, ALU.add))
                            step(nc.vector.reciprocal(sv[5][:, :], sv[5][:, :]))
                            nc.vector.tensor_tensor(sm[3][:, :, :], sm[3][:, :, :], over(sv[5]), ALU.mult)
                            step(nc.vector.tensor_tensor(sv[6][:, :], sv[4][:, :], sv[5][:, :], ALU.mult))
                            step(nc.vector.tensor_tensor(sm[5][:, :, :], sm[5][:, :, :], over(sv[6]), ALU.mult))
                            nc.vector.tensor_tensor(cw[:, :, :], sm[3][:, :, :], sm[5][:, :, :], ALU.add)\
                              .then_inc(cw_ready, 1)

                    turns(dve, NB, body)


def layout(x, adj, nodemask, L0_gnn_W1, L0_gnn_b1, L0_gnn_W2, L0_gnn_b2, L0_gnn_fusion_w, L0_ffn_Wg, L0_ffn_bg,
           L0_ffn_W1, L0_ffn_b1, L0_ffn_W2, L0_ffn_b2, L1_gnn_W, L1_gnn_b, L1_ffn_sW1, L1_ffn_sb1, L1_ffn_sW2,
           L1_ffn_sb2, L1_ffn_sW3, L1_ffn_sb3, L1_ffn_eW1, L1_ffn_eb1, L1_ffn_eW2, L1_ffn_eb2, L1_ffn_eW3,
           L1_ffn_eb3, L1_ffn_gW, L1_ffn_gb):
    f = np.float32
    every = lambda v, n=P: np.broadcast_to(v.reshape(1, -1), (n, v.size))
    x_grp = np.zeros((NGB, P, R, D), f)
    a_grp = np.zeros((NGB, P, R, P), f)
    w_grp = np.zeros((NGB, P, GWID), f)
    j = 0
    for g, nodes in enumerate(GROUPS):
        n, per = GN[g], GPT[g]
        for b in range(GB[g]):
            for k in range(R):
                first = (b * R + k) * per
                for s, graph in enumerate(range(first, min(first + per, B))):
                    r = slice(s * n, (s + 1) * n)
                    x_grp[j, r, k, :] = x[graph][nodes]
                    a_grp[j, r, k, r] = adj[graph][np.ix_(nodes, nodes)].T
            w_grp[j] = np.concatenate([
                L0_gnn_W1[g], L0_gnn_W2[g].reshape(2, P, D).transpose(1, 0, 2).reshape(P, 2 * D),
                L0_gnn_b1[g].reshape(2, P).T, every(L0_gnn_b2[g])], axis=1)
            j += 1
    w_exp = np.concatenate([
        L0_ffn_W1.transpose(2, 0, 1),
        L0_ffn_W2.reshape(E0, D, HC, P).transpose(3, 0, 2, 1).reshape(P, E0, HC * D),
        L0_ffn_b1.reshape(E0, HC, P).transpose(2, 0, 1),
        L0_ffn_b2.T.reshape(P, E0, 1),
        np.zeros((P, E0, 1), f)], axis=2)
    b_out = np.zeros((R * E1 + 1, R, D), f)
    for k in range(R):
        b_out[k * E1:(k + 1) * E1, k, :] = L1_ffn_eb3
        b_out[R * E1, k, :] = L1_ffn_sb3
    cf, ch, sel, selp = consts()
    return {
        "x_tok": x.transpose(1, 0, 2), "x_grp": x_grp, "a_grp": a_grp, "w_grp": w_grp,
        "fus": every(L0_gnn_fusion_w), "wg": L0_ffn_Wg.T, "bg": every(L0_ffn_bg), "w_exp": w_exp,
        "a_t": adj.transpose(2, 0, 1), "w_gcn": L1_gnn_W.T, "b_gcn": every(L1_gnn_b), "mask_t": nodemask.T,
        "w_s": np.concatenate([L1_ffn_sW1, L1_ffn_sW2, L1_ffn_sW3], axis=1),
        "b_s": np.stack([L1_ffn_sb1, L1_ffn_sb2], axis=1),
        "e_w1": L1_ffn_eW1.transpose(1, 0, 2), "e_w2": L1_ffn_eW2.transpose(1, 0, 2),
        "e_w3": L1_ffn_eW3.reshape(2, P, D).transpose(1, 0, 2),
        "b_e": np.concatenate([L1_ffn_eb1.T, L1_ffn_eb2.reshape(2, P).T], axis=1),
        "b_out": b_out, "gw": L1_ffn_gW, "gb": every(L1_ffn_gb),
        "cf_d": cf, "ch_d": ch, "sel_d": sel, "selp_d": selp,
    }


def kernel(**inputs):
    import concourse.bacc as bacc
    from concourse.bass_utils import run_bass_kernel_spmd

    nc = bacc.Bacc("TRN2", target_bir_lowering=False, num_devices=1)
    arrays, args = {}, []
    for name, a in layout(**{k: np.asarray(v) for k, v in inputs.items()}).items():
        arrays["in_" + name] = np.ascontiguousarray(a)
        args.append(nc.dram_tensor("in_" + name, a.shape, mybir.dt.from_np(a.dtype), kind="ExternalInput").ap())
    out = nc.dram_tensor("out_0", (B, N, D), F32, kind="ExternalOutput").ap()
    build(nc, *args, out)
    r = run_bass_kernel_spmd(nc, [arrays], core_ids=[0])
    return r.results[0]["out_0"]
```

```python
import numpy as np
import concourse.bass as bass
from concourse import mybir
from contextlib import ExitStack

F32 = mybir.dt.float32
F16 = mybir.dt.float16
F32R = mybir.dt.float32r
I32 = mybir.dt.int32
ALU = mybir.AluOpType
ACT = mybir.ActivationFunctionType
AX = mybir.AxisListType

P = 128
B = 128
N = P
D = P
R = 4
W = R * P
GROUPS = [list(range(25)), [0, 1, 2, 3, 4, 5, 6, 7, 8], [0, 9, 10, 11, 12, 13, 14], [6, 7, 8, 12, 13, 14],
          [3, 4, 5, 9, 10, 11]]
GN = [len(g) for g in GROUPS]
GPT = [P // n for n in GN]
GB = [-(-(-(-B // k)) // R) for k in GPT]
GOFF = [sum(GN[:g]) for g in range(len(GROUPS))]
GR = sum(GN)
NGB = sum(GB)
GHID = 256
E0 = 8
H0 = 512
HC = H0 // P
TILE = 512
NT = (2 * B * N + E0 * (TILE - 1)) // TILE
NTP = NT + NT % 2
NCOL = NTP * R
EW = HC * P + HC * D + HC + 2
E1 = 4
KV = 97
GWID = GHID + 2 * D + 2 + D
BIG = -3.0e38


def consts():
    i = np.arange(P)
    ident = np.eye(P, dtype=np.float32)
    sel = np.zeros((GR, P), np.float32)
    for g, nodes in enumerate(GROUPS):
        for n, node in enumerate(nodes):
            sel[GOFF[g] + n, node] = 1
    before = (i[:, None] < i[None, :]).astype(np.float32)
    b8 = (np.arange(E0)[None, :] < np.arange(E0)[:, None]).astype(np.float32)
    cf = np.concatenate([
        ident,
        np.broadcast_to(np.arange(E0, 0, -1, dtype=np.float32), (P, E0)),
        np.broadcast_to(b8.reshape(1, -1), (P, E0 * E0)),
        np.broadcast_to(np.arange(P, dtype=np.float32), (P, P)),
        i[:, None].astype(np.float32),
        np.broadcast_to(np.arange(NTP, dtype=np.float32), (P, NTP)),
    ], axis=1)
    ch = np.concatenate([
        before, np.ones((P, P), np.float32),
        np.broadcast_to(np.arange(P, dtype=np.float32), (P, P)),
        np.broadcast_to(np.arange(NCOL, dtype=np.float32), (P, NCOL)),
    ], axis=1).astype(np.float16)
    selp = np.zeros((2 * R * E1, R, 2, P), np.float32)
    for k in range(R):
        for e in range(E1):
            selp[k * E1 + e::R * E1, k, e // 2, (e % 2) * 64:(e % 2) * 64 + 64] = 1
    return cf, ch, sel, selp


CF_ID, CF_PRI, CF_B8, CF_T, CF_P, CF_J = 0, P, P + E0, P + E0 + E0 * E0, 2 * P + E0 + E0 * E0, 2 * P + E0 + E0 * E0 + 1
CF_W = CF_J + NTP
CH_U, CH_1, CH_I, CH_H = 0, P, 2 * P, 3 * P
CH_W = 3 * P + NCOL


def build(nc, x_tok, x_grp, a_grp, w_grp, fus, wg, bg, w_exp, a_t, w_gcn, b_gcn, mask_t,
          w_s, b_s, e_w1, e_w2, e_w3, b_e, b_out, gw, gb, cf_d, ch_d, sel_d, selp_d, out):
    xln_d = nc.dram_tensor("xln_scratch", (B * N, D), F32, kind="Internal").ap()
    y_d = nc.dram_tensor("expert_rows_scratch", (NTP * TILE, D), F32, kind="Internal").ap()
    c_d = [nc.dram_tensor(f"group_rows_scratch{g}", (GB[g] * R * GPT[g] * GN[g], D), F32, kind="Internal").ap()
           for g in range(len(GROUPS))]

    top = ExitStack()
    with top:
        def alloc(ctx, name, shape, dt=F32):
            return ctx.enter_context(nc.sbuf_tensor(name, shape, dt))

        def bank(ctx, name, shape, dt=F32):
            return ctx.enter_context(nc.psum_tensor(name, shape, dt))

        def sem(name):
            return top.enter_context(nc.semaphore(name))

        def pair(name):
            return [sem(name + "_even"), sem(name + "_odd")]

        def turns(eng, n, body):
            body(0, 0, True, False)
            body(0, 1, True, True)
            with eng.Fori(2, n - 1, 2) as i:
                body(i, 0, True, True)
                body(i, 1, True, True)
            body(n, 0, False, True)

        def turns3(eng, n, body):
            body(0, 0, True, False, False)
            body(0, 1, True, True, False)
            with eng.Fori(2, n - 1, 2) as i:
                body(i, 0, True, True, True)
                body(i, 1, True, True, True)
            body(n, 0, False, True, True)
            body(n, 1, False, False, True)

        xtok = alloc(top, "xtok", [P, B, D])
        cf = alloc(top, "cf", [P, CF_W])
        ch = alloc(top, "ch", [P, CH_W], F16)
        mhalf = alloc(top, "mhalf", [P, 2 * R])
        ident = cf[:, CF_ID:CF_ID + P]
        pos_i = alloc(top, "pos_i", [P, 2, B], I32)
        prob = alloc(top, "prob", [P, 2, B])
        ids = alloc(top, "ids", [P, NCOL], I32)
        texp = alloc(top, "texp", [P, NTP], I32)

        x_loaded = sem("x_loaded")
        half_set = sem("half_set")
        passed = sem("passed")

        with ExitStack() as ctx:
            xg = [alloc(ctx, f"xg{p}", [P, R, D]) for p in range(2)]
            ar = [alloc(ctx, f"ar{p}", [P, R, P]) for p in range(2)]
            ag = [alloc(ctx, f"ag{p}", [P, R, P]) for p in range(2)]
            ah = [alloc(ctx, f"ah{p}", [P, R, P]) for p in range(2)]
            wj = [alloc(ctx, f"wj{p}", [P, GWID]) for p in range(2)]
            ones = alloc(ctx, "ones", [P, 1])
            fw = alloc(ctx, "fw", [P, 5])
            fe = alloc(ctx, "fe", [P, 5])
            fm = alloc(ctx, "fm", [P, 4])
            wb = alloc(ctx, "wb", [P, NGB])
            st = [alloc(ctx, f"st{p}", [P, R, 6]) for p in range(2)]
            mv = [alloc(ctx, f"mv{p}", [P, R, 2]) for p in range(2)]
            pre = [alloc(ctx, f"pre{p}", [P, 2 * R]) for p in range(2)]
            root = [alloc(ctx, f"root{p}", [P, 2 * R]) for p in range(2)]
            nz = [alloc(ctx, f"nz{p}", [P, R]) for p in range(2)]
            dinv = [alloc(ctx, f"dinv{p}", [P, R]) for p in range(2)]
            dsc = [alloc(ctx, f"dsc{p}", [P, R]) for p in range(2)]
            wdi = [alloc(ctx, f"wdi{p}", [P, R]) for p in range(2)]
            xs = [alloc(ctx, f"xs{p}", [P, R, D]) for p in range(2)]
            ys = alloc(ctx, "ys", [P, R, D])
            yt = alloc(ctx, "yt", [P, W])
            ht = alloc(ctx, "ht", [P, 2, W])
            zs = alloc(ctx, "zs", [P, R, D])
            b2w = [alloc(ctx, f"b2w{p}", [P, D]) for p in range(2)]
            os_ = [alloc(ctx, f"os{p}", [P, R, D]) for p in range(2)]
            orl = [alloc(ctx, f"orl{p}", [P, R, D]) for p in range(2)]
            p_deg = bank(ctx, "p_deg", [P, 512])
            p_y = bank(ctx, "p_y", [P, R, D])
            p_t = bank(ctx, "p_t", [P, R, D])
            p_h = [bank(ctx, f"p_h{c}", [P, W]) for c in range(2)]
            p_z = bank(ctx, "p_z", [P, R, D])
            p_o = bank(ctx, "p_o", [P, R, D])

            c_loaded = sem("g_consts_loaded")
            loaded = pair("g_loaded")
            set_ = sem("g_set")
            fus_exp = sem("g_fus_exp")
            fus_s = sem("g_fus_steps")
            w_loaded = pair("g_w_loaded")
            ag_ready = sem("g_ag_ready")
            ah_ready = sem("g_ah_ready")
            b2_s = sem("g_b2_s")
            deg_done = sem("g_deg_done")
            stat_s = sem("g_stat_s")
            mv_s = sem("g_mv_s")
            pre_s = sem("g_pre_s")
            pre_ready = sem("g_pre_ready")
            root_done = sem("g_root_done")
            dinv_s = sem("g_dinv_s")
            xs_ready = sem("g_xs_ready")
            y_done = sem("g_y_done")
            ys_ready = sem("g_ys_ready")
            t_done = sem("g_t_done")
            yt_ready = sem("g_yt_ready")
            h_done = sem("g_h_done")
            ht_ready = sem("g_ht_ready")
            z_done = sem("g_z_done")
            zs_ready = sem("g_zs_ready")
            o_done = sem("g_o_done")
            os_ready = sem("g_os_ready")
            orl_ready = sem("g_orl_ready")
            stored = pair("g_stored")

            batch_of = [(g, b) for g in range(len(GROUPS)) for b in range(GB[g])]

            with nc.Block() as block:
                @block.sync
                def _(sp):
                    sp.dma_start(cf[:, :], cf_d).then_inc(c_loaded, 16)
                    sp.dma_start(ch[:, :], ch_d).then_inc(c_loaded, 16)
                    sp.dma_start(fw[:, :], fus).then_inc(c_loaded, 16)

                    def load(j):
                        sp.dma_start(xg[j % 2][:, :, :], x_grp[j]).then_inc(loaded[j % 2], 16)
                        sp.dma_start(ar[j % 2][:, :, :], a_grp[j]).then_inc(loaded[j % 2], 16)

                    def store(j):
                        g, b = batch_of[j]
                        rows = GPT[g] * GN[g]
                        dst = c_d[g][b * R * rows:(b + 1) * R * rows, :].rearrange("(k r) d -> r k d", r=rows)
                        sp.wait_ge(orl_ready, j + 1)
                        sp.dma_start(dst, orl[j % 2][0:rows, :, :]).then_inc(stored[j % 2], 16)

                    load(0)
                    load(1)
                    for j in range(NGB + 3):
                        if j >= 3:
                            store(j - 3)
                        if j < NGB:
                            if j >= 2:
                                sp.wait_ge(z_done, j - 1)
                            sp.dma_start(wj[j % 2][:, :], w_grp[j]).then_inc(w_loaded[j % 2], 16)
                        if j % 2 == 0 and j < NGB:
                            n = B * j // NGB, B * (j + 2) // NGB
                            sp.dma_start(xtok[:, n[0]:n[1], :], x_tok[:, n[0]:n[1], :]).then_inc(x_loaded, 16)
                        if j + 2 < NGB:
                            sp.wait_ge(xs_ready, j + 1)
                            sp.wait_ge(ah_ready, j + 1)
                            load(j + 2)
                    sp.wait_ge(stored[0], 16 * (NGB // 2) + 1)
                    sp.wait_ge(stored[1], 16 * (NGB // 2) + 1)
                    sp.wait_ge(x_loaded, 16 * (NGB // 2))

                @block.gpsimd
                def _(pool):
                    nc.gpsimd.memset(mhalf[:, :], -0.5).then_inc(half_set, 1)
                    pool.wait_ge(half_set, 1)
                    pool.wait_ge(c_loaded, 48)
                    plus = ident.unsqueeze(1).to_broadcast([P, R, P])

                    def body(i, p, first, middle, back):
                        j = i + p
                        if first:
                            pool.wait_ge(loaded[p], 16 * i + 32)
                            if middle:
                                pool.wait_ge(y_done, j)
                            nc.gpsimd.tensor_tensor(ag[p][:, :, :], ar[p][:, :, :], plus, ALU.add)\
                              .then_inc(ag_ready, 1)
                            pool.wait_ge(pre_ready, j + 1)
                            nc.gpsimd.tensor_tensor(root[p][:, :], pre[p][:, :], mhalf[:, :], ALU.pow)\
                              .then_inc(root_done, 1)
                            if back:
                                pool.wait_ge(o_done, j - 1)
                            nc.gpsimd.tensor_tensor(ah[p][:, :, :], ar[p][:, :, :], plus, ALU.add)\
                              .then_inc(ah_ready, 1)

                    turns3(pool, NGB, body)

                @block.scalar
                def _(act):
                    act.sem_inc(stored[0], 1)
                    act.sem_inc(stored[1], 1)
                    act.wait_ge(fus_s, 2)
                    nc.scalar.activation(fe[:, :], fe[:, :], ACT.Exp).then_inc(fus_exp, 1)

                    def body(i, p, first, middle, back):
                        j = i + p
                        q = 1 - p
                        if middle:
                            act.wait_ge(t_done, j)
                            nc.scalar.activation(yt[:, :], p_t[:, :, :].rearrange("p r d -> p (r d)"), ACT.Copy)\
                              .then_inc(yt_ready, 1)
                            for c in range(2):
                                act.wait_ge(h_done, 2 * j + c - 1)
                                nc.scalar.activation(ht[:, c, :], p_h[c][:, :], ACT.Relu,
                                                     bias=wj[q][:, GHID + 2 * D + c:GHID + 2 * D + c + 1])\
                                  .then_inc(ht_ready, 1)
                        if back:
                            act.wait_ge(os_ready, j)
                            act.wait_ge(stored[p], 8 * i - 15)
                            nc.scalar.activation(orl[p][:, :, :], os_[p][:, :, :], ACT.Relu).then_inc(orl_ready, 1)

                    turns3(act, NGB, body)

                @block.tensor
                def _(pe):
                    def body(i, p, first, middle, back):
                        j = i + p
                        q = 1 - p
                        if middle:
                            pe.wait_ge(xs_ready, j)
                            for k in range(R):
                                last = nc.tensor.matmul(p_y[:, k, :], ag[q][:, k, :], xs[q][:, k, :],
                                                        start=True, stop=True)
                            last.then_inc(y_done, 1)
                        if back:
                            pe.wait_ge(ht_ready, 2 * j - 2)
                            for k in range(R):
                                for c in range(2):
                                    last = nc.tensor.matmul(p_z[:, k, :], ht[:, c, k * P:(k + 1) * P],
                                                            wj[p][:, GHID + c * D:GHID + (c + 1) * D],
                                                            start=(c == 0), stop=(c == 1))
                            last.then_inc(z_done, 1)
                        if first:
                            pe.wait_ge(ag_ready, j + 1)
                            for k in range(R):
                                last = nc.tensor.matmul(p_deg[:, k:k + 1], ag[p][:, k, :], ones[:, :],
                                                        start=True, stop=True)
                            last.then_inc(deg_done, 1)
                        if middle:
                            pe.wait_ge(ys_ready, j)
                            for k in range(R):
                                last = nc.tensor.transpose(p_t[:, k, :], ys[:, k, :], ident)
                            last.then_inc(t_done, 1)
                        if back:
                            pe.wait_ge(zs_ready, j - 1)
                            pe.wait_ge(ah_ready, j - 1)
                            pe.wait_ge(os_ready, j - 1)
                            for k in range(R):
                                last = nc.tensor.matmul(p_o[:, k, :], ah[p][:, k, :], zs[:, k, :],
                                                        start=True, stop=True)
                            last.then_inc(o_done, 1)
                        if middle:
                            pe.wait_ge(w_loaded[q], 8 * i + 16 if p else 8 * i)
                            pe.wait_ge(yt_ready, j)
                            for c in range(2):
                                nc.tensor.matmul(p_h[c][:, :], wj[q][:, c * P:(c + 1) * P], yt[:, :],
                                                 start=True, stop=True).then_inc(h_done, 1)

                    pe.wait_ge(set_, 1)
                    pe.wait_ge(c_loaded, 48)
                    turns3(pe, NGB, body)

                @block.vector
                def _(dve):
                    nc.vector.memset(ones[:, :], 1.0).then_inc(set_, 1)
                    dve.wait_ge(c_loaded, 48)
                    nc.vector.reduce_max(fm[:, 0:1], fw[:, :], AX.X).then_inc(fus_s, 1)
                    dve.wait_ge(fus_s, 1)
                    nc.vector.tensor_scalar(fe[:, :], fw[:, :], fm[:, 0:1], None, ALU.subtract).then_inc(fus_s, 1)
                    dve.wait_ge(fus_exp, 1)
                    nc.vector.reduce_sum(fm[:, 1:2], fe[:, :], AX.X).then_inc(fus_s, 1)
                    dve.wait_ge(fus_s, 3)
                    nc.vector.reciprocal(fm[:, 2:3], fm[:, 1:2]).then_inc(fus_s, 1)
                    dve.wait_ge(fus_s, 4)
                    nc.vector.tensor_scalar(fw[:, :], fe[:, :], fm[:, 2:3], None, ALU.mult).then_inc(fus_s, 1)
                    dve.wait_ge(fus_s, 5)
                    for g in range(len(GROUPS)):
                        a = sum(GB[:g])
                        last = nc.vector.tensor_copy(wb[:, a:a + GB[g]], fw[:, g:g + 1].to_broadcast([P, GB[g]]))
                    last.then_inc(fus_s, 1)
                    dve.wait_ge(fus_s, 6)

                    dve.sem_inc(os_ready, 1)

                    def body(i, p, first, middle, back):
                        j = i + p
                        q = 1 - p
                        if first:
                            dve.wait_ge(loaded[p], 16 * i + 32)
                            for k in range(R):
                                last = nc.vector.bn_stats(st[p][:, k, :], xg[p][:, k, :])
                            last.then_inc(stat_s, 1)
                        if middle:
                            dve.wait_ge(y_done, j)
                            nc.vector.tensor_tensor(ys[:, :, :], p_y[:, :, :],
                                                    dinv[q][:, :].unsqueeze(2).to_broadcast([P, R, D]), ALU.mult)\
                              .then_inc(ys_ready, 1)
                        if first:
                            dve.wait_ge(stat_s, j + 1)
                            dve.sem_inc(passed, 1)
                            for k in range(R):
                                last = nc.vector.bn_aggr(mv[p][:, k, :], st[p][:, k, :])
                            last.then_inc(mv_s, 1)
                            dve.wait_ge(mv_s, j + 1)
                            nc.vector.tensor_scalar(pre[p][:, 0:R], mv[p][:, :, 1], 1e-5, None, ALU.add)
                        if back:
                            dve.wait_ge(z_done, j - 1)
                            nc.vector.tensor_tensor(zs[:, :, :], p_z[:, :, :],
                                                    dinv[p][:, :].unsqueeze(2).to_broadcast([P, R, D]), ALU.mult)\
                              .then_inc(zs_ready, 1)
                        if first:
                            dve.wait_ge(deg_done, j + 1)
                            nc.vector.tensor_scalar(nz[p][:, :], p_deg[:, 0:R], 0.0, None, ALU.is_equal)\
                              .then_inc(pre_s, 1)
                            dve.wait_ge(pre_s, j + 1)
                            nc.vector.tensor_tensor(pre[p][:, R:2 * R], p_deg[:, 0:R], nz[p][:, :], ALU.add)\
                              .then_inc(pre_ready, 1)
                            nc.vector.tensor_scalar(nz[p][:, :], nz[p][:, :], -1.0, 1.0, ALU.mult, ALU.add)\
                              .then_inc(dinv_s, 1)
                        if middle:
                            dve.wait_ge(w_loaded[q], 8 * i + 16 if p else 8 * i)
                            if back:
                                dve.wait_ge(os_ready, j - 1)
                            nc.vector.tensor_scalar(wdi[q][:, :], dinv[q][:, :], wb[:, bass.ds(j - 1, 1)], None,
                                                    ALU.mult)
                            nc.vector.tensor_scalar(b2w[q][:, :], wj[q][:, GWID - D:GWID], wb[:, bass.ds(j - 1, 1)],
                                                    None, ALU.mult).then_inc(b2_s, 1)
                        if first:
                            dve.wait_ge(dinv_s, 3 * j + 1)
                            dve.wait_ge(root_done, j + 1)
                            nc.vector.tensor_tensor(dinv[p][:, :], nz[p][:, :], root[p][:, R:2 * R], ALU.mult)\
                              .then_inc(dinv_s, 1)
                            dve.wait_ge(dinv_s, 3 * j + 2)
                            nc.vector.tensor_tensor(dsc[p][:, :], dinv[p][:, :], root[p][:, 0:R], ALU.mult)\
                              .then_inc(dinv_s, 1)
                            dve.wait_ge(dinv_s, 3 * j + 3)
                            for k in range(R):
                                last = nc.vector.tensor_scalar(xs[p][:, k, :], xg[p][:, k, :], mv[p][:, k, 0:1],
                                                               dsc[p][:, k:k + 1], ALU.subtract, ALU.mult)
                            last.then_inc(xs_ready, 1)
                        if back:
                            dve.wait_ge(o_done, j - 1)
                            dve.wait_ge(b2_s, j - 1)
                            for k in range(R):
                                last = nc.vector.scalar_tensor_tensor(os_[p][:, k, :], p_o[:, k, :],
                                                                      wdi[p][:, k:k + 1], b2w[p][:, :],
                                                                      ALU.mult, ALU.add)
                            last.then_inc(os_ready, 1)

                    turns3(dve, NGB, body)

        lgp = top.enter_context(ExitStack())
        p_lg = bank(lgp, "p_lg", [P, B * E0])
        with ExitStack() as ctx:
            ct = [alloc(ctx, f"ct{p}", [GR, R, D]) for p in range(2)]
            sel = alloc(ctx, "sel", [GR, P])
            wgt = alloc(ctx, "wgt", [P, E0])
            st = [alloc(ctx, f"gst{p}", [P, R, 6]) for p in range(2)]
            mv = [alloc(ctx, f"gmv{p}", [P, R, 2]) for p in range(2)]
            pre = [alloc(ctx, f"gpre{p}", [P, R]) for p in range(2)]
            root = [alloc(ctx, f"groot{p}", [P, R]) for p in range(2)]
            xl = [alloc(ctx, f"xl{p}", [P, R, D]) for p in range(2)]
            xt = [alloc(ctx, f"gxt{p}", [P, W]) for p in range(2)]
            p_sel = [bank(ctx, f"p_sel{p}", [P, R, D]) for p in range(2)]
            p_t = bank(ctx, "p_gt", [P, R, D])
            NB = B // R
            c_loaded = sem("r_consts_loaded")
            loaded = pair("r_loaded")
            sel_done = sem("r_sel_done")
            x1_ready = sem("r_x1_ready")
            stat_s = sem("r_stat_s")
            mv_s = sem("r_mv_s")
            pre_ready = sem("r_pre_ready")
            root_done = sem("r_root_done")
            xl_ready = sem("r_xl_ready")
            t_done = sem("r_t_done")
            xt_ready = sem("r_xt_ready")
            stored = pair("r_stored")

            with nc.Block() as block:
                @block.sync
                def _(sp):
                    sp.dma_start(sel[:, :], sel_d).then_inc(c_loaded, 16)
                    sp.dma_start(wgt[:, :], wg).then_inc(c_loaded, 16)

                    def load(j, p):
                        for g in range(len(GROUPS)):
                            src = c_d[g][0:B * GN[g], :].rearrange("(b n) d -> n b d", n=GN[g])
                            sp.dma_start(ct[p][GOFF[g]:GOFF[g] + GN[g], :, :], src[:, bass.ds(R * j, R), :])\
                              .then_inc(loaded[p], 16)

                    def store(j, p):
                        sp.wait_ge(xl_ready, j + 1)
                        sp.dma_start(xln_d.rearrange("(b n) d -> n b d", n=N)[:, bass.ds(R * j, R), :],
                                     xl[p][:, :, :]).then_inc(stored[p], 16)

                    load(0, 0)
                    load(1, 1)
                    with sp.Fori(0, NB - 3, 2) as i:
                        for p in range(2):
                            sp.wait_ge(sel_done, i + p + 1)
                            load(i + p + 2, p)
                            store(i + p, p)
                    store(NB - 2, 0)
                    store(NB - 1, 1)
                    for p in range(2):
                        sp.wait_ge(stored[p], 8 * NB + 1)

                @block.gpsimd
                def _(pool):
                    with pool.Fori(0, NB - 1, 2) as i:
                        for p in range(2):
                            pool.wait_ge(pre_ready, i + p + 1)
                            nc.gpsimd.tensor_tensor(root[p][:, :], pre[p][:, :], mhalf[:, 0:R], ALU.pow)\
                              .then_inc(root_done, 1)

                @block.scalar
                def _(act):
                    def body(i, p, front, back):
                        j = i + p
                        if back:
                            act.wait_ge(t_done, j)
                            nc.scalar.activation(xt[1 - p][:, :], p_t[:, :, :].rearrange("p r d -> p (r d)"), ACT.Copy)\
                              .then_inc(xt_ready, 1)

                    turns(act, NB, body)

                @block.tensor
                def _(pe):
                    def body(i, p, front, back):
                        j = i + p
                        q = 1 - p
                        if front:
                            pe.wait_ge(loaded[p], 40 * i + 80)
                            if not (isinstance(j, int) and j < 2):
                                pe.wait_ge(x1_ready, j - 1)
                            nc.tensor.matmul(p_sel[p][:, :, :].rearrange("p r d -> p (r d)"), sel[:, :],
                                             ct[p][:, :, :].rearrange("p r d -> p (r d)"),
                                             start=True, stop=True).then_inc(sel_done, 1)
                        if back:
                            pe.wait_ge(xl_ready, j)
                            for k in range(R):
                                last = nc.tensor.transpose(p_t[:, k, :], xl[q][:, k, :], ident)
                            last.then_inc(t_done, 1)
                            pe.wait_ge(xt_ready, j)
                            for k in range(R):
                                nc.tensor.matmul(p_lg[:, bass.ds((j - 1) * (R * E0) + k * E0, E0)],
                                                 xt[q][:, k * P:(k + 1) * P], wgt[:, :],
                                                 start=True, stop=True)

                    pe.wait_ge(c_loaded, 32)
                    turns(pe, NB, body)

                @block.vector
                def _(dve):
                    dve.sem_inc(stored[0], 1)
                    dve.sem_inc(stored[1], 1)

                    def body(i, p, front, back):
                        j = i + p
                        q = 1 - p
                        if front:
                            rows = xtok[:, bass.ds(R * j, R), :]
                            dve.wait_ge(sel_done, j + 1)
                            nc.vector.tensor_tensor(rows, rows, p_sel[p][:, :, :], ALU.add).then_inc(x1_ready, 1)
                        if back:
                            dve.wait_ge(root_done, j)
                            dve.wait_ge(stored[q], 8 * i + 1 if p else 8 * i - 15)
                            for k in range(R):
                                last = nc.vector.tensor_scalar(xl[q][:, k, :], xtok[:, bass.ds(R * (j - 1) + k, 1), :],
                                                               mv[q][:, k, 0:1], root[q][:, k:k + 1],
                                                               ALU.subtract, ALU.mult)
                            last.then_inc(xl_ready, 1)
                        if front:
                            dve.wait_ge(x1_ready, j + 1)
                            dve.sem_inc(passed, 1)
                            for k in range(R):
                                last = nc.vector.bn_stats(st[p][:, k, :], xtok[:, bass.ds(R * j + k, 1), :])
                            last.then_inc(stat_s, 1)
                            dve.wait_ge(stat_s, j + 1)
                            dve.sem_inc(passed, 1)
                            for k in range(R):
                                last = nc.vector.bn_aggr(mv[p][:, k, :], st[p][:, k, :])
                            last.then_inc(mv_s, 1)
                            dve.wait_ge(mv_s, j + 1)
                            nc.vector.tensor_scalar(pre[p][:, :], mv[p][:, :, 1], 1e-5, None, ALU.add)\
                              .then_inc(pre_ready, 1)

                    turns(dve, NB, body)

        with ExitStack() as ctx:
            lg = alloc(ctx, "lg", [P, B, E0])
            bgs = alloc(ctx, "bgs", [P, E0])
            wide = alloc(ctx, "wide", [P, B, E0])
            mask = [alloc(ctx, f"mask{k}", [P, B, E0]) for k in range(2)]
            top_s = [alloc(ctx, f"top_s{k}", [P, B]) for k in range(2)]
            pm = alloc(ctx, "pm", [P, B])
            dif = alloc(ctx, "dif", [P, B])
            mb = alloc(ctx, "mb", [P, B, E0], F16)
            tot = alloc(ctx, "tot", [P, E0], F16)
            tu = alloc(ctx, "tu", [P, E0, B], F16)
            cnt_i = alloc(ctx, "cnt_i", [P, E0], I32)
            ntl = alloc(ctx, "ntl", [P, E0])
            b8 = alloc(ctx, "b8", [P, E0, E0])
            base = alloc(ctx, "base", [P, E0])
            end = alloc(ctx, "end", [P, E0])
            base_r = alloc(ctx, "base_r", [P, E0])
            posf = alloc(ctx, "posf", [P, E0, B])
            pos_f = alloc(ctx, "pos_f", [P, 2, B])
            lo_i = alloc(ctx, "lo_i", [P, 2, B], I32)
            hi_i = alloc(ctx, "hi_i", [P, 2, B], I32)
            lo_f = alloc(ctx, "lo_f", [P, 2, B])
            hi_f = alloc(ctx, "hi_f", [P, 2, B])
            tge = alloc(ctx, "tge", [P, NTP, E0])
            tex = alloc(ctx, "tex", [P, NTP])
            lp = [alloc(ctx, f"lp{k}", [P, P], F16) for k in range(4)]
            lt = [alloc(ctx, f"lt{k}", [P, P], F16) for k in range(4)]
            hh = [alloc(ctx, f"hh{k}", [P, NCOL], F16) for k in range(4)]
            zero = alloc(ctx, "zero", [P, NCOL], F16)
            idf = alloc(ctx, "idf", [P, NCOL])
            p_rank = bank(ctx, "p_rank", [P, E0, B])
            p_tot = bank(ctx, "p_tot", [P, 512])
            p_cnt = bank(ctx, "p_cnt", [P, 512])
            p_ip = bank(ctx, "p_ip", [P, 512])
            p_it = bank(ctx, "p_it", [P, 512])

            c_loaded = sem("s_consts_loaded")
            s = sem("s_steps")
            dif_ready = sem("s_dif_ready")
            exp_done = sem("s_exp_done")
            mb_ready = sem("s_mb_ready")
            tot_done = sem("s_tot_done")
            tot_ready = sem("s_tot_ready")
            tu_ready = sem("s_tu_ready")
            cnt_done = sem("s_cnt_done")
            rank_done = sem("s_rank_done")
            zero_set = sem("s_zero_set")
            hot_ready = sem("s_hot_ready")
            hot_used = sem("s_hot_used")
            ids_done = sem("s_ids_done")

            with nc.Block() as block:
                @block.sync
                def _(sp):
                    sp.dma_start(bgs[:, :], bg).then_inc(c_loaded, 16)

                @block.gpsimd
                def _(pool):
                    nc.gpsimd.memset(zero[:, :], 0.0).then_inc(zero_set, 1)

                @block.scalar
                def _(act):
                    act.wait_ge(dif_ready, 1)
                    nc.scalar.activation(dif[:, :], dif[:, :], ACT.Exp).then_inc(exp_done, 1)

                @block.tensor
                def _(pe):
                    ones16 = ch[:, CH_1:CH_1 + P]
                    pe.wait_ge(mb_ready, 1)
                    for e in range(E0):
                        last = nc.tensor.matmul(p_tot[:, e:e + 1], mb[:, :, e], ones16[:, 0:1], start=True, stop=True)
                    last.then_inc(tot_done, 1)
                    pe.wait_ge(tot_ready, 1)
                    nc.tensor.matmul(p_cnt[:, 0:E0], ones16, tot[:, :], start=True, stop=True).then_inc(cnt_done, 1)
                    pe.wait_ge(tu_ready, 1)
                    for h in range(2):
                        e = slice(h * E0 // 2, (h + 1) * E0 // 2)
                        nc.tensor.matmul(p_rank[:, e, :], ch[:, CH_U:CH_U + P],
                                         mb[:, :, e].rearrange("p b e -> p e b"), start=True, stop=False)
                        nc.tensor.matmul(p_rank[:, e, :], ones16, tu[:, e, :], start=False, stop=True)\
                          .then_inc(rank_done, 1)
                    pe.wait_ge(zero_set, 1)
                    for acc in (p_ip, p_it):
                        nc.tensor.matmul(acc[:, 0:NCOL], ch[:, CH_U:CH_U + P], zero[:, :], start=True, stop=False)
                    with pe.Fori(0, B - 1, 2) as i:
                        for p in range(2):
                            pe.wait_ge(hot_ready, i + p + 1)
                            for k in range(2):
                                nc.tensor.matmul(p_ip[:, 0:NCOL], lp[2 * p + k][:, :], hh[2 * p + k][:, :],
                                                 start=False, stop=False)
                                last = nc.tensor.matmul(p_it[:, 0:NCOL], lt[2 * p + k][:, :], hh[2 * p + k][:, :],
                                                        start=False, stop=False)
                            last.then_inc(hot_used, 1)
                    for acc in (p_ip, p_it):
                        nc.tensor.matmul(acc[:, 0:NCOL], ch[:, CH_U:CH_U + P], zero[:, :], start=False, stop=True)\
                          .then_inc(ids_done, 1)

                @block.vector
                def _(dve):
                    count = [0]

                    def step(ins):
                        count[0] += 1
                        ins.then_inc(s, 1)
                        dve.wait_ge(s, count[0])

                    pri = cf[:, CF_PRI:CF_PRI + E0].unsqueeze(1).to_broadcast([P, B, E0])
                    flat = lambda t: t[:, :, :].rearrange("p b e -> p (b e)")
                    dve.wait_ge(c_loaded, 16)
                    h = B // 2
                    nc.vector.tensor_tensor(lg[:, 0:h, :], p_lg[:, 0:h * E0].rearrange("p (b e) -> p b e", e=E0),
                                            bgs[:, :].unsqueeze(1).to_broadcast([P, h, E0]), ALU.add)
                    step(nc.vector.tensor_tensor(lg[:, h:B, :],
                                                 p_lg[:, h * E0:B * E0].rearrange("p (b e) -> p b e", e=E0),
                                                 bgs[:, :].unsqueeze(1).to_broadcast([P, h, E0]), ALU.add))
                    src = lg
                    for k in range(2):
                        step(nc.vector.tensor_reduce(top_s[k][:, :], src[:, :, :], AX.X, ALU.max))
                        step(nc.vector.tensor_tensor(wide[:, :, :], src[:, :, :],
                                                     top_s[k][:, :].unsqueeze(2).to_broadcast([P, B, E0]),
                                                     ALU.is_equal))
                        step(nc.vector.tensor_tensor(wide[:, :, :], wide[:, :, :], pri, ALU.mult))
                        step(nc.vector.tensor_reduce(pm[:, :], wide[:, :, :], AX.X, ALU.max))
                        step(nc.vector.tensor_tensor(mask[k][:, :, :], wide[:, :, :],
                                                     pm[:, :].unsqueeze(2).to_broadcast([P, B, E0]), ALU.is_equal))
                        if k == 0:
                            step(nc.vector.scalar_tensor_tensor(flat(lg), flat(mask[0]), BIG, flat(lg),
                                                                ALU.mult, ALU.add))
                    nc.vector.tensor_tensor(mb[:, :, :], mask[0][:, :, :], mask[1][:, :, :], ALU.add)\
                      .then_inc(mb_ready, 1)
                    nc.vector.tensor_tensor(dif[:, :], top_s[1][:, :], top_s[0][:, :], ALU.subtract)\
                      .then_inc(dif_ready, 1)
                    dve.wait_ge(tot_done, 1)
                    nc.vector.tensor_copy(tot[:, :], p_tot[:, 0:E0]).then_inc(tot_ready, 1)
                    nc.vector.tensor_tensor(tu[:, :, :], p_tot[:, 0:E0].unsqueeze(2).to_broadcast([P, E0, B]),
                                            ch[:, CH_U:CH_U + P].unsqueeze(1).to_broadcast([P, E0, B]), ALU.mult)\
                      .then_inc(tu_ready, 1)
                    dve.wait_ge(cnt_done, 1)
                    step(nc.vector.tensor_scalar(cnt_i[:, :], p_cnt[:, 0:E0], float(TILE - 1), None, ALU.add))
                    step(nc.vector.tensor_single_scalar(cnt_i[:, :], cnt_i[:, :], TILE.bit_length() - 1,
                                                        ALU.logical_shift_right))
                    step(nc.vector.tensor_copy(ntl[:, :], cnt_i[:, :]))
                    step(nc.vector.tensor_tensor(b8[:, :, :], ntl[:, :].unsqueeze(1).to_broadcast([P, E0, E0]),
                                                 cf[:, CF_B8:CF_B8 + E0 * E0].rearrange("p (a b) -> p a b", b=E0),
                                                 ALU.mult))
                    step(nc.vector.tensor_reduce(base[:, :], b8[:, :, :], AX.X, ALU.add))
                    nc.vector.tensor_tensor(end[:, :], base[:, :], ntl[:, :], ALU.add)
                    step(nc.vector.tensor_scalar(base_r[:, :], base[:, :], float(TILE), None, ALU.mult))
                    step(nc.vector.tensor_tensor(tge[:, :, :],
                                                 cf[:, CF_J:CF_J + NTP].unsqueeze(2).to_broadcast([P, NTP, E0]),
                                                 end[:, :].unsqueeze(1).to_broadcast([P, NTP, E0]), ALU.is_ge))
                    step(nc.vector.tensor_reduce(tex[:, :], tge[:, :, :], AX.X, ALU.add))
                    step(nc.vector.tensor_scalar(texp[:, :], tex[:, :], float(E0 - 1), None, ALU.min))
                    for hb in range(2):
                        dve.wait_ge(rank_done, hb + 1)
                        e = slice(hb * E0 // 2, (hb + 1) * E0 // 2)
                        step(nc.vector.tensor_tensor(posf[:, e, :], p_rank[:, e, :],
                                                     base_r[:, e].unsqueeze(2).to_broadcast([P, E0 // 2, B]), ALU.add))
                    for k in range(2):
                        step(nc.vector.tensor_tensor(wide[:, :, :], mask[k][:, :, :],
                                                     posf[:, :, :].rearrange("p e b -> p b e"), ALU.mult))
                        step(nc.vector.tensor_reduce(pos_f[:, k, :], wide[:, :, :], AX.X, ALU.add))
                    step(nc.vector.tensor_copy(pos_i[:, :, :], pos_f[:, :, :]))
                    nc.vector.tensor_single_scalar(lo_i[:, :, :], pos_i[:, :, :], P - 1, ALU.bitwise_and)
                    step(nc.vector.tensor_single_scalar(hi_i[:, :, :], pos_i[:, :, :], P.bit_length() - 1,
                                                        ALU.logical_shift_right))
                    nc.vector.tensor_copy(lo_f[:, :, :], lo_i[:, :, :])
                    step(nc.vector.tensor_copy(hi_f[:, :, :], hi_i[:, :, :]))
                    dve.wait_ge(exp_done, 1)
                    step(nc.vector.tensor_scalar(pm[:, :], dif[:, :], 1.0, None, ALU.add))
                    step(nc.vector.reciprocal(prob[:, 0, :], pm[:, :]))
                    step(nc.vector.tensor_tensor(prob[:, 1, :], dif[:, :], prob[:, 0, :], ALU.mult))

                    iota = ch[:, CH_I:CH_I + P]
                    iota_h = ch[:, CH_H:CH_H + NCOL]

                    def one_hots(j, p):
                        for k in range(2):
                            m = 2 * p + k
                            nc.vector.tensor_scalar(lp[m][:, :], iota, lo_f[:, k, bass.ds(j, 1)],
                                                    cf[:, CF_P:CF_P + 1], ALU.is_equal, ALU.mult)
                            nc.vector.tensor_scalar(lt[m][:, :], iota, lo_f[:, k, bass.ds(j, 1)],
                                                    cf[:, bass.ds(j + CF_T, 1)], ALU.is_equal, ALU.mult)
                            last = nc.vector.tensor_scalar(hh[m][:, :], iota_h, hi_f[:, k, bass.ds(j, 1)], None,
                                                           ALU.is_equal)
                        last.then_inc(hot_ready, 1)

                    one_hots(0, 0)
                    one_hots(1, 1)
                    with dve.Fori(2, B - 1, 2) as i:
                        for p in range(2):
                            dve.wait_ge(hot_used, i + p - 1)
                            one_hots(i + p, p)
                    dve.wait_ge(ids_done, 2)
                    step(nc.vector.tensor_scalar(idf[:, :], p_it[:, 0:NCOL], float(P), None, ALU.mult))
                    step(nc.vector.tensor_tensor(idf[:, :], idf[:, :], p_ip[:, 0:NCOL], ALU.add))
                    step(nc.vector.tensor_copy(ids[:, :], idf[:, :]))
        lgp.close()

        with ExitStack() as ctx:
            wall = alloc(ctx, "wall", [P, E0, EW])
            wc = [alloc(ctx, f"wc{p}", [P, EW]) for p in range(2)]
            xg = [alloc(ctx, f"exg{p}", [P, R, D]) for p in range(2)]
            xt = [alloc(ctx, f"ext{p}", [P, W]) for p in range(2)]
            ht = [alloc(ctx, f"eht{p}", [P, HC, W]) for p in range(2)]
            yt = [alloc(ctx, f"eyt{p}", [P, W]) for p in range(2)]
            yo = [alloc(ctx, f"eyo{p}", [P, R, D]) for p in range(2)]
            idx = [alloc(ctx, f"eidx{p}", [P, R], I32) for p in range(2)]
            p_x = bank(ctx, "p_ex", [P, R, D])
            p_h = [bank(ctx, f"p_eh{c}", [P, W]) for c in range(HC)]
            p_y = [bank(ctx, f"p_ey{p}", [P, W]) for p in range(2)]
            p_yo = bank(ctx, "p_eyo", [P, R, D])
            w1 = lambda p, c: wc[p][:, c * P:(c + 1) * P]
            w2 = lambda p, c: wc[p][:, H0 + c * D:H0 + (c + 1) * D]
            CB1 = H0 + HC * D

            w_loaded = sem("e_w_loaded")
            wc_ready = sem("e_wc_ready")
            gathered = pair("e_gathered")
            idx_ready = sem("e_idx_ready")
            x_done = sem("e_x_done")
            xt_ready = sem("e_xt_ready")
            h_done = sem("e_h_done")
            ht_ready = sem("e_ht_ready")
            y_done = sem("e_y_done")
            yt_ready = sem("e_yt_ready")
            yo_done = sem("e_yo_done")
            yo_ready = sem("e_yo_ready")
            stored = pair("e_stored")

            with nc.Block() as block:
                @block.sync
                def _(sp):
                    sp.dma_start(wall[:, :, :], w_exp).then_inc(w_loaded, 16)
                    dst = y_d.rearrange("(t p) d -> p t d", p=P)
                    with sp.Fori(0, NTP - 1, 2) as i:
                        for p in range(2):
                            sp.wait_ge(yo_ready, i + p + 1)
                            sp.dma_start(dst[:, bass.ds((i + p) * R, R), :], yo[p][:, :, :]).then_inc(stored[p], 16)
                    for p in range(2):
                        sp.wait_ge(stored[p], 8 * NTP + 1)

                @block.gpsimd
                def _(pool):
                    def gather(j, p):
                        nc.gpsimd.tensor_copy(idx[p][:, :], ids[:, bass.ds(j * R, R)]).then_inc(idx_ready, 1)
                        pool.wait_ge(idx_ready, j + 1)
                        pool.sem_inc(passed, 1)
                        for k in range(R):
                            pool.indirect_dma_start(
                                out=xg[p][:, k, :], out_offset=None, in_=xln_d,
                                in_offset=bass.IndirectOffsetOnAxis(ap=idx[p][:, k:k + 1], axis=0))\
                                .then_inc(gathered[p], 16)

                    gather(0, 0)
                    gather(1, 1)
                    with pool.Fori(2, NTP - 1, 2) as i:
                        for p in range(2):
                            pool.wait_ge(x_done, i + p - 1)
                            gather(i + p, p)

                @block.scalar
                def _(act):
                    def evacuate(j, p):
                        act.wait_ge(x_done, j + 1)
                        nc.scalar.activation(xt[p][:, :], p_x[:, :, :].rearrange("p r d -> p (r d)"), ACT.Copy)\
                          .then_inc(xt_ready, 1)

                    def hidden(j, p):
                        for c in range(HC):
                            act.wait_ge(h_done, HC * j + c + 1)
                            nc.scalar.activation(ht[p][:, c, :], p_h[c][:, :], ACT.Relu,
                                                 bias=wc[p][:, CB1 + c:CB1 + c + 1]).then_inc(ht_ready, 1)

                    evacuate(0, 0)
                    with act.Fori(0, NTP - 3, 2) as i:
                        for p in range(2):
                            hidden(i + p, p)
                            evacuate(i + p + 1, 1 - p)
                    hidden(NTP - 2, 0)
                    evacuate(NTP - 1, 1)
                    hidden(NTP - 1, 1)

                @block.tensor
                def _(pe):
                    def transpose_x(j, p, half):
                        pe.wait_ge(gathered[p], half * 16 * R + 16 * R)
                        for k in range(R):
                            last = nc.tensor.transpose(p_x[:, k, :], xg[p][:, k, :], ident)
                        last.then_inc(x_done, 1)

                    def up(j, p, c):
                        nc.tensor.matmul(p_h[c][:, :], w1(p, c), xt[p][:, :], start=True, stop=True).then_inc(h_done, 1)

                    def down(j, p, c):
                        pe.wait_ge(ht_ready, HC * j + c + 1)
                        last = nc.tensor.matmul(p_y[p][:, :], w2(p, c), ht[p][:, c, :], start=(c == 0),
                                                stop=(c == HC - 1))
                        if c == HC - 1:
                            last.then_inc(y_done, 1)

                    def transpose_y(j, p):
                        pe.wait_ge(yt_ready, j + 1)
                        for k in range(R):
                            last = nc.tensor.transpose(p_yo[:, k, :], yt[p][:, k * P:(k + 1) * P], ident)
                        last.then_inc(yo_done, 1)

                    def turn(i, p, after, before):
                        j = i + p
                        pe.wait_ge(wc_ready, j + 1)
                        pe.wait_ge(xt_ready, j + 1)
                        up(j, p, 0)
                        up(j, p, 1)
                        down(j, p, 0)
                        up(j, p, 2)
                        down(j, p, 1)
                        up(j, p, 3)
                        if after:
                            if isinstance(i, int):
                                transpose_x(j + 1, 1 - p, (j + 1) // 2)
                            else:
                                pe.wait_ge(gathered[1 - p], (i + 2 * p) * (8 * R) + 16 * R)
                                for k in range(R):
                                    last = nc.tensor.transpose(p_x[:, k, :], xg[1 - p][:, k, :], ident)
                                last.then_inc(x_done, 1)
                        down(j, p, 2)
                        if before:
                            transpose_y(j - 1, 1 - p)
                        down(j, p, 3)

                    transpose_x(0, 0, 0)
                    turn(0, 0, True, False)
                    turn(0, 1, True, True)
                    with pe.Fori(2, NTP - 3, 2) as i:
                        turn(i, 0, True, True)
                        turn(i, 1, True, True)
                    turn(NTP - 2, 0, True, True)
                    turn(NTP - 2, 1, False, True)
                    transpose_y(NTP - 1, 1)

                @block.vector
                def _(dve):
                    dve.sem_inc(stored[0], 1)
                    dve.sem_inc(stored[1], 1)

                    def take(j, p):
                        e = dve.value_load(texp[0:1, bass.ds(j, 1)], min_val=0, max_val=E0 - 1)
                        nc.vector.tensor_copy(wc[p][:, :], wall[:, bass.ds(e, 1), :].rearrange("p a w -> p (a w)"))\
                          .then_inc(wc_ready, 1)

                    def rows(i, p):
                        j = i + p
                        dve.wait_ge(y_done, j + 1)
                        nc.vector.tensor_scalar(yt[p][:, :], p_y[p][:, :], wc[p][:, CB1 + HC:CB1 + HC + 1], None,
                                                ALU.add).then_inc(yt_ready, 1)

                    def turned(i, p):
                        j = i + p
                        dve.wait_ge(yo_done, j + 1)
                        dve.wait_ge(stored[p], 8 * i + 1)
                        nc.vector.tensor_copy(yo[p][:, :, :], p_yo[:, :, :]).then_inc(yo_ready, 1)

                    dve.wait_ge(w_loaded, 16)
                    take(0, 0)
                    take(1, 1)
                    with dve.Fori(0, NTP - 3, 2) as i:
                        for p in range(2):
                            rows(i, p)
                            dve.wait_ge(yt_ready, i + p + 1)
                            take(i + p + 2, p)
                            turned(i, p)
                    for p in range(2):
                        rows(NTP - 2, p)
                        turned(NTP - 2, p)

        with ExitStack() as ctx:
            NB = B // R
            wgcn = alloc(ctx, "wgcn", [P, D])
            bgcn = alloc(ctx, "bgcn", [P, D])
            maskt = alloc(ctx, "maskt", [P, B])
            ws = alloc(ctx, "ws", [P, 3 * P])
            bs = alloc(ctx, "bs", [P, 2])
            w1 = alloc(ctx, "w1", [P, E1, P])
            w2 = alloc(ctx, "w2", [P, E1, P // 2])
            w3 = alloc(ctx, "w3", [P, 2, D])
            be = alloc(ctx, "be", [P, E1 + 2])
            vraw = alloc(ctx, "vraw", [KV, R, D])
            vout = alloc(ctx, "vout", [KV, R, D], F32R)
            gws = alloc(ctx, "gws", [P, E1])
            gbs = alloc(ctx, "gbs", [P, E1])
            selraw = alloc(ctx, "selraw", [2 * R * E1, R, 2, P])
            selp = alloc(ctx, "selp", [2 * R * E1, R, 2, P], F32R)
            ones = alloc(ctx, "ones_l", [P, 1])
            at = [alloc(ctx, f"at{p}", [P, R, P]) for p in range(2)]
            yg = [alloc(ctx, f"yg{p}", [P, 2, R, D]) for p in range(2)]
            idx = [alloc(ctx, f"idx{p}", [P, 2, R], I32) for p in range(2)]
            st = [alloc(ctx, f"st_l{k}", [P, R, 6]) for k in range(2)]
            mv = [alloc(ctx, f"mv_l{k}", [P, R, 2]) for k in range(2)]
            pre = [alloc(ctx, f"pre_l{k}", [P, 2 * R]) for k in range(2)]
            root = [alloc(ctx, f"root_l{k}", [P, 2 * R]) for k in range(2)]
            rd = alloc(ctx, "rd", [P, R])
            nb = [alloc(ctx, f"nb{k}", [P, R]) for k in range(2)]
            dm = alloc(ctx, "dm", [P, R])
            xn = [alloc(ctx, f"xn{k}", [P, R, D]) for k in range(2)]
            x3t = alloc(ctx, "x3t", [P, W])
            x4t = alloc(ctx, "x4t", [P, W])
            gg = alloc(ctx, "gg", [P, R, D])
            gr = alloc(ctx, "gr", [P, R, D])
            hs = [alloc(ctx, f"hs{k}", [P, W]) for k in range(2)]
            he = [alloc(ctx, f"he{e}", [P, W]) for e in range(E1)]
            rp = [alloc(ctx, f"rp{k}", [P, W]) for k in range(2)]
            rc = [alloc(ctx, f"rc{k}", [P, W]) for k in range(2)]
            cw = alloc(ctx, "cw", [P, R, E1])
            cws = alloc(ctx, "cws", [P, P // (R * E1), R, E1], F32R)
            cwt = alloc(ctx, "cwt", [KV, P], F32R)
            outx = [alloc(ctx, f"outx{p}", [P, R, D]) for p in range(2)]
            sm = [alloc(ctx, f"sm{k}", [P, R, E1]) for k in range(6)]
            sv = [alloc(ctx, f"sv{k}", [P, R]) for k in range(8)]
            p_h = [bank(ctx, f"p_lh{k}", [P, W]) for k in range(2)]
            p_t = bank(ctx, "p_lt", [P, R, D])
            p_hl = bank(ctx, "p_hl", [P, R, D])
            p_ag = bank(ctx, "p_ag", [P, R, D])
            p_sm = bank(ctx, "p_sm", [P, 512])
            p_cb = bank(ctx, "p_cb", [P, R, D])
            p_out = bank(ctx, "p_out", [P, R, D])
            LG, CT = 16, P
            flat = lambda t: t[:, :, :].rearrange("p r d -> p (r d)")

            c_loaded = sem("l_consts_loaded")
            set_ = sem("l_set")
            v_s = sem("l_v_s")
            cw_s = sem("l_cw_s")
            a_loaded = pair("l_a_loaded")
            gathered = pair("l_gathered")
            idx_ready = sem("l_idx_ready")
            a_ready = sem("l_a_ready")
            x2_ready = sem("l_x2_ready")
            deg_done = sem("l_deg_done")
            pre_ready = [sem(f"l_pre_ready{k}") for k in range(2)]
            root_done = [sem(f"l_root_done{k}") for k in range(2)]
            nb_ready = [sem(f"l_nb_ready{k}") for k in range(2)]
            ln = [sem(f"l_norm_steps{k}") for k in range(2)]
            x3_ready = sem("l_x3_ready")
            rd_ready = sem("l_rd_ready")
            weigh = sem("l_weigh_steps")
            sx = sem("l_router_steps")
            xn_ready = [sem(f"l_xn_ready{k}") for k in range(2)]
            t_done = sem("l_t_done")
            x3t_ready = sem("l_x3t_ready")
            x4t_ready = sem("l_x4t_ready")
            hl_done = sem("l_hl_done")
            gg_ready = sem("l_gg_ready")
            ag_done = sem("l_ag_done")
            gr_ready = sem("l_gr_ready")
            lg_done = sem("l_lg_done")
            d_ready = sem("l_d_ready")
            exp_done = sem("l_exp_done")
            cw_ready = sem("l_cw_ready")
            ct_done = sem("l_ct_done")
            cwt_ready = sem("l_cwt_ready")
            cb_done = sem("l_cb_done")
            h_done = sem("l_h_done")
            h_ready = sem("l_h_ready")
            rc_ready = sem("l_rc_ready")
            out_done = sem("l_out_done")
            out_ready = sem("l_out_ready")
            stored = pair("l_stored")
            SX = 17
            NC = 13

            with nc.Block() as block:
                @block.sync
                def _(sp):
                    def load(j, p):
                        sp.dma_start(at[p][:, :, :], a_t[:, bass.ds(R * j, R), :]).then_inc(a_loaded[p], 16)

                    def store(j, p):
                        sp.wait_ge(out_ready, j + 2)
                        sp.dma_start(out.rearrange("b n d -> n b d")[:, bass.ds(R * j, R), :], outx[p][:, :, :])\
                          .then_inc(stored[p], 16)

                    load(0, 0)
                    load(1, 1)
                    for dst, src in ((wgcn[:, :], w_gcn), (bgcn[:, :], b_gcn), (maskt[:, :], mask_t),
                                     (ws[:, :], w_s), (bs[:, :], b_s), (w1[:, :, :], e_w1), (w2[:, :, :], e_w2),
                                     (w3[:, :, :], e_w3), (be[:, :], b_e), (vraw[:, :, :], b_out),
                                     (gws[:, :], gw), (gbs[:, :], gb), (selraw[:, :, :, :], selp_d)):
                        sp.dma_start(dst, src).then_inc(c_loaded, 16)
                    sp.wait_ge(ag_done, 1)
                    load(2, 0)
                    with sp.Fori(0, NB - 5, 2) as i:
                        for p in range(2):
                            sp.wait_ge(ag_done, i + p + 2)
                            load(i + p + 3, 1 - p)
                            store(i + p, p)
                    sp.wait_ge(ag_done, NB - 2)
                    load(NB - 1, 1)
                    for j in range(NB - 4, NB):
                        store(j, j % 2)
                    for p in range(2):
                        sp.wait_ge(stored[p], 8 * NB + 1)

                @block.gpsimd
                def _(pool):
                    def gather(j, p):
                        nc.gpsimd.tensor_copy(idx[p][:, :, :], pos_i[:, :, bass.ds(R * j, R)]).then_inc(idx_ready, 1)
                        pool.wait_ge(idx_ready, j + 1)
                        pool.sem_inc(passed, 1)
                        for c in range(2):
                            for k in range(R):
                                pool.indirect_dma_start(
                                    out=yg[p][:, c, k, :], out_offset=None, in_=y_d,
                                    in_offset=bass.IndirectOffsetOnAxis(ap=idx[p][:, c, k:k + 1], axis=0))\
                                    .then_inc(gathered[p], 16)

                    def plus_one(j, p, n):
                        pool.wait_ge(a_loaded[p], n)
                        nc.gpsimd.tensor_tensor(at[p][:, :, :], at[p][:, :, :],
                                                ident.unsqueeze(1).to_broadcast([P, R, P]), ALU.add)\
                          .then_inc(a_ready, 1)

                    def roots(n, k):
                        pool.wait_ge(pre_ready[k], n)
                        w = (2 - k) * R
                        nc.gpsimd.tensor_tensor(root[k][:, 0:w], pre[k][:, 0:w], mhalf[:, 0:w], ALU.pow)\
                          .then_inc(root_done[k], 1)

                    gather(0, 0)
                    plus_one(0, 0, 16)
                    gather(1, 1)
                    plus_one(1, 1, 16)
                    roots(1, 0)
                    pool.wait_ge(x2_ready, 2)
                    gather(2, 0)
                    with pool.Fori(1, NB - 4, 2) as i:
                        for p in range(2):
                            j = i + p
                            plus_one(j + 1, p, 8 * i + 24)
                            roots(j, 1)
                            roots(j + 1, 0)
                            pool.wait_ge(x2_ready, 2 * j + 2)
                            gather(j + 2, 1 - p)
                    plus_one(NB - 2, 0, 8 * NB)
                    roots(NB - 3, 1)
                    roots(NB - 2, 0)
                    pool.wait_ge(x2_ready, 2 * (NB - 3) + 2)
                    gather(NB - 1, 1)
                    plus_one(NB - 1, 1, 8 * NB)
                    for j in (NB - 2, NB - 1):
                        roots(j, 1)
                        roots(j + 1, 0)
                    roots(NB, 1)

                @block.scalar
                def _(act):
                    act.sem_inc(stored[0], 1)
                    act.sem_inc(stored[1], 1)
                    act.wait_ge(c_loaded, 16 * NC)
                    act.wait_ge(set_, 2)

                    def relu(c, u, dst, bias):
                        act.wait_ge(h_done, 8 * c + u + 1)
                        nc.scalar.activation(dst, p_h[u % 2][:, :], ACT.Relu, bias=bias).then_inc(h_ready, 1)

                    def normalise(j, k, scale):
                        act.wait_ge(nb_ready[k], j + 1)
                        act.sem_inc(passed, 1)
                        for r in range(R):
                            last = nc.scalar.activation(
                                xn[k][:, r, :], xtok[:, bass.ds(R * j + r, 1), :].rearrange("p a d -> p (a d)"),
                                ACT.Identity, scale=scale[:, r:r + 1], bias=nb[k][:, r:r + 1])
                        last.then_inc(xn_ready[k], 1)

                    def body(i, p, first, middle, back):
                        j = i + p
                        if middle:
                            act.wait_ge(t_done, 2 * j - 1)
                            nc.scalar.activation(x3t[:, :], flat(p_t), ACT.Copy).then_inc(x3t_ready, 1)
                        if back:
                            relu(j - 2, 0, he[0][:, :], be[:, 0:1])
                            act.wait_ge(d_ready, 2 * j - 3)
                            nc.scalar.activation(sm[1][:, :, :], sm[1][:, :, :], ACT.Exp).then_inc(exp_done, 1)
                            relu(j - 2, 1, he[1][:, :], be[:, 1:2])
                        if middle:
                            act.wait_ge(ag_done, j)
                            for k in range(R):
                                last = nc.scalar.activation(gr[:, k, :], p_ag[:, k, :], ACT.Relu, scale=dm[:, k:k + 1])
                            last.then_inc(gr_ready, 1)
                        if back:
                            relu(j - 2, 2, he[2][:, :], be[:, 2:3])
                            relu(j - 2, 3, he[3][:, :], be[:, 3:4])
                            act.wait_ge(d_ready, 2 * j - 2)
                            nc.scalar.activation(sv[4][:, :], sv[4][:, :], ACT.Exp).then_inc(exp_done, 1)
                            relu(j - 2, 4, hs[0][:, :], bs[:, 0:1])
                            relu(j - 2, 5, rp[0][:, :], be[:, E1:E1 + 1])
                            relu(j - 2, 6, rp[1][:, :], be[:, E1 + 1:E1 + 2])
                            relu(j - 2, 7, hs[1][:, :], bs[:, 1:2])
                            act.wait_ge(ct_done, j - 1)
                            nc.scalar.activation(cwt[0:3 * R * E1, :], p_sm[0:3 * R * E1, CT:CT + P], ACT.Copy)\
                              .then_inc(cwt_ready, 1)
                        if middle:
                            normalise(j - 1, 1, root[1])
                            act.wait_ge(t_done, 2 * j)
                            nc.scalar.activation(x4t[:, :], flat(p_t), ACT.Copy).then_inc(x4t_ready, 1)
                        if first:
                            normalise(j, 0, rd)

                    turns3(act, NB, body)

                @block.tensor
                def _(pe):
                    def product(c, u, mms):
                        pe.wait_ge(h_ready, 8 * c + u + 1)
                        for dst, lhs, rhs in mms:
                            last = nc.tensor.matmul(dst, lhs, rhs, start=True, stop=True)
                        last.then_inc(h_done, 1)

                    def spread(dst, pair_):
                        for k in range(R):
                            last = nc.tensor.matmul(dst[:, k, :], selp[:, k, pair_, :], cwt[0:2 * R * E1, :],
                                                    start=True, stop=True)
                        last.then_inc(cb_done, 1)

                    def up(c, e):
                        product(c, e, [(p_h[e % 2][:, :], w1[:, e, :], x4t[:, :])])

                    def second(c, u, pair_):
                        a = 2 * pair_
                        product(c, u, [(p_h[u % 2][0:64, :], w2[:, a, :], he[a][:, :]),
                                       (p_h[u % 2][64:128, :], w2[:, a + 1, :], he[a + 1][:, :])])

                    def body(i, p, first, middle, back):
                        j = i + p
                        c = j - 2
                        q = 1 - p
                        if middle:
                            pe.wait_ge(xn_ready[0], j)
                            for k in range(R):
                                last = nc.tensor.transpose(p_t[:, k, :], xn[0][:, k, :], ident)
                            last.then_inc(t_done, 1)
                        if back:
                            up(c, 0)
                        if middle:
                            pe.wait_ge(x3t_ready, j)
                            for k in range(R):
                                last = nc.tensor.matmul(p_hl[:, k, :], x3t[:, k * P:(k + 1) * P], wgcn[:, :],
                                                        start=True, stop=True)
                            last.then_inc(hl_done, 1)
                        if first:
                            if back:
                                pe.wait_ge(sx, SX * c + 1)
                            pe.wait_ge(a_ready, j + 1)
                            for k in range(R):
                                last = nc.tensor.matmul(p_sm[:, k:k + 1], at[p][:, k, :], ones[:, :],
                                                        start=True, stop=True)
                            last.then_inc(deg_done, 1)
                        if back:
                            up(c, 1)
                        if middle:
                            pe.wait_ge(gg_ready, j)
                            for k in range(R):
                                last = nc.tensor.matmul(p_ag[:, k, :], at[q][:, k, :], gg[:, k, :],
                                                        start=True, stop=True)
                            last.then_inc(ag_done, 1)
                        if back:
                            up(c, 2)
                            up(c, 3)
                            product(c, 4, [(p_h[0][:, :], ws[:, 0:P], x4t[:, :])])
                        if back:
                            second(c, 5, 0)
                            second(c, 6, 1)
                            product(c, 7, [(p_h[1][:, :], ws[:, P:2 * P], hs[0][:, :])])
                            pe.wait_ge(cw_ready, j - 1)
                            nc.tensor.transpose(p_sm[:, CT:CT + P],
                                                cws[:, :, :, :].rearrange("p c r e -> p (c r e)").bitcast(F32),
                                                ident).then_inc(ct_done, 1)
                            pe.wait_ge(cwt_ready, j - 1)
                            spread(p_cb, 0)
                            spread(p_hl, 1)
                            pe.wait_ge(out_ready, c + 1)
                            nc.tensor.matmul(flat(p_out), cwt[:, :], flat(vout), start=True, stop=False)
                            pe.wait_ge(h_ready, 8 * c + 10)
                            for k in range(R):
                                nc.tensor.matmul(p_out[:, k, :], hs[1][:, k * P:(k + 1) * P], ws[:, 2 * P:3 * P],
                                                 start=False, stop=False)
                        if middle:
                            pe.wait_ge(xn_ready[1], j)
                            for k in range(R):
                                last = nc.tensor.transpose(p_t[:, k, :], xn[1][:, k, :], ident)
                            last.then_inc(t_done, 1)
                        if back:
                            for u in range(2):
                                pe.wait_ge(rc_ready, 2 * c + u + 1)
                                for k in range(R):
                                    last = nc.tensor.matmul(p_out[:, k, :], rc[u][:, k * P:(k + 1) * P], w3[:, u, :],
                                                            start=False, stop=(u == 1 and k == R - 1))
                            last.then_inc(out_done, 1)
                        if middle:
                            pe.wait_ge(x4t_ready, j)
                            for k in range(R):
                                last = nc.tensor.matmul(p_sm[:, LG + k * E1:LG + (k + 1) * E1],
                                                        x4t[:, k * P:(k + 1) * P], gws[:, :], start=True, stop=True)
                            last.then_inc(lg_done, 1)

                    pe.wait_ge(set_, 4)
                    pe.wait_ge(c_loaded, 16 * NC)
                    turns3(pe, NB, body)

                @block.vector
                def _(dve):
                    dve.sem_inc(h_ready, 2)
                    dve.sem_inc(out_ready, 1)
                    nc.vector.memset(ones[:, :], 1.0).then_inc(set_, 1)
                    nc.vector.memset(outx[1][:, 0, :], 1.0)
                    nc.vector.memset(outx[0][:, 0, :], 0.0).then_inc(v_s, 1)
                    dve.wait_ge(v_s, 1)
                    nc.vector.tensor_copy(cwt[:, :], outx[1][0:KV, 0, :])
                    nc.vector.tensor_copy(cws[:, :, :, :].rearrange("p c r e -> p (c r e)"), outx[0][:, 0, :])\
                      .then_inc(set_, 1)
                    dve.wait_ge(c_loaded, 16 * NC)
                    nc.vector.tensor_copy(selp[:, :, :, :], selraw[:, :, :, :])
                    nc.vector.tensor_copy(vout[:, :, :], vraw[:, :, :]).then_inc(v_s, 1)
                    dve.wait_ge(v_s, 2)
                    for a, b in ((32, 64), (96, 97)):
                        hi = vout[a:b, :, :].bitcast(F32)
                        nc.vector.tensor_tensor(vout[a:b, :, :], vraw[a:b, :, :], hi, ALU.subtract)\
                          .then_inc(set_, 1)
                    pri = cf[:, CF_PRI + E0 - E1:CF_PRI + E0].unsqueeze(1).to_broadcast([P, R, E1])
                    over = lambda v: v[:, :].unsqueeze(2).to_broadcast([P, R, E1])
                    row = lambda j, r: xtok[:, bass.ds(R * j + r, 1), :].rearrange("p a d -> p (a d)")

                    def largest(src, v):
                        return nc.vector.tensor_reduce(v[:, :], src[:, :, :], AX.X, ALU.max)

                    def same(dst, src, v):
                        return nc.vector.tensor_tensor(dst[:, :, :], src[:, :, :], over(v), ALU.is_equal)

                    def times(dst, src, w):
                        return nc.vector.tensor_tensor(dst[:, :, :], src[:, :, :], w, ALU.mult)

                    def body(i, p, first, middle, back):
                        j = i + p
                        b = j - 1

                        def router(ins):
                            ins.then_inc(sx, 1)

                        def after(n):
                            dve.wait_ge(sx, SX * (j - 2) + n)

                        def choice(c, r):
                            ins = nc.vector.scalar_tensor_tensor(row(j, r), yg[p][:, c, r, :],
                                                                 prob[:, c, bass.ds(R * j + r, 1)], row(j, r),
                                                                 ALU.mult, ALU.add)
                            if r == R - 1:
                                ins.then_inc(x2_ready, 1)

                        def gcn_rows(r):
                            ins = nc.vector.scalar_tensor_tensor(gg[:, r, :], bgcn[:, :],
                                                                 root[0][:, R + r:R + r + 1], p_hl[:, r, :],
                                                                 ALU.mult, ALU.add)
                            if r == R - 1:
                                ins.then_inc(gg_ready, 1)

                        def stats(n, k, r):
                            ins = nc.vector.bn_stats(st[k][:, r, :], row(n, r))
                            if r == R - 1:
                                ins.then_inc(ln[k], 1)

                        if back:
                            dve.wait_ge(lg_done, j - 1)
                            router(nc.vector.tensor_tensor(sm[0][:, :, :],
                                                           p_sm[:, LG:LG + R * E1].rearrange("p (r e) -> p r e", e=E1),
                                                           gbs[:, :].unsqueeze(1).to_broadcast([P, R, E1]), ALU.add))
                        if first:
                            dve.wait_ge(gathered[p], 64 * i + 128)
                            choice(0, 0)
                        if back:
                            after(1)
                            router(largest(sm[0], sv[0]))
                        if first:
                            choice(0, 1)
                        if back:
                            after(2)
                            nc.vector.tensor_tensor(sm[1][:, :, :], sm[0][:, :, :], over(sv[0]), ALU.subtract)\
                              .then_inc(d_ready, 1)
                        if first:
                            choice(0, 2)
                        if middle:
                            dve.wait_ge(hl_done, j)
                            gcn_rows(0)
                            gcn_rows(1)
                        if back:
                            dve.wait_ge(exp_done, 2 * j - 3)
                            router(nc.vector.tensor_reduce(sv[1][:, :], sm[1][:, :, :], AX.X, ALU.add))
                        if middle:
                            gcn_rows(2)
                        if back:
                            after(3)
                            router(nc.vector.reciprocal(sv[1][:, :], sv[1][:, :]))
                        if middle:
                            gcn_rows(3)
                        if back:
                            after(4)
                            router(times(sm[2], sm[1], over(sv[1])))
                        if first:
                            choice(0, 3)
                        if back:
                            after(5)
                            router(largest(sm[2], sv[2]))
                        if first:
                            dve.wait_ge(deg_done, j + 1)
                            nc.vector.tensor_scalar(pre[0][:, R:2 * R], p_sm[:, 0:R], 1e-8, None, ALU.add)
                            dve.wait_ge(x2_ready, 2 * j + 1)
                            choice(1, 0)
                        if back:
                            after(6)
                            router(same(sm[4], sm[2], sv[2]))
                        if first:
                            choice(1, 1)
                        if back:
                            after(7)
                            router(times(sm[4], sm[4], pri))
                        if first:
                            choice(1, 2)
                        if back:
                            after(8)
                            router(largest(sm[4], sv[7]))
                        if first:
                            choice(1, 3)
                        if back:
                            after(9)
                            router(same(sm[3], sm[4], sv[7]))
                        if first:
                            dve.wait_ge(x2_ready, 2 * j + 2)
                            dve.sem_inc(passed, 1)
                            stats(j, 0, 0)
                        if back:
                            after(10)
                            router(nc.vector.scalar_tensor_tensor(flat(sm[2]), flat(sm[3]), BIG, flat(sm[2]),
                                                                  ALU.mult, ALU.add))
                        if first:
                            stats(j, 0, 1)
                        if back:
                            after(11)
                            router(largest(sm[2], sv[3]))
                        if middle:
                            dve.wait_ge(gr_ready, j)
                            batch = xtok[:, bass.ds(R * b, R), :]
                            nc.vector.tensor_tensor(batch, batch, gr[:, :, :], ALU.add).then_inc(x3_ready, 1)
                        if back:
                            after(12)
                            nc.vector.tensor_tensor(sv[4][:, :], sv[3][:, :], sv[2][:, :], ALU.subtract)\
                              .then_inc(d_ready, 1)
                            router(same(sm[4], sm[2], sv[3]))
                        if middle:
                            dve.wait_ge(x3_ready, j)
                            dve.sem_inc(passed, 1)
                            stats(b, 1, 0)
                        if back:
                            after(13)
                            router(times(sm[4], sm[4], pri))
                        if middle:
                            stats(b, 1, 1)
                        if back:
                            after(14)
                            router(largest(sm[4], sv[7]))
                        if middle:
                            stats(b, 1, 2)
                        if back:
                            dve.wait_ge(exp_done, 2 * j - 2)
                            router(nc.vector.tensor_scalar(sv[5][:, :], sv[4][:, :], 1.0, None, ALU.add))
                        if middle:
                            stats(b, 1, 3)
                        if back:
                            after(16)
                            nc.vector.reciprocal(sv[5][:, :], sv[5][:, :])
                            router(same(sm[5], sm[4], sv[7]))
                        if middle:
                            dve.wait_ge(ln[1], 2 * j - 1)
                            dve.sem_inc(passed, 1)
                            for r in range(R):
                                last = nc.vector.bn_aggr(mv[1][:, r, :], st[1][:, r, :])
                            last.then_inc(ln[1], 1)
                        if back:
                            after(17)
                            times(sm[3], sm[3], over(sv[5]))
                            nc.vector.tensor_tensor(sv[6][:, :], sv[4][:, :], sv[5][:, :], ALU.mult)\
                              .then_inc(weigh, 1)
                        if middle:
                            dve.wait_ge(ln[1], 2 * j)
                            nc.vector.tensor_scalar(pre[1][:, 0:R], mv[1][:, :, 1], 1e-5, None, ALU.add)\
                              .then_inc(pre_ready[1], 1)
                        if back:
                            dve.wait_ge(weigh, 2 * j - 3)
                            times(sm[5], sm[5], over(sv[6])).then_inc(weigh, 1)
                        if first:
                            stats(j, 0, 2)
                        if back:
                            dve.wait_ge(weigh, 2 * j - 2)
                            nc.vector.tensor_tensor(cw[:, :, :], sm[3][:, :, :], sm[5][:, :, :], ALU.add)\
                              .then_inc(cw_s, 1)
                        if first:
                            stats(j, 0, 3)
                        if back:
                            dve.wait_ge(cw_s, 2 * j - 3)
                            nc.vector.tensor_copy(cws[:, 0, :, :], cw[:, :, :])
                            nc.vector.tensor_copy(cws[:, 2, :, :], cw[:, :, :]).then_inc(cw_s, 1)
                        if first:
                            dve.wait_ge(ln[0], 2 * j + 1)
                            dve.sem_inc(passed, 1)
                            for r in range(R):
                                last = nc.vector.bn_aggr(mv[0][:, r, :], st[0][:, r, :])
                            last.then_inc(ln[0], 1)
                        if back:
                            dve.wait_ge(cw_s, 2 * j - 2)
                            nc.vector.tensor_tensor(cws[:, 1, :, :], cw[:, :, :], cws[:, 0, :, :].bitcast(F32),
                                                    ALU.subtract).then_inc(cw_ready, 1)
                        if first:
                            dve.wait_ge(ln[0], 2 * j + 2)
                            nc.vector.tensor_scalar(pre[0][:, 0:R], mv[0][:, :, 1], 1e-5, None, ALU.add)\
                              .then_inc(pre_ready[0], 1)
                        if middle:
                            dve.wait_ge(root_done[1], j)
                            nc.vector.scalar_tensor_tensor(nb[1][:, :], mv[1][:, :, 0], -1.0, root[1][:, 0:R],
                                                           ALU.mult, ALU.mult).then_inc(nb_ready[1], 1)
                        if back:
                            dve.wait_ge(h_ready, 8 * j - 8)
                            dve.wait_ge(cb_done, 2 * j - 3)
                            nc.vector.tensor_tensor(rc[0][:, :], rp[0][:, :], flat(p_cb), ALU.mult)\
                              .then_inc(rc_ready, 1)
                        if back:
                            dve.wait_ge(h_ready, 8 * j - 7)
                            dve.wait_ge(cb_done, 2 * j - 2)
                            nc.vector.tensor_tensor(rc[1][:, :], rp[1][:, :], flat(p_hl), ALU.mult)\
                              .then_inc(rc_ready, 1)
                        if first:
                            dve.wait_ge(root_done[0], j + 1)
                            nc.vector.tensor_tensor(dm[:, :], root[0][:, R:2 * R], maskt[:, bass.ds(R * j, R)],
                                                    ALU.mult)
                            nc.vector.tensor_tensor(rd[:, :], root[0][:, 0:R], root[0][:, R:2 * R], ALU.mult)\
                              .then_inc(rd_ready, 1)
                            dve.wait_ge(rd_ready, j + 1)
                            nc.vector.scalar_tensor_tensor(nb[0][:, :], mv[0][:, :, 0], -1.0, rd[:, :],
                                                           ALU.mult, ALU.mult).then_inc(nb_ready[0], 1)
                        if back:
                            dve.wait_ge(out_done, j - 1)
                            dve.wait_ge(stored[p], 8 * i - 15)
                            nc.vector.tensor_tensor(outx[p][:, :, :], xtok[:, bass.ds(R * (j - 2), R), :],
                                                    p_out[:, :, :], ALU.add).then_inc(out_ready, 1)

                    turns3(dve, NB, body)




def layout(x, adj, nodemask, L0_gnn_W1, L0_gnn_b1, L0_gnn_W2, L0_gnn_b2, L0_gnn_fusion_w, L0_ffn_Wg, L0_ffn_bg,
           L0_ffn_W1, L0_ffn_b1, L0_ffn_W2, L0_ffn_b2, L1_gnn_W, L1_gnn_b, L1_ffn_sW1, L1_ffn_sb1, L1_ffn_sW2,
           L1_ffn_sb2, L1_ffn_sW3, L1_ffn_sb3, L1_ffn_eW1, L1_ffn_eb1, L1_ffn_eW2, L1_ffn_eb2, L1_ffn_eW3,
           L1_ffn_eb3, L1_ffn_gW, L1_ffn_gb):
    f = np.float32
    every = lambda v, n=P: np.broadcast_to(v.reshape(1, -1), (n, v.size))
    x_grp = np.zeros((NGB, P, R, D), f)
    a_grp = np.zeros((NGB, P, R, P), f)
    w_grp = np.zeros((NGB, P, GWID), f)
    j = 0
    for g, nodes in enumerate(GROUPS):
        n, per = GN[g], GPT[g]
        for b in range(GB[g]):
            for k in range(R):
                first = (b * R + k) * per
                for s, graph in enumerate(range(first, min(first + per, B))):
                    r = slice(s * n, (s + 1) * n)
                    x_grp[j, r, k, :] = x[graph][nodes]
                    a_grp[j, r, k, r] = adj[graph][np.ix_(nodes, nodes)].T
            w_grp[j] = np.concatenate([
                L0_gnn_W1[g], L0_gnn_W2[g].reshape(2, P, D).transpose(1, 0, 2).reshape(P, 2 * D),
                L0_gnn_b1[g].reshape(2, P).T, every(L0_gnn_b2[g])], axis=1)
            j += 1
    w_exp = np.concatenate([
        L0_ffn_W1.transpose(2, 0, 1),
        L0_ffn_W2.reshape(E0, D, HC, P).transpose(3, 0, 2, 1).reshape(P, E0, HC * D),
        L0_ffn_b1.reshape(E0, HC, P).transpose(2, 0, 1),
        L0_ffn_b2.T.reshape(P, E0, 1),
        np.zeros((P, E0, 1), f)], axis=2)
    b_out = np.zeros((KV, R, D), f)
    for k in range(R):
        for c in range(3):
            b_out[(c * R + k) * E1:(c * R + k + 1) * E1, k, :] = L1_ffn_eb3
        b_out[2 * 32, k, :] = b_out[3 * 32, k, :] = L1_ffn_sb3
    cf, ch, sel, selp = consts()
    return {
        "x_tok": x.transpose(1, 0, 2), "x_grp": x_grp, "a_grp": a_grp, "w_grp": w_grp,
        "fus": every(L0_gnn_fusion_w), "wg": L0_ffn_Wg.T, "bg": every(L0_ffn_bg), "w_exp": w_exp,
        "a_t": adj.transpose(2, 0, 1), "w_gcn": L1_gnn_W.T, "b_gcn": every(L1_gnn_b), "mask_t": nodemask.T,
        "w_s": np.concatenate([L1_ffn_sW1, L1_ffn_sW2, L1_ffn_sW3], axis=1),
        "b_s": np.stack([L1_ffn_sb1, L1_ffn_sb2], axis=1),
        "e_w1": L1_ffn_eW1.transpose(1, 0, 2), "e_w2": L1_ffn_eW2.transpose(1, 0, 2),
        "e_w3": L1_ffn_eW3.reshape(2, P, D).transpose(1, 0, 2),
        "b_e": np.concatenate([L1_ffn_eb1.T, L1_ffn_eb2.reshape(2, P).T], axis=1),
        "b_out": b_out, "gw": L1_ffn_gW, "gb": every(L1_ffn_gb),
        "cf_d": cf, "ch_d": ch, "sel_d": sel, "selp_d": selp,
    }


def kernel(**inputs):
    import concourse.bacc as bacc
    from concourse.bass_utils import run_bass_kernel_spmd

    nc = bacc.Bacc("TRN2", target_bir_lowering=False, num_devices=1)
    arrays, args = {}, []
    for name, a in layout(**{k: np.asarray(v) for k, v in inputs.items()}).items():
        arrays["in_" + name] = np.ascontiguousarray(a)
        args.append(nc.dram_tensor("in_" + name, a.shape, mybir.dt.from_np(a.dtype), kind="ExternalInput").ap())
    out = nc.dram_tensor("out_0", (B, N, D), F32, kind="ExternalOutput").ap()
    build(nc, *args, out)
    r = run_bass_kernel_spmd(nc, [arrays], core_ids=[0])
    return r.results[0]["out_0"]
```

```python
import numpy as np
import concourse.bass as bass
from concourse import mybir
from contextlib import ExitStack

F32 = mybir.dt.float32
F16 = mybir.dt.float16
F32R = mybir.dt.float32r
I32 = mybir.dt.int32
ALU = mybir.AluOpType
ACT = mybir.ActivationFunctionType
AX = mybir.AxisListType

P = 128
B = 128
N = P
D = P
R = 4
W = R * P
GROUPS = [list(range(25)), [0, 1, 2, 3, 4, 5, 6, 7, 8], [0, 9, 10, 11, 12, 13, 14], [6, 7, 8, 12, 13, 14],
          [3, 4, 5, 9, 10, 11]]
GN = [len(g) for g in GROUPS]
GPT = [P // n for n in GN]
GB = [-(-(-(-B // k)) // R) for k in GPT]
GOFF = [sum(GN[:g]) for g in range(len(GROUPS))]
GR = sum(GN)
NGB = sum(GB)
GHID = 256
E0 = 8
H0 = 512
HC = H0 // P
TILE = 512
NT = (2 * B * N + E0 * (TILE - 1)) // TILE
NTP = NT + NT % 2
TB = 8
NCOL = NTP * R
WW = HC * P + HC * D
EW = WW + HC + 2
E1 = 4
KV = 97
GWID = GHID + 2 * D + 2 + D
BIG = -3.0e38


def consts():
    i = np.arange(P)
    ident = np.eye(P, dtype=np.float32)
    sel = np.zeros((GR, P), np.float32)
    for g, nodes in enumerate(GROUPS):
        for n, node in enumerate(nodes):
            sel[GOFF[g] + n, node] = 1
    before = (i[:, None] < i[None, :]).astype(np.float32)
    b8 = (np.arange(E0)[None, :] < np.arange(E0)[:, None]).astype(np.float32)
    cf = np.concatenate([
        ident,
        np.broadcast_to(np.arange(E0, 0, -1, dtype=np.float32), (P, E0)),
        np.broadcast_to(b8.reshape(1, -1), (P, E0 * E0)),
        np.broadcast_to(np.arange(P, dtype=np.float32), (P, P)),
        i[:, None].astype(np.float32),
        np.broadcast_to(np.arange(NTP, dtype=np.float32), (P, NTP)),
    ], axis=1)
    ch = np.concatenate([
        before, np.ones((P, P), np.float32),
        np.broadcast_to(np.arange(P, dtype=np.float32), (P, P)),
        np.broadcast_to(np.arange(NCOL, dtype=np.float32), (P, NCOL)),
    ], axis=1).astype(np.float16)
    selp = np.zeros((2 * R * E1, R, 2, P), np.float32)
    for k in range(R):
        for e in range(E1):
            selp[k * E1 + e::R * E1, k, e // 2, (e % 2) * 64:(e % 2) * 64 + 64] = 1
    return cf, ch, sel, selp


CF_ID, CF_PRI, CF_B8, CF_T, CF_P, CF_J = 0, P, P + E0, P + E0 + E0 * E0, 2 * P + E0 + E0 * E0, 2 * P + E0 + E0 * E0 + 1
CF_W = CF_J + NTP
CH_U, CH_1, CH_I, CH_H = 0, P, 2 * P, 3 * P
CH_W = 3 * P + NCOL


def build(nc, x_tok, x_grp, a_grp, w_grp, fus, wg, bg, w_exp, a_t, w_gcn, b_gcn, mask_t,
          w_s, b_s, e_w1, e_w2, e_w3, b_e, b_out, gw, gb, cf_d, ch_d, sel_d, selp_d, out):
    xln_d = nc.dram_tensor("xln_scratch", (B * N, D), F32, kind="Internal").ap()
    y_d = nc.dram_tensor("expert_rows_scratch", (NTP * TILE, D), F32, kind="Internal").ap()
    c_d = [nc.dram_tensor(f"group_rows_scratch{g}", (GB[g] * R * GPT[g] * GN[g], D), F32, kind="Internal").ap()
           for g in range(len(GROUPS))]

    top = ExitStack()
    with top:
        def alloc(ctx, name, shape, dt=F32):
            return ctx.enter_context(nc.sbuf_tensor(name, shape, dt))

        def bank(ctx, name, shape, dt=F32):
            return ctx.enter_context(nc.psum_tensor(name, shape, dt))

        def sem(name):
            return top.enter_context(nc.semaphore(name))

        def pair(name):
            return [sem(name + "_even"), sem(name + "_odd")]

        def turns3(eng, n, body):
            body(0, 0, True, False, False)
            body(0, 1, True, True, False)
            with eng.Fori(2, n - 1, 2) as i:
                body(i, 0, True, True, True)
                body(i, 1, True, True, True)
            body(n, 0, False, True, True)
            body(n, 1, False, False, True)

        def turns4(eng, n, body):
            for j in range(4):
                body(j - j % 2, j % 2, True, j >= 1, j >= 2, j >= 3)
            with eng.Fori(4, n - 1, 2) as i:
                body(i, 0, True, True, True, True)
                body(i, 1, True, True, True, True)
            for j in range(n, n + 3):
                body(j - j % 2, j % 2, False, j < n + 1, j < n + 2, True)

        xtok = alloc(top, "xtok", [P, B, D])
        cf = alloc(top, "cf", [P, CF_W])
        ch = alloc(top, "ch", [P, CH_W], F16)
        mhalf = alloc(top, "mhalf", [P, 2 * R])
        ident = cf[:, CF_ID:CF_ID + P]
        pos_i = alloc(top, "pos_i", [P, 2, B], I32)
        prob = alloc(top, "prob", [P, 2, B])
        ids = alloc(top, "ids", [P, NCOL], I32)
        texp = alloc(top, "texp", [P, NTP], I32)

        x_loaded = sem("x_loaded")
        half_set = sem("half_set")
        passed = sem("passed")

        with ExitStack() as ctx:
            xg = [alloc(ctx, f"xg{p}", [P, R, D]) for p in range(2)]
            ar = [alloc(ctx, f"ar{p}", [P, R, P]) for p in range(2)]
            ag = [alloc(ctx, f"ag{p}", [P, R, P]) for p in range(2)]
            ah = [alloc(ctx, f"ah{p}", [P, R, P]) for p in range(2)]
            wj = [alloc(ctx, f"wj{p}", [P, GWID]) for p in range(2)]
            ones = alloc(ctx, "ones", [P, 1])
            fw = alloc(ctx, "fw", [P, 5])
            fe = alloc(ctx, "fe", [P, 5])
            fm = alloc(ctx, "fm", [P, 4])
            wb = alloc(ctx, "wb", [P, NGB])
            st = [alloc(ctx, f"st{p}", [P, R, 6]) for p in range(2)]
            mv = [alloc(ctx, f"mv{p}", [P, R, 2]) for p in range(2)]
            pre = [alloc(ctx, f"pre{p}", [P, 2 * R]) for p in range(2)]
            root = [alloc(ctx, f"root{p}", [P, 2 * R]) for p in range(2)]
            nz = [alloc(ctx, f"nz{p}", [P, R]) for p in range(2)]
            dinv = [alloc(ctx, f"dinv{p}", [P, R]) for p in range(2)]
            dsc = [alloc(ctx, f"dsc{p}", [P, R]) for p in range(2)]
            wdi = [alloc(ctx, f"wdi{p}", [P, R]) for p in range(2)]
            xs = [alloc(ctx, f"xs{p}", [P, R, D]) for p in range(2)]
            ys = alloc(ctx, "ys", [P, R, D])
            yt = alloc(ctx, "yt", [P, W])
            ht = alloc(ctx, "ht", [P, 2, W])
            zs = alloc(ctx, "zs", [P, R, D])
            b2w = [alloc(ctx, f"b2w{p}", [P, D]) for p in range(2)]
            os_ = [alloc(ctx, f"os{p}", [P, R, D]) for p in range(2)]
            orl = [alloc(ctx, f"orl{p}", [P, R, D]) for p in range(2)]
            p_deg = bank(ctx, "p_deg", [P, 512])
            p_y = bank(ctx, "p_y", [P, R, D])
            p_t = bank(ctx, "p_t", [P, R, D])
            p_h = [bank(ctx, f"p_h{c}", [P, W]) for c in range(2)]
            p_z = bank(ctx, "p_z", [P, R, D])
            p_o = bank(ctx, "p_o", [P, R, D])

            c_loaded = sem("g_consts_loaded")
            loaded = pair("g_loaded")
            set_ = sem("g_set")
            fus_exp = sem("g_fus_exp")
            fus_s = sem("g_fus_steps")
            w_loaded = pair("g_w_loaded")
            ag_ready = sem("g_ag_ready")
            ah_ready = sem("g_ah_ready")
            b2_s = sem("g_b2_s")
            deg_done = sem("g_deg_done")
            stat_s = sem("g_stat_s")
            mv_s = sem("g_mv_s")
            pre_s = sem("g_pre_s")
            pre_ready = sem("g_pre_ready")
            root_done = sem("g_root_done")
            dinv_s = sem("g_dinv_s")
            xs_ready = sem("g_xs_ready")
            y_done = sem("g_y_done")
            ys_ready = sem("g_ys_ready")
            t_done = sem("g_t_done")
            yt_ready = sem("g_yt_ready")
            h_done = sem("g_h_done")
            ht_ready = sem("g_ht_ready")
            z_done = sem("g_z_done")
            zs_ready = sem("g_zs_ready")
            o_done = sem("g_o_done")
            os_ready = sem("g_os_ready")
            orl_ready = sem("g_orl_ready")
            stored = pair("g_stored")

            batch_of = [(g, b) for g in range(len(GROUPS)) for b in range(GB[g])]

            with nc.Block() as block:
                @block.sync
                def _(sp):
                    sp.dma_start(cf[:, :], cf_d).then_inc(c_loaded, 16)
                    sp.dma_start(ch[:, :], ch_d).then_inc(c_loaded, 16)
                    sp.dma_start(fw[:, :], fus).then_inc(c_loaded, 16)

                    def load(j):
                        sp.dma_start(xg[j % 2][:, :, :], x_grp[j]).then_inc(loaded[j % 2], 16)
                        sp.dma_start(ar[j % 2][:, :, :], a_grp[j]).then_inc(loaded[j % 2], 16)

                    def store(j):
                        g, b = batch_of[j]
                        rows = GPT[g] * GN[g]
                        dst = c_d[g][b * R * rows:(b + 1) * R * rows, :].rearrange("(k r) d -> r k d", r=rows)
                        sp.wait_ge(orl_ready, j + 1)
                        sp.dma_start(dst, orl[j % 2][0:rows, :, :]).then_inc(stored[j % 2], 16)

                    load(0)
                    load(1)
                    for j in range(NGB + 3):
                        if j >= 3:
                            store(j - 3)
                        if j < NGB:
                            if j >= 2:
                                sp.wait_ge(z_done, j - 1)
                            sp.dma_start(wj[j % 2][:, :], w_grp[j]).then_inc(w_loaded[j % 2], 16)
                        if j % 2 == 0 and j < NGB:
                            n = B * j // NGB, B * (j + 2) // NGB
                            sp.dma_start(xtok[:, n[0]:n[1], :], x_tok[:, n[0]:n[1], :]).then_inc(x_loaded, 16)
                        if j + 2 < NGB:
                            sp.wait_ge(xs_ready, j + 1)
                            sp.wait_ge(ah_ready, j + 1)
                            load(j + 2)
                    sp.wait_ge(stored[0], 16 * (NGB // 2) + 1)
                    sp.wait_ge(stored[1], 16 * (NGB // 2) + 1)
                    sp.wait_ge(x_loaded, 16 * (NGB // 2))

                @block.gpsimd
                def _(pool):
                    nc.gpsimd.memset(mhalf[:, :], -0.5).then_inc(half_set, 1)
                    pool.wait_ge(half_set, 1)
                    pool.wait_ge(c_loaded, 48)
                    plus = ident.unsqueeze(1).to_broadcast([P, R, P])

                    def body(i, p, first, middle, back):
                        j = i + p
                        if first:
                            pool.wait_ge(loaded[p], 16 * i + 32)
                            if middle:
                                pool.wait_ge(y_done, j)
                            nc.gpsimd.tensor_tensor(ag[p][:, :, :], ar[p][:, :, :], plus, ALU.add)\
                              .then_inc(ag_ready, 1)
                            pool.wait_ge(pre_ready, j + 1)
                            nc.gpsimd.tensor_tensor(root[p][:, :], pre[p][:, :], mhalf[:, :], ALU.pow)\
                              .then_inc(root_done, 1)
                            if back:
                                pool.wait_ge(o_done, j - 1)
                            nc.gpsimd.tensor_tensor(ah[p][:, :, :], ar[p][:, :, :], plus, ALU.add)\
                              .then_inc(ah_ready, 1)

                    turns3(pool, NGB, body)

                @block.scalar
                def _(act):
                    act.sem_inc(stored[0], 1)
                    act.sem_inc(stored[1], 1)
                    act.wait_ge(fus_s, 2)
                    nc.scalar.activation(fe[:, :], fe[:, :], ACT.Exp).then_inc(fus_exp, 1)

                    def body(i, p, first, middle, back):
                        j = i + p
                        q = 1 - p
                        if middle:
                            act.wait_ge(t_done, j)
                            nc.scalar.activation(yt[:, :], p_t[:, :, :].rearrange("p r d -> p (r d)"), ACT.Copy)\
                              .then_inc(yt_ready, 1)
                            for c in range(2):
                                act.wait_ge(h_done, 2 * j + c - 1)
                                nc.scalar.activation(ht[:, c, :], p_h[c][:, :], ACT.Relu,
                                                     bias=wj[q][:, GHID + 2 * D + c:GHID + 2 * D + c + 1])\
                                  .then_inc(ht_ready, 1)
                        if back:
                            act.wait_ge(os_ready, j)
                            act.wait_ge(stored[p], 8 * i - 15)
                            nc.scalar.activation(orl[p][:, :, :], os_[p][:, :, :], ACT.Relu).then_inc(orl_ready, 1)

                    turns3(act, NGB, body)

                @block.tensor
                def _(pe):
                    def body(i, p, first, middle, back):
                        j = i + p
                        q = 1 - p
                        if middle:
                            pe.wait_ge(xs_ready, j)
                            for k in range(R):
                                last = nc.tensor.matmul(p_y[:, k, :], ag[q][:, k, :], xs[q][:, k, :],
                                                        start=True, stop=True)
                            last.then_inc(y_done, 1)
                        if back:
                            pe.wait_ge(ht_ready, 2 * j - 2)
                            for k in range(R):
                                for c in range(2):
                                    last = nc.tensor.matmul(p_z[:, k, :], ht[:, c, k * P:(k + 1) * P],
                                                            wj[p][:, GHID + c * D:GHID + (c + 1) * D],
                                                            start=(c == 0), stop=(c == 1))
                            last.then_inc(z_done, 1)
                        if first:
                            pe.wait_ge(ag_ready, j + 1)
                            for k in range(R):
                                last = nc.tensor.matmul(p_deg[:, k:k + 1], ag[p][:, k, :], ones[:, :],
                                                        start=True, stop=True)
                            last.then_inc(deg_done, 1)
                        if middle:
                            pe.wait_ge(ys_ready, j)
                            for k in range(R):
                                last = nc.tensor.transpose(p_t[:, k, :], ys[:, k, :], ident)
                            last.then_inc(t_done, 1)
                        if back:
                            pe.wait_ge(zs_ready, j - 1)
                            pe.wait_ge(ah_ready, j - 1)
                            pe.wait_ge(os_ready, j - 1)
                            for k in range(R):
                                last = nc.tensor.matmul(p_o[:, k, :], ah[p][:, k, :], zs[:, k, :],
                                                        start=True, stop=True)
                            last.then_inc(o_done, 1)
                        if middle:
                            pe.wait_ge(w_loaded[q], 8 * i + 16 if p else 8 * i)
                            pe.wait_ge(yt_ready, j)
                            for c in range(2):
                                nc.tensor.matmul(p_h[c][:, :], wj[q][:, c * P:(c + 1) * P], yt[:, :],
                                                 start=True, stop=True).then_inc(h_done, 1)

                    pe.wait_ge(set_, 1)
                    pe.wait_ge(c_loaded, 48)
                    turns3(pe, NGB, body)

                @block.vector
                def _(dve):
                    nc.vector.memset(ones[:, :], 1.0).then_inc(set_, 1)
                    dve.wait_ge(c_loaded, 48)
                    nc.vector.reduce_max(fm[:, 0:1], fw[:, :], AX.X).then_inc(fus_s, 1)
                    dve.wait_ge(fus_s, 1)
                    nc.vector.tensor_scalar(fe[:, :], fw[:, :], fm[:, 0:1], None, ALU.subtract).then_inc(fus_s, 1)
                    dve.wait_ge(fus_exp, 1)
                    nc.vector.reduce_sum(fm[:, 1:2], fe[:, :], AX.X).then_inc(fus_s, 1)
                    dve.wait_ge(fus_s, 3)
                    nc.vector.reciprocal(fm[:, 2:3], fm[:, 1:2]).then_inc(fus_s, 1)
                    dve.wait_ge(fus_s, 4)
                    nc.vector.tensor_scalar(fw[:, :], fe[:, :], fm[:, 2:3], None, ALU.mult).then_inc(fus_s, 1)
                    dve.wait_ge(fus_s, 5)
                    for g in range(len(GROUPS)):
                        a = sum(GB[:g])
                        last = nc.vector.tensor_copy(wb[:, a:a + GB[g]], fw[:, g:g + 1].to_broadcast([P, GB[g]]))
                    last.then_inc(fus_s, 1)
                    dve.wait_ge(fus_s, 6)

                    dve.sem_inc(os_ready, 1)

                    def body(i, p, first, middle, back):
                        j = i + p
                        q = 1 - p
                        if first:
                            dve.wait_ge(loaded[p], 16 * i + 32)
                            for k in range(R):
                                last = nc.vector.bn_stats(st[p][:, k, :], xg[p][:, k, :])
                            last.then_inc(stat_s, 1)
                        if middle:
                            dve.wait_ge(y_done, j)
                            nc.vector.tensor_tensor(ys[:, :, :], p_y[:, :, :],
                                                    dinv[q][:, :].unsqueeze(2).to_broadcast([P, R, D]), ALU.mult)\
                              .then_inc(ys_ready, 1)
                        if first:
                            dve.wait_ge(stat_s, j + 1)
                            dve.sem_inc(passed, 1)
                            for k in range(R):
                                last = nc.vector.bn_aggr(mv[p][:, k, :], st[p][:, k, :])
                            last.then_inc(mv_s, 1)
                            dve.wait_ge(mv_s, j + 1)
                            nc.vector.tensor_scalar(pre[p][:, 0:R], mv[p][:, :, 1], 1e-5, None, ALU.add)
                        if back:
                            dve.wait_ge(z_done, j - 1)
                            nc.vector.tensor_tensor(zs[:, :, :], p_z[:, :, :],
                                                    dinv[p][:, :].unsqueeze(2).to_broadcast([P, R, D]), ALU.mult)\
                              .then_inc(zs_ready, 1)
                        if first:
                            dve.wait_ge(deg_done, j + 1)
                            nc.vector.tensor_scalar(nz[p][:, :], p_deg[:, 0:R], 0.0, None, ALU.is_equal)\
                              .then_inc(pre_s, 1)
                            dve.wait_ge(pre_s, j + 1)
                            nc.vector.tensor_tensor(pre[p][:, R:2 * R], p_deg[:, 0:R], nz[p][:, :], ALU.add)\
                              .then_inc(pre_ready, 1)
                            nc.vector.tensor_scalar(nz[p][:, :], nz[p][:, :], -1.0, 1.0, ALU.mult, ALU.add)\
                              .then_inc(dinv_s, 1)
                        if middle:
                            dve.wait_ge(w_loaded[q], 8 * i + 16 if p else 8 * i)
                            if back:
                                dve.wait_ge(os_ready, j - 1)
                            nc.vector.tensor_scalar(wdi[q][:, :], dinv[q][:, :], wb[:, bass.ds(j - 1, 1)], None,
                                                    ALU.mult)
                            nc.vector.tensor_scalar(b2w[q][:, :], wj[q][:, GWID - D:GWID], wb[:, bass.ds(j - 1, 1)],
                                                    None, ALU.mult).then_inc(b2_s, 1)
                        if first:
                            dve.wait_ge(dinv_s, 3 * j + 1)
                            dve.wait_ge(root_done, j + 1)
                            nc.vector.tensor_tensor(dinv[p][:, :], nz[p][:, :], root[p][:, R:2 * R], ALU.mult)\
                              .then_inc(dinv_s, 1)
                            dve.wait_ge(dinv_s, 3 * j + 2)
                            nc.vector.tensor_tensor(dsc[p][:, :], dinv[p][:, :], root[p][:, 0:R], ALU.mult)\
                              .then_inc(dinv_s, 1)
                            dve.wait_ge(dinv_s, 3 * j + 3)
                            for k in range(R):
                                last = nc.vector.tensor_scalar(xs[p][:, k, :], xg[p][:, k, :], mv[p][:, k, 0:1],
                                                               dsc[p][:, k:k + 1], ALU.subtract, ALU.mult)
                            last.then_inc(xs_ready, 1)
                        if back:
                            dve.wait_ge(o_done, j - 1)
                            dve.wait_ge(b2_s, j - 1)
                            for k in range(R):
                                last = nc.vector.scalar_tensor_tensor(os_[p][:, k, :], p_o[:, k, :],
                                                                      wdi[p][:, k:k + 1], b2w[p][:, :],
                                                                      ALU.mult, ALU.add)
                            last.then_inc(os_ready, 1)

                    turns3(dve, NGB, body)

        wall = alloc(top, "wall", [P, E0, EW])
        w_loaded = sem("w_loaded")
        lgp = top.enter_context(ExitStack())
        lg = alloc(lgp, "lg", [P, B, E0])
        with ExitStack() as ctx:
            RG = 2 * R
            NB = B // RG
            ct = [alloc(ctx, f"ct{p}", [GR, RG, D]) for p in range(2)]
            sel = alloc(ctx, "sel", [GR, P])
            wgt = alloc(ctx, "wgt", [P, E0])
            bgs = alloc(ctx, "bgs", [P, E0])
            st = alloc(ctx, "gst", [P, RG, 6])
            mv = [alloc(ctx, f"gmv{p}", [P, RG, 2]) for p in range(2)]
            pre = [alloc(ctx, f"gpre{p}", [P, RG]) for p in range(2)]
            root = [alloc(ctx, f"groot{p}", [P, RG]) for p in range(2)]
            nb = [alloc(ctx, f"gnb{p}", [P, RG]) for p in range(2)]
            xl = [alloc(ctx, f"xl{p}", [P, RG, D]) for p in range(2)]
            xt = alloc(ctx, "gxt", [P, 2, W])
            p_sel = [bank(ctx, f"p_sel{p}", [P, RG, D]) for p in range(2)]
            p_t = [bank(ctx, f"p_gt{h}", [P, R, D]) for h in range(2)]
            p_lg = bank(ctx, "p_lg", [P, 512])
            c_loaded = sem("r_consts_loaded")
            loaded = pair("r_loaded")
            sel_done = sem("r_sel_done")
            x1_ready = sem("r_x1_ready")
            stat_s = sem("r_stat_s")
            mv_s = sem("r_mv_s")
            pre_ready = sem("r_pre_ready")
            root_done = sem("r_root_done")
            nb_ready = sem("r_nb_ready")
            xl_ready = sem("r_xl_ready")
            t_done = sem("r_t_done")
            xt_ready = sem("r_xt_ready")
            lg_done = sem("r_lg_done")
            lg_ready = sem("r_lg_ready")
            stored = pair("r_stored")

            with nc.Block() as block:
                @block.sync
                def _(sp):
                    def load(j, p):
                        for g in range(len(GROUPS)):
                            src = c_d[g][0:B * GN[g], :].rearrange("(b n) d -> n b d", n=GN[g])
                            sp.dma_start(ct[p][GOFF[g]:GOFF[g] + GN[g], :, :], src[:, bass.ds(RG * j, RG), :])\
                              .then_inc(loaded[p], 16)

                    def store(j, p):
                        sp.wait_ge(xl_ready, 2 * j + 2)
                        sp.dma_start(xln_d.rearrange("(b n) d -> n b d", n=N)[:, bass.ds(RG * j, RG), :],
                                     xl[p][:, :, :]).then_inc(stored[p], 16)

                    load(0, 0)
                    sp.dma_start(sel[:, :], sel_d).then_inc(c_loaded, 16)
                    sp.dma_start(wgt[:, :], wg).then_inc(c_loaded, 16)
                    sp.dma_start(bgs[:, :], bg).then_inc(c_loaded, 16)
                    load(1, 1)
                    with sp.Fori(0, NB - 3, 2) as i:
                        for p in range(2):
                            sp.wait_ge(sel_done, i + p + 1)
                            load(i + p + 2, p)
                            store(i + p, p)
                    store(NB - 2, 0)
                    store(NB - 1, 1)
                    for p in range(2):
                        sp.wait_ge(stored[p], 8 * NB + 1)

                @block.gpsimd
                def _(pool):
                    def roots(j, p):
                        pool.wait_ge(pre_ready, j + 1)
                        nc.gpsimd.tensor_tensor(root[p][:, :], pre[p][:, :], mhalf[:, 0:RG], ALU.pow)\
                          .then_inc(root_done, 1)

                    roots(0, 0)
                    roots(1, 1)
                    with pool.Fori(2, NB - 1, 2) as i:
                        for p in range(2):
                            pool.wait_ge(xl_ready, 2 * (i + p) - 2)
                            roots(i + p, p)

                @block.scalar
                def _(act):
                    def body(i, p, first, second, third, last_):
                        j = i + p
                        if third:
                            act.wait_ge(stored[p], 8 * i - 15)
                            act.wait_ge(nb_ready, j - 1)
                            act.sem_inc(passed, 1)
                            for k in range(RG):
                                ins = nc.scalar.activation(
                                    xl[p][:, k, :],
                                    xtok[:, bass.ds(RG * (j - 2) + k, 1), :].rearrange("p a d -> p (a d)"),
                                    ACT.Identity, scale=root[p][:, k:k + 1], bias=nb[p][:, k:k + 1])
                                if k % R == R - 1:
                                    ins.then_inc(xl_ready, 1)
                            for h in range(2):
                                act.wait_ge(t_done, 2 * j - 3 + h)
                                nc.scalar.activation(xt[:, h, :], p_t[h][:, :, :].rearrange("p r d -> p (r d)"),
                                                     ACT.Copy).then_inc(xt_ready, 1)

                    turns4(act, NB, body)

                @block.tensor
                def _(pe):
                    def body(i, p, first, second, third, last_):
                        j = i + p
                        if first:
                            pe.wait_ge(loaded[p], 40 * i + 80)
                            if third:
                                pe.wait_ge(x1_ready, j - 1)
                            for h in range(2):
                                last = nc.tensor.matmul(
                                    p_sel[p][:, h * R:(h + 1) * R, :].rearrange("p r d -> p (r d)"), sel[:, :],
                                    ct[p][:, h * R:(h + 1) * R, :].rearrange("p r d -> p (r d)"),
                                    start=True, stop=True)
                            last.then_inc(sel_done, 1)
                        if last_:
                            pe.wait_ge(xt_ready, 2 * j - 4)
                            pe.wait_ge(lg_ready, j - 2)
                            for k in range(RG):
                                last = nc.tensor.matmul(p_lg[:, k * E0:(k + 1) * E0],
                                                        xt[:, k // R, (k % R) * P:(k % R + 1) * P], wgt[:, :],
                                                        start=True, stop=True)
                            last.then_inc(lg_done, 1)
                        if third:
                            for h in range(2):
                                pe.wait_ge(xl_ready, 2 * j - 3 + h)
                                for k in range(R):
                                    last = nc.tensor.transpose(p_t[h][:, k, :], xl[p][:, h * R + k, :], ident)
                                last.then_inc(t_done, 1)

                    pe.wait_ge(c_loaded, 48)
                    turns4(pe, NB, body)

                @block.vector
                def _(dve):
                    dve.sem_inc(stored[0], 1)
                    dve.sem_inc(stored[1], 1)
                    dve.sem_inc(lg_ready, 1)
                    dve.wait_ge(c_loaded, 48)

                    def body(i, p, first, second, third, last_):
                        j = i + p
                        q = 1 - p
                        b = j - 1
                        if third:
                            dve.wait_ge(root_done, j - 1)
                            nc.vector.scalar_tensor_tensor(nb[p][:, :], mv[p][:, :, 0], -1.0, root[p][:, :],
                                                           ALU.mult, ALU.mult).then_inc(nb_ready, 1)
                        if second:
                            rows = xtok[:, bass.ds(RG * b, RG), :]
                            dve.wait_ge(sel_done, j)
                            nc.vector.tensor_tensor(rows, rows, p_sel[q][:, :, :], ALU.add).then_inc(x1_ready, 1)
                            dve.wait_ge(x1_ready, j)
                            dve.sem_inc(passed, 1)
                            for k in range(RG):
                                last = nc.vector.bn_stats(st[:, k, :], xtok[:, bass.ds(RG * b + k, 1), :])
                            last.then_inc(stat_s, 1)
                            dve.wait_ge(stat_s, j)
                            dve.sem_inc(passed, 1)
                            for k in range(RG):
                                last = nc.vector.bn_aggr(mv[q][:, k, :], st[:, k, :])
                            last.then_inc(mv_s, 1)
                            dve.wait_ge(mv_s, j)
                            nc.vector.tensor_scalar(pre[q][:, :], mv[q][:, :, 1], 1e-5, None, ALU.add)\
                              .then_inc(pre_ready, 1)
                        if last_:
                            dve.wait_ge(lg_done, j - 2)
                            nc.vector.tensor_tensor(lg[:, bass.ds(RG * (j - 3), RG), :],
                                                    p_lg[:, 0:RG * E0].rearrange("p (b e) -> p b e", e=E0),
                                                    bgs[:, :].unsqueeze(1).to_broadcast([P, RG, E0]), ALU.add)\
                              .then_inc(lg_ready, 1)

                    turns4(dve, NB, body)

        with ExitStack() as ctx:
            wide = alloc(ctx, "wide", [P, B, E0])
            mask = [alloc(ctx, f"mask{k}", [P, B, E0]) for k in range(2)]
            top_s = [alloc(ctx, f"top_s{k}", [P, B]) for k in range(2)]
            pm = alloc(ctx, "pm", [P, B])
            dif = alloc(ctx, "dif", [P, B])
            mb = alloc(ctx, "mb", [P, B, E0], F16)
            tot = alloc(ctx, "tot", [P, E0], F16)
            tu = alloc(ctx, "tu", [P, E0, B], F16)
            cnt_i = alloc(ctx, "cnt_i", [P, E0], I32)
            ntl = alloc(ctx, "ntl", [P, E0])
            b8 = alloc(ctx, "b8", [P, E0, E0])
            base = alloc(ctx, "base", [P, E0])
            end = alloc(ctx, "end", [P, E0])
            base_r = alloc(ctx, "base_r", [P, E0])
            posf = alloc(ctx, "posf", [P, E0, B])
            pos_f = alloc(ctx, "pos_f", [P, 2, B])
            lo_i = alloc(ctx, "lo_i", [P, 2, B], I32)
            hi_i = alloc(ctx, "hi_i", [P, 2, B], I32)
            tge = alloc(ctx, "tge", [P, NTP, E0])
            tex = alloc(ctx, "tex", [P, NTP])
            lo_h = alloc(ctx, "lo_h", [P, 2, B], F16)
            hi_h = alloc(ctx, "hi_h", [P, 2, B], F16)
            iota_l = alloc(ctx, "iota_l", [P, P, TB], F16)
            iota_c = alloc(ctx, "iota_c", [P, NCOL, TB], F16)
            hot = [alloc(ctx, f"hot{k}", [P, P, TB], F16) for k in range(2)]
            lp = [[alloc(ctx, f"lp{p}{k}", [P, P, TB], F16) for k in range(2)] for p in range(2)]
            lt = [[alloc(ctx, f"lt{p}{k}", [P, P, TB], F16) for k in range(2)] for p in range(2)]
            hh = [[alloc(ctx, f"hh{p}{k}", [P, NCOL, TB], F16) for k in range(2)] for p in range(2)]
            zero = alloc(ctx, "zero", [P, NCOL], F16)
            idf = alloc(ctx, "idf", [P, NCOL])
            p_rank = bank(ctx, "p_rank", [P, E0, B])
            p_tot = bank(ctx, "p_tot", [P, 512])
            p_cnt = bank(ctx, "p_cnt", [P, 512])
            p_ip = bank(ctx, "p_ip", [P, 512])
            p_it = bank(ctx, "p_it", [P, 512])

            s = sem("s_steps")
            dif_ready = sem("s_dif_ready")
            exp_done = sem("s_exp_done")
            mb_ready = sem("s_mb_ready")
            tot_done = sem("s_tot_done")
            tot_ready = sem("s_tot_ready")
            tu_ready = sem("s_tu_ready")
            cnt_done = sem("s_cnt_done")
            rank_done = sem("s_rank_done")
            zero_set = sem("s_zero_set")
            iota_set = sem("s_iota_set")
            hot_s = sem("s_hot_s")
            lp_ready = sem("s_lp_ready")
            hot_ready = sem("s_hot_ready")
            hot_used = sem("s_hot_used")
            ids_done = sem("s_ids_done")

            with nc.Block() as block:
                @block.gpsimd
                def _(pool):
                    nc.gpsimd.memset(zero[:, :], 0.0).then_inc(zero_set, 1)

                @block.sync
                def _(sp):
                    sp.dma_start(wall[:, :, :], w_exp).then_inc(w_loaded, 16)
                    sp.wait_ge(w_loaded, 16)

                @block.scalar
                def _(act):
                    iota = ch[:, CH_I:CH_I + P].unsqueeze(2).to_broadcast([P, P, TB])
                    nc.scalar.activation(iota_l[:, :, :], iota, ACT.Copy).then_inc(iota_set, 1)
                    iota = ch[:, CH_H:CH_H + NCOL].unsqueeze(2).to_broadcast([P, NCOL, TB])
                    nc.scalar.activation(iota_c[:, :, :], iota, ACT.Copy).then_inc(iota_set, 1)
                    act.wait_ge(dif_ready, 1)
                    nc.scalar.activation(dif[:, :], dif[:, :], ACT.Exp).then_inc(exp_done, 1)

                    def times_node(m, p):
                        act.wait_ge(hot_s, m + 1)
                        for k in range(2):
                            last = nc.scalar.activation(lp[p][k][:, :, :], hot[k][:, :, :], ACT.Copy,
                                                        scale=cf[:, CF_P:CF_P + 1])
                        last.then_inc(lp_ready, 1)

                    times_node(0, 0)
                    times_node(1, 1)
                    with act.Fori(2, B // TB - 1, 2) as i:
                        for p in range(2):
                            act.wait_ge(hot_used, i + p - 1)
                            times_node(i + p, p)

                @block.tensor
                def _(pe):
                    ones16 = ch[:, CH_1:CH_1 + P]
                    pe.wait_ge(mb_ready, 1)
                    for e in range(E0):
                        last = nc.tensor.matmul(p_tot[:, e:e + 1], mb[:, :, e], ones16[:, 0:1], start=True, stop=True)
                    last.then_inc(tot_done, 1)
                    pe.wait_ge(tot_ready, 1)
                    nc.tensor.matmul(p_cnt[:, 0:E0], ones16, tot[:, :], start=True, stop=True).then_inc(cnt_done, 1)
                    pe.wait_ge(tu_ready, 1)
                    for h in range(2):
                        e = slice(h * E0 // 2, (h + 1) * E0 // 2)
                        nc.tensor.matmul(p_rank[:, e, :], ch[:, CH_U:CH_U + P],
                                         mb[:, :, e].rearrange("p b e -> p e b"), start=True, stop=False)
                        nc.tensor.matmul(p_rank[:, e, :], ones16, tu[:, e, :], start=False, stop=True)\
                          .then_inc(rank_done, 1)
                    pe.wait_ge(zero_set, 1)
                    for acc in (p_ip, p_it):
                        nc.tensor.matmul(acc[:, 0:NCOL], ch[:, CH_U:CH_U + P], zero[:, :], start=True, stop=False)
                    with pe.Fori(0, B // TB - 1, 2) as i:
                        for p in range(2):
                            pe.wait_ge(hot_ready, i + p + 1)
                            pe.wait_ge(lp_ready, i + p + 1)
                            for t in range(TB):
                                for k in range(2):
                                    nc.tensor.matmul(p_ip[:, 0:NCOL], lp[p][k][:, :, t], hh[p][k][:, :, t],
                                                     start=False, stop=False)
                                    last = nc.tensor.matmul(p_it[:, 0:NCOL], lt[p][k][:, :, t], hh[p][k][:, :, t],
                                                            start=False, stop=False)
                            last.then_inc(hot_used, 1)
                    for acc in (p_ip, p_it):
                        nc.tensor.matmul(acc[:, 0:NCOL], ch[:, CH_U:CH_U + P], zero[:, :], start=False, stop=True)\
                          .then_inc(ids_done, 1)

                @block.vector
                def _(dve):
                    count = [0]

                    def step(ins):
                        count[0] += 1
                        ins.then_inc(s, 1)
                        dve.wait_ge(s, count[0])

                    pri = cf[:, CF_PRI:CF_PRI + E0].unsqueeze(1).to_broadcast([P, B, E0])
                    flat = lambda t: t[:, :, :].rearrange("p b e -> p (b e)")
                    src = lg
                    for k in range(2):
                        step(nc.vector.tensor_reduce(top_s[k][:, :], src[:, :, :], AX.X, ALU.max))
                        step(nc.vector.tensor_tensor(wide[:, :, :], src[:, :, :],
                                                     top_s[k][:, :].unsqueeze(2).to_broadcast([P, B, E0]),
                                                     ALU.is_equal))
                        step(nc.vector.tensor_tensor(wide[:, :, :], wide[:, :, :], pri, ALU.mult))
                        step(nc.vector.tensor_reduce(pm[:, :], wide[:, :, :], AX.X, ALU.max))
                        step(nc.vector.tensor_tensor(mask[k][:, :, :], wide[:, :, :],
                                                     pm[:, :].unsqueeze(2).to_broadcast([P, B, E0]), ALU.is_equal))
                        if k == 0:
                            step(nc.vector.scalar_tensor_tensor(flat(lg), flat(mask[0]), BIG, flat(lg),
                                                                ALU.mult, ALU.add))
                    nc.vector.tensor_tensor(mb[:, :, :], mask[0][:, :, :], mask[1][:, :, :], ALU.add)\
                      .then_inc(mb_ready, 1)
                    nc.vector.tensor_tensor(dif[:, :], top_s[1][:, :], top_s[0][:, :], ALU.subtract)\
                      .then_inc(dif_ready, 1)
                    dve.wait_ge(tot_done, 1)
                    nc.vector.tensor_copy(tot[:, :], p_tot[:, 0:E0]).then_inc(tot_ready, 1)
                    nc.vector.tensor_tensor(tu[:, :, :], p_tot[:, 0:E0].unsqueeze(2).to_broadcast([P, E0, B]),
                                            ch[:, CH_U:CH_U + P].unsqueeze(1).to_broadcast([P, E0, B]), ALU.mult)\
                      .then_inc(tu_ready, 1)
                    dve.wait_ge(cnt_done, 1)
                    step(nc.vector.tensor_scalar(cnt_i[:, :], p_cnt[:, 0:E0], float(TILE - 1), None, ALU.add))
                    step(nc.vector.tensor_single_scalar(cnt_i[:, :], cnt_i[:, :], TILE.bit_length() - 1,
                                                        ALU.logical_shift_right))
                    step(nc.vector.tensor_copy(ntl[:, :], cnt_i[:, :]))
                    step(nc.vector.tensor_tensor(b8[:, :, :], ntl[:, :].unsqueeze(1).to_broadcast([P, E0, E0]),
                                                 cf[:, CF_B8:CF_B8 + E0 * E0].rearrange("p (a b) -> p a b", b=E0),
                                                 ALU.mult))
                    step(nc.vector.tensor_reduce(base[:, :], b8[:, :, :], AX.X, ALU.add))
                    nc.vector.tensor_tensor(end[:, :], base[:, :], ntl[:, :], ALU.add)
                    step(nc.vector.tensor_scalar(base_r[:, :], base[:, :], float(TILE), None, ALU.mult))
                    step(nc.vector.tensor_tensor(tge[:, :, :],
                                                 cf[:, CF_J:CF_J + NTP].unsqueeze(2).to_broadcast([P, NTP, E0]),
                                                 end[:, :].unsqueeze(1).to_broadcast([P, NTP, E0]), ALU.is_ge))
                    step(nc.vector.tensor_reduce(tex[:, :], tge[:, :, :], AX.X, ALU.add))
                    step(nc.vector.tensor_scalar(texp[:, :], tex[:, :], float(E0 - 1), None, ALU.min))
                    for hb in range(2):
                        dve.wait_ge(rank_done, hb + 1)
                        e = slice(hb * E0 // 2, (hb + 1) * E0 // 2)
                        step(nc.vector.tensor_tensor(posf[:, e, :], p_rank[:, e, :],
                                                     base_r[:, e].unsqueeze(2).to_broadcast([P, E0 // 2, B]), ALU.add))
                    for k in range(2):
                        step(nc.vector.tensor_tensor(wide[:, :, :], mask[k][:, :, :],
                                                     posf[:, :, :].rearrange("p e b -> p b e"), ALU.mult))
                        step(nc.vector.tensor_reduce(pos_f[:, k, :], wide[:, :, :], AX.X, ALU.add))
                    step(nc.vector.tensor_copy(pos_i[:, :, :], pos_f[:, :, :]))
                    nc.vector.tensor_single_scalar(lo_i[:, :, :], pos_i[:, :, :], P - 1, ALU.bitwise_and)
                    step(nc.vector.tensor_single_scalar(hi_i[:, :, :], pos_i[:, :, :], P.bit_length() - 1,
                                                        ALU.logical_shift_right))
                    nc.vector.tensor_copy(lo_h[:, :, :], lo_i[:, :, :])
                    step(nc.vector.tensor_copy(hi_h[:, :, :], hi_i[:, :, :]))
                    dve.wait_ge(exp_done, 1)
                    step(nc.vector.tensor_scalar(pm[:, :], dif[:, :], 1.0, None, ALU.add))
                    step(nc.vector.reciprocal(prob[:, 0, :], pm[:, :]))
                    step(nc.vector.tensor_tensor(prob[:, 1, :], dif[:, :], prob[:, 0, :], ALU.mult))

                    def one_hots(m, p):
                        tiles = bass.ds(TB * m, TB)
                        def column(k):
                            nc.vector.tensor_tensor(hh[p][k][:, :, :], iota_c[:, :, :],
                                                    hi_h[:, k, tiles].unsqueeze(1).to_broadcast([P, NCOL, TB]),
                                                    ALU.is_equal)

                        column(0)
                        if not (isinstance(m, int) and m == 0):
                            dve.wait_ge(hot_ready, m)
                            dve.wait_ge(lp_ready, m)
                        for k in range(2):
                            last = nc.vector.tensor_tensor(hot[k][:, :, :], iota_l[:, :, :],
                                                           lo_h[:, k, tiles].unsqueeze(1).to_broadcast([P, P, TB]),
                                                           ALU.is_equal)
                        last.then_inc(hot_s, 1)
                        column(1)
                        dve.wait_ge(hot_s, m + 1)
                        graph = ch[:, bass.ds(TB * m + CH_I, TB)].unsqueeze(1).to_broadcast([P, P, TB])
                        for k in range(2):
                            last = nc.vector.tensor_tensor(lt[p][k][:, :, :], hot[k][:, :, :], graph, ALU.mult)
                        last.then_inc(hot_ready, 1)

                    dve.wait_ge(iota_set, 2)
                    one_hots(0, 0)
                    one_hots(1, 1)
                    with dve.Fori(2, B // TB - 1, 2) as i:
                        for p in range(2):
                            dve.wait_ge(hot_used, i + p - 1)
                            one_hots(i + p, p)
                    dve.wait_ge(ids_done, 2)
                    step(nc.vector.tensor_scalar(idf[:, :], p_it[:, 0:NCOL], float(P), None, ALU.mult))
                    step(nc.vector.tensor_tensor(idf[:, :], idf[:, :], p_ip[:, 0:NCOL], ALU.add))
                    step(nc.vector.tensor_copy(ids[:, :], idf[:, :]))
        lgp.close()

        wgcn = alloc(top, "wgcn", [P, D])
        bgcn = alloc(top, "bgcn", [P, D])
        maskt = alloc(top, "maskt", [P, B])
        ws = alloc(top, "ws", [P, 3 * P])
        bs = alloc(top, "bs", [P, 2])
        w1 = alloc(top, "w1", [P, E1, P])
        w2 = alloc(top, "w2", [P, E1, P // 2])
        w3 = alloc(top, "w3", [P, 2, D])
        be = alloc(top, "be", [P, E1 + 2])
        vraw = alloc(top, "vraw", [KV, R, D])
        gws = alloc(top, "gws", [P, E1])
        gbs = alloc(top, "gbs", [P, E1])
        selraw = alloc(top, "selraw", [2 * R * E1, R, 2, P])
        c_loaded = sem("l_consts_loaded")
        NC = 13

        with ExitStack() as ctx:
            wh = [alloc(ctx, f"wh{p}", [P, WW], F32R) for p in range(2)]
            wl = [alloc(ctx, f"wl{p}", [P, WW], F32R) for p in range(2)]
            bc = [alloc(ctx, f"bc{p}", [P, EW - WW]) for p in range(2)]
            xg = [alloc(ctx, f"exg{p}", [P, R, D]) for p in range(2)]
            xh = [alloc(ctx, f"exh{p}", [P, W], F32R) for p in range(2)]
            xl = [alloc(ctx, f"exl{p}", [P, W], F32R) for p in range(2)]
            hr = [alloc(ctx, f"ehr{k}", [P, W]) for k in range(2)]
            hh = alloc(ctx, "ehh", [P, HC, W], F32R)
            hl = alloc(ctx, "ehl", [P, HC, W], F32R)
            yt = [alloc(ctx, f"eyt{p}", [P, W]) for p in range(2)]
            yo = [alloc(ctx, f"eyo{p}", [P, R, D]) for p in range(2)]
            idx = [alloc(ctx, f"eidx{p}", [P, R], I32) for p in range(2)]
            p_x = bank(ctx, "p_ex", [P, R, D])
            p_h = [bank(ctx, f"p_eh{c}", [P, W]) for c in range(HC)]
            p_y = [bank(ctx, f"p_ey{p}", [P, W]) for p in range(2)]
            p_yo = bank(ctx, "p_eyo", [P, R, D])
            cols1 = lambda c: slice(c * P, (c + 1) * P)
            cols2 = lambda c: slice(H0 + c * D, H0 + (c + 1) * D)

            w1_ready = sem("e_w1_ready")
            w2_ready = sem("e_w2_ready")
            gathered = pair("e_gathered")
            idx_ready = sem("e_idx_ready")
            x_done = sem("e_x_done")
            xh_ready = sem("e_xh_ready")
            xl_ready = sem("e_xl_ready")
            h_done = sem("e_h_done")
            hr_ready = sem("e_hr_ready")
            hh_ready = sem("e_hh_ready")
            hl_ready = sem("e_hl_ready")
            wh_ready = sem("e_wh_ready")
            y_done = sem("e_y_done")
            yt_ready = sem("e_yt_ready")
            yo_done = sem("e_yo_done")
            yo_ready = sem("e_yo_ready")
            stored = pair("e_stored")

            with nc.Block() as block:
                @block.sync
                def _(sp):
                    for dst, src in ((wgcn[:, :], w_gcn), (bgcn[:, :], b_gcn), (maskt[:, :], mask_t),
                                     (ws[:, :], w_s), (bs[:, :], b_s), (w1[:, :, :], e_w1), (w2[:, :, :], e_w2),
                                     (w3[:, :, :], e_w3), (be[:, :], b_e), (vraw[:, :, :], b_out),
                                     (gws[:, :], gw), (gbs[:, :], gb), (selraw[:, :, :, :], selp_d)):
                        sp.dma_start(dst, src).then_inc(c_loaded, 16)
                    dst = y_d.rearrange("(t p) d -> p t d", p=P)
                    with sp.Fori(0, NTP - 1, 2) as i:
                        for p in range(2):
                            sp.wait_ge(yo_ready, i + p + 1)
                            sp.dma_start(dst[:, bass.ds((i + p) * R, R), :], yo[p][:, :, :]).then_inc(stored[p], 16)
                    for p in range(2):
                        sp.wait_ge(stored[p], 8 * NTP + 1)
                    sp.wait_ge(c_loaded, 16 * NC)

                @block.gpsimd
                def _(pool):
                    def gather(j, p):
                        nc.gpsimd.tensor_copy(idx[p][:, :], ids[:, bass.ds(j * R, R)]).then_inc(idx_ready, 1)
                        pool.wait_ge(idx_ready, j + 1)
                        pool.sem_inc(passed, 1)
                        for k in range(R):
                            pool.indirect_dma_start(
                                out=xg[p][:, k, :], out_offset=None, in_=xln_d,
                                in_offset=bass.IndirectOffsetOnAxis(ap=idx[p][:, k:k + 1], axis=0))\
                                .then_inc(gathered[p], 16)

                    gather(0, 0)
                    gather(1, 1)
                    with pool.Fori(2, NTP - 1, 2) as i:
                        for p in range(2):
                            pool.wait_ge(x_done, i + p - 1)
                            gather(i + p, p)

                @block.scalar
                def _(act):
                    def evacuate(j, p):
                        act.wait_ge(x_done, j + 1)
                        nc.scalar.activation(xh[p][:, :], p_x[:, :, :].rearrange("p r d -> p (r d)"), ACT.Copy)\
                          .then_inc(xh_ready, 1)

                    def hidden(j, p, c):
                        act.wait_ge(h_done, HC * j + c + 1)
                        act.wait_ge(hl_ready, HC * j + c + 1)
                        nc.scalar.activation(hr[c % 2][:, :], p_h[c][:, :], ACT.Relu, bias=bc[p][:, c:c + 1])\
                          .then_inc(hr_ready, 1)
                        act.wait_ge(hr_ready, HC * j + c + 1)
                        nc.scalar.activation(hh[:, c, :], hr[c % 2][:, :], ACT.Copy).then_inc(hh_ready, 1)

                    def turned(j, i, p):
                        act.wait_ge(yo_done, j + 1)
                        act.wait_ge(stored[p], 8 * i + 1)
                        nc.scalar.activation(yo[p][:, :, :], p_yo[:, :, :], ACT.Copy).then_inc(yo_ready, 1)

                    def turn(i, p, after, before):
                        j = i + p
                        hidden(j, p, 0)
                        hidden(j, p, 1)
                        if after:
                            evacuate(j + 1, 1 - p)
                        hidden(j, p, 2)
                        if before:
                            turned(j - 1, i if p else i - 2, 1 - p)
                        hidden(j, p, 3)

                    evacuate(0, 0)
                    turn(0, 0, True, False)
                    turn(0, 1, True, True)
                    with act.Fori(2, NTP - 3, 2) as i:
                        turn(i, 0, True, True)
                        turn(i, 1, True, True)
                    turn(NTP - 2, 0, True, True)
                    turn(NTP - 2, 1, False, True)
                    turned(NTP - 1, NTP - 2, 1)

                @block.tensor
                def _(pe):
                    def transpose_x(j, p, half):
                        pe.wait_ge(gathered[p], half * 16 * R + 16 * R)
                        for k in range(R):
                            last = nc.tensor.transpose(p_x[:, k, :], xg[p][:, k, :], ident)
                        last.then_inc(x_done, 1)

                    def parts(dst, w_hi, w_lo, a_hi, a_lo, start, stop):
                        nc.tensor.matmul(dst, w_hi, a_hi, start=start, stop=False)
                        nc.tensor.matmul(dst, w_hi, a_lo, start=False, stop=False)
                        return nc.tensor.matmul(dst, w_lo, a_hi, start=False, stop=stop)

                    def up(j, p, c):
                        parts(p_h[c][:, :], wh[p][:, cols1(c)], wl[p][:, cols1(c)], xh[p][:, :], xl[p][:, :],
                              True, True).then_inc(h_done, 1)

                    def down(j, p, c):
                        pe.wait_ge(hl_ready, HC * j + c + 3)
                        last = parts(p_y[p][:, :], wh[p][:, cols2(c)], wl[p][:, cols2(c)], hh[:, c, :], hl[:, c, :],
                                     c == 0, c == HC - 1)
                        if c == HC - 1:
                            last.then_inc(y_done, 1)

                    def transpose_y(j, p):
                        pe.wait_ge(yt_ready, j + 1)
                        if not (isinstance(j, int) and j == 0):
                            pe.wait_ge(yo_ready, j)
                        for k in range(R):
                            last = nc.tensor.transpose(p_yo[:, k, :], yt[p][:, k * P:(k + 1) * P], ident)
                        last.then_inc(yo_done, 1)

                    def turn(i, p, after, before):
                        j = i + p
                        q = 1 - p
                        pe.wait_ge(w1_ready, j + 1)
                        pe.wait_ge(xl_ready, j + 1)
                        up(j, p, 0)
                        if before:
                            down(j - 1, q, 2)
                        up(j, p, 1)
                        if before:
                            down(j - 1, q, 3)
                        if after:
                            if isinstance(i, int):
                                transpose_x(j + 1, q, (j + 1) // 2)
                            else:
                                pe.wait_ge(gathered[q], (i + 2 * p) * (8 * R) + 16 * R)
                                for k in range(R):
                                    last = nc.tensor.transpose(p_x[:, k, :], xg[q][:, k, :], ident)
                                last.then_inc(x_done, 1)
                        up(j, p, 2)
                        pe.wait_ge(w2_ready, j + 1)
                        down(j, p, 0)
                        if before:
                            transpose_y(j - 1, q)
                        up(j, p, 3)
                        down(j, p, 1)

                    transpose_x(0, 0, 0)
                    turn(0, 0, True, False)
                    turn(0, 1, True, True)
                    with pe.Fori(2, NTP - 3, 2) as i:
                        turn(i, 0, True, True)
                        turn(i, 1, True, True)
                    turn(NTP - 2, 0, True, True)
                    turn(NTP - 2, 1, False, True)
                    down(NTP - 1, 1, 2)
                    down(NTP - 1, 1, 3)
                    transpose_y(NTP - 1, 1)

                @block.vector
                def _(dve):
                    dve.sem_inc(stored[0], 1)
                    dve.sem_inc(stored[1], 1)
                    dve.sem_inc(hl_ready, 2)

                    def take(j, p, w, half, ready):
                        cols = slice(half * H0, (half + 1) * H0)
                        nc.vector.tensor_copy(wh[p][:, cols], w[:, cols]).then_inc(wh_ready, 1)
                        dve.wait_ge(wh_ready, 2 * j + half + 1)
                        nc.vector.tensor_tensor(wl[p][:, cols], w[:, cols], wh[p][:, cols].bitcast(F32),
                                                ALU.subtract).then_inc(ready, 1)

                    def of_tile(j):
                        e = dve.value_load(texp[0:1, bass.ds(j, 1)], min_val=0, max_val=E0 - 1)
                        return wall[:, bass.ds(e, 1), :].rearrange("p a w -> p (a w)")

                    def take_1(j, p, w):
                        nc.vector.tensor_copy(bc[p][:, :], w[:, WW:EW])
                        take(j, p, w, 0, w1_ready)

                    def x_lo(j, p):
                        dve.wait_ge(xh_ready, j + 1)
                        nc.vector.tensor_tensor(xl[p][:, :], p_x[:, :, :].rearrange("p r d -> p (r d)"),
                                                xh[p][:, :].bitcast(F32), ALU.subtract).then_inc(xl_ready, 1)

                    def h_lo(j, c):
                        dve.wait_ge(hh_ready, HC * j + c + 1)
                        nc.vector.tensor_tensor(hl[:, c, :], hr[c % 2][:, :], hh[:, c, :].bitcast(F32), ALU.subtract)\
                          .then_inc(hl_ready, 1)

                    def rows(j, p):
                        dve.wait_ge(y_done, j + 1)
                        nc.vector.tensor_scalar(yt[p][:, :], p_y[p][:, :], bc[p][:, HC:HC + 1], None,
                                                ALU.add).then_inc(yt_ready, 1)

                    def turn(i, p, after, before):
                        j = i + p
                        q = 1 - p
                        if after and before:
                            w = of_tile(j + 1)
                        h_lo(j, 0)
                        if before:
                            rows(j - 1, q)
                        if after and before:
                            dve.wait_ge(yt_ready, j)
                            take_1(j + 1, q, w)
                        h_lo(j, 1)
                        if after:
                            x_lo(j + 1, q)
                        h_lo(j, 2)
                        if after and before:
                            take(j + 1, q, w, 1, w2_ready)
                        h_lo(j, 3)

                    for t in range(2):
                        w = of_tile(t)
                        take_1(t, t, w)
                        take(t, t, w, 1, w2_ready)
                    x_lo(0, 0)
                    turn(0, 0, True, False)
                    turn(0, 1, True, True)
                    with dve.Fori(2, NTP - 3, 2) as i:
                        turn(i, 0, True, True)
                        turn(i, 1, True, True)
                    turn(NTP - 2, 0, True, True)
                    turn(NTP - 2, 1, False, True)
                    rows(NTP - 1, 1)

        with ExitStack() as ctx:
            NB = B // R
            vout = alloc(ctx, "vout", [KV, R, D], F32R)
            selp = alloc(ctx, "selp", [2 * R * E1, R, 2, P], F32R)
            ones = alloc(ctx, "ones_l", [P, 1])
            at = [alloc(ctx, f"at{p}", [P, R, P]) for p in range(2)]
            yg = [alloc(ctx, f"yg{p}", [P, 2, R, D]) for p in range(2)]
            idx = [alloc(ctx, f"idx{p}", [P, 2, R], I32) for p in range(2)]
            st = [alloc(ctx, f"st_l{k}", [P, R, 6]) for k in range(2)]
            mv = [alloc(ctx, f"mv_l{k}", [P, R, 2]) for k in range(2)]
            pre = [alloc(ctx, f"pre_l{k}", [P, 2 * R]) for k in range(2)]
            root = [alloc(ctx, f"root_l{k}", [P, 2 * R]) for k in range(2)]
            rd = alloc(ctx, "rd", [P, R])
            nb = [alloc(ctx, f"nb{k}", [P, R]) for k in range(2)]
            dm = alloc(ctx, "dm", [P, R])
            xn = [alloc(ctx, f"xn{k}", [P, R, D]) for k in range(2)]
            x3t = alloc(ctx, "x3t", [P, W])
            x4t = alloc(ctx, "x4t", [P, W])
            gg = alloc(ctx, "gg", [P, R, D])
            gr = alloc(ctx, "gr", [P, R, D])
            hs = [alloc(ctx, f"hs{k}", [P, W]) for k in range(2)]
            he = [alloc(ctx, f"he{e}", [P, W]) for e in range(E1)]
            rp = [alloc(ctx, f"rp{k}", [P, W]) for k in range(2)]
            rc = [alloc(ctx, f"rc{k}", [P, W]) for k in range(2)]
            cw = alloc(ctx, "cw", [P, R, E1])
            cws = alloc(ctx, "cws", [P, P // (R * E1), R, E1], F32R)
            cwt = alloc(ctx, "cwt", [KV, P], F32R)
            outx = [alloc(ctx, f"outx{p}", [P, R, D]) for p in range(2)]
            sm = [alloc(ctx, f"sm{k}", [P, R, E1]) for k in range(6)]
            sv = [alloc(ctx, f"sv{k}", [P, R]) for k in range(8)]
            p_h = [bank(ctx, f"p_lh{k}", [P, W]) for k in range(2)]
            p_t = bank(ctx, "p_lt", [P, R, D])
            p_hl = bank(ctx, "p_hl", [P, R, D])
            p_ag = bank(ctx, "p_ag", [P, R, D])
            p_sm = bank(ctx, "p_sm", [P, 512])
            p_cb = bank(ctx, "p_cb", [P, R, D])
            p_out = bank(ctx, "p_out", [P, R, D])
            LG, CT = 16, P
            flat = lambda t: t[:, :, :].rearrange("p r d -> p (r d)")

            set_ = sem("l_set")
            v_s = sem("l_v_s")
            cw_s = sem("l_cw_s")
            a_loaded = pair("l_a_loaded")
            gathered = pair("l_gathered")
            idx_ready = sem("l_idx_ready")
            a_ready = sem("l_a_ready")
            x2_ready = sem("l_x2_ready")
            deg_done = sem("l_deg_done")
            pre_ready = [sem(f"l_pre_ready{k}") for k in range(2)]
            root_done = [sem(f"l_root_done{k}") for k in range(2)]
            nb_ready = [sem(f"l_nb_ready{k}") for k in range(2)]
            ln = [sem(f"l_norm_steps{k}") for k in range(2)]
            x3_ready = sem("l_x3_ready")
            rd_ready = sem("l_rd_ready")
            weigh = sem("l_weigh_steps")
            sx = sem("l_router_steps")
            xn_ready = [sem(f"l_xn_ready{k}") for k in range(2)]
            t_done = sem("l_t_done")
            x3t_ready = sem("l_x3t_ready")
            x4t_ready = sem("l_x4t_ready")
            hl_done = sem("l_hl_done")
            gg_ready = sem("l_gg_ready")
            ag_done = sem("l_ag_done")
            gr_ready = sem("l_gr_ready")
            lg_done = sem("l_lg_done")
            d_ready = sem("l_d_ready")
            exp_done = sem("l_exp_done")
            cw_ready = sem("l_cw_ready")
            ct_done = sem("l_ct_done")
            cwt_ready = sem("l_cwt_ready")
            cb_done = sem("l_cb_done")
            h_done = sem("l_h_done")
            h_ready = sem("l_h_ready")
            rc_ready = sem("l_rc_ready")
            out_done = sem("l_out_done")
            out_ready = sem("l_out_ready")
            stored = pair("l_stored")
            SX = 17

            with nc.Block() as block:
                @block.sync
                def _(sp):
                    def load(j, p):
                        sp.dma_start(at[p][:, :, :], a_t[:, bass.ds(R * j, R), :]).then_inc(a_loaded[p], 16)

                    def store(j, p):
                        sp.wait_ge(out_ready, j + 2)
                        sp.dma_start(out.rearrange("b n d -> n b d")[:, bass.ds(R * j, R), :], outx[p][:, :, :])\
                          .then_inc(stored[p], 16)

                    load(0, 0)
                    load(1, 1)
                    sp.wait_ge(ag_done, 1)
                    load(2, 0)
                    with sp.Fori(0, NB - 5, 2) as i:
                        for p in range(2):
                            sp.wait_ge(ag_done, i + p + 2)
                            load(i + p + 3, 1 - p)
                            store(i + p, p)
                    sp.wait_ge(ag_done, NB - 2)
                    load(NB - 1, 1)
                    for j in range(NB - 4, NB):
                        store(j, j % 2)
                    for p in range(2):
                        sp.wait_ge(stored[p], 8 * NB + 1)

                @block.gpsimd
                def _(pool):
                    def gather(j, p):
                        nc.gpsimd.tensor_copy(idx[p][:, :, :], pos_i[:, :, bass.ds(R * j, R)]).then_inc(idx_ready, 1)
                        pool.wait_ge(idx_ready, j + 1)
                        pool.sem_inc(passed, 1)
                        for c in range(2):
                            for k in range(R):
                                pool.indirect_dma_start(
                                    out=yg[p][:, c, k, :], out_offset=None, in_=y_d,
                                    in_offset=bass.IndirectOffsetOnAxis(ap=idx[p][:, c, k:k + 1], axis=0))\
                                    .then_inc(gathered[p], 16)

                    def plus_one(j, p, n):
                        pool.wait_ge(a_loaded[p], n)
                        nc.gpsimd.tensor_tensor(at[p][:, :, :], at[p][:, :, :],
                                                ident.unsqueeze(1).to_broadcast([P, R, P]), ALU.add)\
                          .then_inc(a_ready, 1)

                    def roots(n, k):
                        pool.wait_ge(pre_ready[k], n)
                        w = (2 - k) * R
                        nc.gpsimd.tensor_tensor(root[k][:, 0:w], pre[k][:, 0:w], mhalf[:, 0:w], ALU.pow)\
                          .then_inc(root_done[k], 1)

                    gather(0, 0)
                    plus_one(0, 0, 16)
                    gather(1, 1)
                    plus_one(1, 1, 16)
                    roots(1, 0)
                    pool.wait_ge(x2_ready, 2)
                    gather(2, 0)
                    with pool.Fori(1, NB - 4, 2) as i:
                        for p in range(2):
                            j = i + p
                            plus_one(j + 1, p, 8 * i + 24)
                            roots(j, 1)
                            roots(j + 1, 0)
                            pool.wait_ge(x2_ready, 2 * j + 2)
                            gather(j + 2, 1 - p)
                    plus_one(NB - 2, 0, 8 * NB)
                    roots(NB - 3, 1)
                    roots(NB - 2, 0)
                    pool.wait_ge(x2_ready, 2 * (NB - 3) + 2)
                    gather(NB - 1, 1)
                    plus_one(NB - 1, 1, 8 * NB)
                    for j in (NB - 2, NB - 1):
                        roots(j, 1)
                        roots(j + 1, 0)
                    roots(NB, 1)

                @block.scalar
                def _(act):
                    act.sem_inc(stored[0], 1)
                    act.sem_inc(stored[1], 1)
                    act.wait_ge(set_, 2)

                    def relu(c, u, dst, bias):
                        act.wait_ge(h_done, 8 * c + u + 1)
                        nc.scalar.activation(dst, p_h[u % 2][:, :], ACT.Relu, bias=bias).then_inc(h_ready, 1)

                    def normalise(j, k, scale):
                        act.wait_ge(nb_ready[k], j + 1)
                        act.sem_inc(passed, 1)
                        for r in range(R):
                            last = nc.scalar.activation(
                                xn[k][:, r, :], xtok[:, bass.ds(R * j + r, 1), :].rearrange("p a d -> p (a d)"),
                                ACT.Identity, scale=scale[:, r:r + 1], bias=nb[k][:, r:r + 1])
                        last.then_inc(xn_ready[k], 1)

                    def body(i, p, first, middle, back):
                        j = i + p
                        if middle:
                            act.wait_ge(t_done, 2 * j - 1)
                            nc.scalar.activation(x3t[:, :], flat(p_t), ACT.Copy).then_inc(x3t_ready, 1)
                        if back:
                            relu(j - 2, 0, he[0][:, :], be[:, 0:1])
                            act.wait_ge(d_ready, 2 * j - 3)
                            nc.scalar.activation(sm[1][:, :, :], sm[1][:, :, :], ACT.Exp).then_inc(exp_done, 1)
                            relu(j - 2, 1, he[1][:, :], be[:, 1:2])
                        if middle:
                            act.wait_ge(ag_done, j)
                            for k in range(R):
                                last = nc.scalar.activation(gr[:, k, :], p_ag[:, k, :], ACT.Relu, scale=dm[:, k:k + 1])
                            last.then_inc(gr_ready, 1)
                        if back:
                            relu(j - 2, 2, he[2][:, :], be[:, 2:3])
                            relu(j - 2, 3, he[3][:, :], be[:, 3:4])
                            act.wait_ge(d_ready, 2 * j - 2)
                            nc.scalar.activation(sv[4][:, :], sv[4][:, :], ACT.Exp).then_inc(exp_done, 1)
                            relu(j - 2, 4, hs[0][:, :], bs[:, 0:1])
                            relu(j - 2, 5, rp[0][:, :], be[:, E1:E1 + 1])
                            relu(j - 2, 6, rp[1][:, :], be[:, E1 + 1:E1 + 2])
                            act.wait_ge(ct_done, j - 1)
                            nc.scalar.activation(cwt[0:3 * R * E1, :], p_sm[0:3 * R * E1, CT:CT + P], ACT.Copy)\
                              .then_inc(cwt_ready, 1)
                            relu(j - 2, 7, hs[1][:, :], bs[:, 1:2])
                        if middle:
                            normalise(j - 1, 1, root[1])
                            act.wait_ge(t_done, 2 * j)
                            nc.scalar.activation(x4t[:, :], flat(p_t), ACT.Copy).then_inc(x4t_ready, 1)
                        if first:
                            normalise(j, 0, rd)

                    turns3(act, NB, body)

                @block.tensor
                def _(pe):
                    def product(c, u, mms):
                        pe.wait_ge(h_ready, 8 * c + u + 1)
                        for dst, lhs, rhs in mms:
                            last = nc.tensor.matmul(dst, lhs, rhs, start=True, stop=True)
                        last.then_inc(h_done, 1)

                    def spread(dst, pair_):
                        for k in range(R):
                            last = nc.tensor.matmul(dst[:, k, :], selp[:, k, pair_, :], cwt[0:2 * R * E1, :],
                                                    start=True, stop=True)
                        last.then_inc(cb_done, 1)

                    def up(c, e):
                        product(c, e, [(p_h[e % 2][:, :], w1[:, e, :], x4t[:, :])])

                    def second(c, u, pair_):
                        a = 2 * pair_
                        product(c, u, [(p_h[u % 2][0:64, :], w2[:, a, :], he[a][:, :]),
                                       (p_h[u % 2][64:128, :], w2[:, a + 1, :], he[a + 1][:, :])])

                    def body(i, p, first, middle, back):
                        j = i + p
                        c = j - 2
                        q = 1 - p
                        if middle:
                            pe.wait_ge(xn_ready[0], j)
                            for k in range(R):
                                last = nc.tensor.transpose(p_t[:, k, :], xn[0][:, k, :], ident)
                            last.then_inc(t_done, 1)
                        if back:
                            up(c, 0)
                        if middle:
                            pe.wait_ge(x3t_ready, j)
                            for k in range(R):
                                last = nc.tensor.matmul(p_hl[:, k, :], x3t[:, k * P:(k + 1) * P], wgcn[:, :],
                                                        start=True, stop=True)
                            last.then_inc(hl_done, 1)
                        if first:
                            if back:
                                pe.wait_ge(sx, SX * c + 1)
                            pe.wait_ge(a_ready, j + 1)
                            for k in range(R):
                                last = nc.tensor.matmul(p_sm[:, k:k + 1], at[p][:, k, :], ones[:, :],
                                                        start=True, stop=True)
                            last.then_inc(deg_done, 1)
                        if back:
                            up(c, 1)
                        if middle:
                            pe.wait_ge(gg_ready, j)
                            for k in range(R):
                                last = nc.tensor.matmul(p_ag[:, k, :], at[q][:, k, :], gg[:, k, :],
                                                        start=True, stop=True)
                            last.then_inc(ag_done, 1)
                        if back:
                            up(c, 2)
                            up(c, 3)
                            product(c, 4, [(p_h[0][:, :], ws[:, 0:P], x4t[:, :])])
                        if back:
                            second(c, 5, 0)
                            second(c, 6, 1)
                            product(c, 7, [(p_h[1][:, :], ws[:, P:2 * P], hs[0][:, :])])
                            pe.wait_ge(cw_ready, j - 1)
                            nc.tensor.transpose(p_sm[:, CT:CT + P],
                                                cws[:, :, :, :].rearrange("p c r e -> p (c r e)").bitcast(F32),
                                                ident).then_inc(ct_done, 1)
                            pe.wait_ge(cwt_ready, j - 1)
                            spread(p_cb, 0)
                            spread(p_hl, 1)
                            pe.wait_ge(out_ready, c + 1)
                            nc.tensor.matmul(flat(p_out), cwt[:, :], flat(vout), start=True, stop=False)
                            pe.wait_ge(h_ready, 8 * c + 10)
                            for k in range(R):
                                nc.tensor.matmul(p_out[:, k, :], hs[1][:, k * P:(k + 1) * P], ws[:, 2 * P:3 * P],
                                                 start=False, stop=False)
                        if middle:
                            pe.wait_ge(xn_ready[1], j)
                            for k in range(R):
                                last = nc.tensor.transpose(p_t[:, k, :], xn[1][:, k, :], ident)
                            last.then_inc(t_done, 1)
                        if back:
                            for u in range(2):
                                pe.wait_ge(rc_ready, 2 * c + u + 1)
                                for k in range(R):
                                    last = nc.tensor.matmul(p_out[:, k, :], rc[u][:, k * P:(k + 1) * P], w3[:, u, :],
                                                            start=False, stop=(u == 1 and k == R - 1))
                            last.then_inc(out_done, 1)
                        if middle:
                            pe.wait_ge(x4t_ready, j)
                            for k in range(R):
                                last = nc.tensor.matmul(p_sm[:, LG + k * E1:LG + (k + 1) * E1],
                                                        x4t[:, k * P:(k + 1) * P], gws[:, :], start=True, stop=True)
                            last.then_inc(lg_done, 1)

                    pe.wait_ge(set_, 4)
                    turns3(pe, NB, body)

                @block.vector
                def _(dve):
                    dve.sem_inc(h_ready, 2)
                    dve.sem_inc(out_ready, 1)
                    nc.vector.memset(ones[:, :], 1.0).then_inc(set_, 1)
                    nc.vector.memset(outx[1][:, 0, :], 1.0)
                    nc.vector.memset(outx[0][:, 0, :], 0.0).then_inc(v_s, 1)
                    dve.wait_ge(v_s, 1)
                    nc.vector.tensor_copy(cwt[:, :], outx[1][0:KV, 0, :])
                    nc.vector.tensor_copy(cws[:, :, :, :].rearrange("p c r e -> p (c r e)"), outx[0][:, 0, :])\
                      .then_inc(set_, 1)
                    nc.vector.tensor_copy(selp[:, :, :, :], selraw[:, :, :, :])
                    nc.vector.tensor_copy(vout[:, :, :], vraw[:, :, :]).then_inc(v_s, 1)
                    dve.wait_ge(v_s, 2)
                    for a, b in ((32, 64), (96, 97)):
                        hi = vout[a:b, :, :].bitcast(F32)
                        nc.vector.tensor_tensor(vout[a:b, :, :], vraw[a:b, :, :], hi, ALU.subtract)\
                          .then_inc(set_, 1)
                    pri = cf[:, CF_PRI + E0 - E1:CF_PRI + E0].unsqueeze(1).to_broadcast([P, R, E1])
                    over = lambda v: v[:, :].unsqueeze(2).to_broadcast([P, R, E1])
                    row = lambda j, r: xtok[:, bass.ds(R * j + r, 1), :].rearrange("p a d -> p (a d)")

                    def largest(src, v):
                        return nc.vector.tensor_reduce(v[:, :], src[:, :, :], AX.X, ALU.max)

                    def same(dst, src, v):
                        return nc.vector.tensor_tensor(dst[:, :, :], src[:, :, :], over(v), ALU.is_equal)

                    def times(dst, src, w):
                        return nc.vector.tensor_tensor(dst[:, :, :], src[:, :, :], w, ALU.mult)

                    def body(i, p, first, middle, back):
                        j = i + p
                        b = j - 1

                        def router(ins):
                            ins.then_inc(sx, 1)

                        def after(n):
                            dve.wait_ge(sx, SX * (j - 2) + n)

                        def choice(c, r):
                            ins = nc.vector.scalar_tensor_tensor(row(j, r), yg[p][:, c, r, :],
                                                                 prob[:, c, bass.ds(R * j + r, 1)], row(j, r),
                                                                 ALU.mult, ALU.add)
                            if r == R - 1:
                                ins.then_inc(x2_ready, 1)

                        def gcn_rows(r):
                            ins = nc.vector.scalar_tensor_tensor(gg[:, r, :], bgcn[:, :],
                                                                 root[0][:, R + r:R + r + 1], p_hl[:, r, :],
                                                                 ALU.mult, ALU.add)
                            if r == R - 1:
                                ins.then_inc(gg_ready, 1)

                        def stats(n, k, r):
                            ins = nc.vector.bn_stats(st[k][:, r, :], row(n, r))
                            if r == R - 1:
                                ins.then_inc(ln[k], 1)

                        if back:
                            dve.wait_ge(lg_done, j - 1)
                            router(nc.vector.tensor_tensor(sm[0][:, :, :],
                                                           p_sm[:, LG:LG + R * E1].rearrange("p (r e) -> p r e", e=E1),
                                                           gbs[:, :].unsqueeze(1).to_broadcast([P, R, E1]), ALU.add))
                        if first:
                            dve.wait_ge(gathered[p], 64 * i + 128)
                            choice(0, 0)
                        if back:
                            after(1)
                            router(largest(sm[0], sv[0]))
                        if first:
                            choice(0, 1)
                        if back:
                            after(2)
                            nc.vector.tensor_tensor(sm[1][:, :, :], sm[0][:, :, :], over(sv[0]), ALU.subtract)\
                              .then_inc(d_ready, 1)
                        if first:
                            choice(0, 2)
                        if middle:
                            dve.wait_ge(hl_done, j)
                            gcn_rows(0)
                            gcn_rows(1)
                        if back:
                            dve.wait_ge(exp_done, 2 * j - 3)
                            router(nc.vector.tensor_reduce(sv[1][:, :], sm[1][:, :, :], AX.X, ALU.add))
                        if middle:
                            gcn_rows(2)
                        if back:
                            after(3)
                            router(nc.vector.reciprocal(sv[1][:, :], sv[1][:, :]))
                        if middle:
                            gcn_rows(3)
                        if back:
                            after(4)
                            router(times(sm[2], sm[1], over(sv[1])))
                        if first:
                            choice(0, 3)
                        if back:
                            after(5)
                            router(largest(sm[2], sv[2]))
                        if first:
                            dve.wait_ge(deg_done, j + 1)
                            nc.vector.tensor_scalar(pre[0][:, R:2 * R], p_sm[:, 0:R], 1e-8, None, ALU.add)
                            dve.wait_ge(x2_ready, 2 * j + 1)
                            choice(1, 0)
                        if back:
                            after(6)
                            router(same(sm[4], sm[2], sv[2]))
                        if first:
                            choice(1, 1)
                        if back:
                            after(7)
                            router(times(sm[4], sm[4], pri))
                        if first:
                            choice(1, 2)
                        if back:
                            after(8)
                            router(largest(sm[4], sv[7]))
                        if first:
                            choice(1, 3)
                        if back:
                            after(9)
                            router(same(sm[3], sm[4], sv[7]))
                        if first:
                            dve.wait_ge(x2_ready, 2 * j + 2)
                            dve.sem_inc(passed, 1)
                            stats(j, 0, 0)
                        if back:
                            after(10)
                            router(nc.vector.scalar_tensor_tensor(flat(sm[2]), flat(sm[3]), BIG, flat(sm[2]),
                                                                  ALU.mult, ALU.add))
                        if first:
                            stats(j, 0, 1)
                        if back:
                            after(11)
                            router(largest(sm[2], sv[3]))
                        if middle:
                            dve.wait_ge(gr_ready, j)
                            batch = xtok[:, bass.ds(R * b, R), :]
                            nc.vector.tensor_tensor(batch, batch, gr[:, :, :], ALU.add).then_inc(x3_ready, 1)
                        if back:
                            after(12)
                            nc.vector.tensor_tensor(sv[4][:, :], sv[3][:, :], sv[2][:, :], ALU.subtract)\
                              .then_inc(d_ready, 1)
                            router(same(sm[4], sm[2], sv[3]))
                        if middle:
                            dve.wait_ge(x3_ready, j)
                            dve.sem_inc(passed, 1)
                            stats(b, 1, 0)
                        if back:
                            after(13)
                            router(times(sm[4], sm[4], pri))
                        if middle:
                            stats(b, 1, 1)
                        if back:
                            after(14)
                            router(largest(sm[4], sv[7]))
                        if middle:
                            stats(b, 1, 2)
                        if back:
                            dve.wait_ge(exp_done, 2 * j - 2)
                            router(nc.vector.tensor_scalar(sv[5][:, :], sv[4][:, :], 1.0, None, ALU.add))
                        if middle:
                            stats(b, 1, 3)
                        if back:
                            after(16)
                            nc.vector.reciprocal(sv[5][:, :], sv[5][:, :])
                            router(same(sm[5], sm[4], sv[7]))
                        if middle:
                            dve.wait_ge(ln[1], 2 * j - 1)
                            dve.sem_inc(passed, 1)
                            for r in range(R):
                                last = nc.vector.bn_aggr(mv[1][:, r, :], st[1][:, r, :])
                            last.then_inc(ln[1], 1)
                        if back:
                            after(17)
                            times(sm[3], sm[3], over(sv[5]))
                            nc.vector.tensor_tensor(sv[6][:, :], sv[4][:, :], sv[5][:, :], ALU.mult)\
                              .then_inc(weigh, 1)
                        if middle:
                            dve.wait_ge(ln[1], 2 * j)
                            nc.vector.tensor_scalar(pre[1][:, 0:R], mv[1][:, :, 1], 1e-5, None, ALU.add)\
                              .then_inc(pre_ready[1], 1)
                        if back:
                            dve.wait_ge(weigh, 2 * j - 3)
                            times(sm[5], sm[5], over(sv[6])).then_inc(weigh, 1)
                        if first:
                            stats(j, 0, 2)
                        if back:
                            dve.wait_ge(weigh, 2 * j - 2)
                            nc.vector.tensor_tensor(cw[:, :, :], sm[3][:, :, :], sm[5][:, :, :], ALU.add)\
                              .then_inc(cw_s, 1)
                        if first:
                            stats(j, 0, 3)
                        if back:
                            dve.wait_ge(cw_s, 2 * j - 3)
                            nc.vector.tensor_copy(cws[:, 0, :, :], cw[:, :, :])
                            nc.vector.tensor_copy(cws[:, 2, :, :], cw[:, :, :]).then_inc(cw_s, 1)
                        if first:
                            dve.wait_ge(ln[0], 2 * j + 1)
                            dve.sem_inc(passed, 1)
                            for r in range(R):
                                last = nc.vector.bn_aggr(mv[0][:, r, :], st[0][:, r, :])
                            last.then_inc(ln[0], 1)
                        if back:
                            dve.wait_ge(cw_s, 2 * j - 2)
                            nc.vector.tensor_tensor(cws[:, 1, :, :], cw[:, :, :], cws[:, 0, :, :].bitcast(F32),
                                                    ALU.subtract).then_inc(cw_ready, 1)
                        if first:
                            dve.wait_ge(ln[0], 2 * j + 2)
                            nc.vector.tensor_scalar(pre[0][:, 0:R], mv[0][:, :, 1], 1e-5, None, ALU.add)\
                              .then_inc(pre_ready[0], 1)
                        if middle:
                            dve.wait_ge(root_done[1], j)
                            nc.vector.scalar_tensor_tensor(nb[1][:, :], mv[1][:, :, 0], -1.0, root[1][:, 0:R],
                                                           ALU.mult, ALU.mult).then_inc(nb_ready[1], 1)
                        if back:
                            dve.wait_ge(h_ready, 8 * j - 8)
                            dve.wait_ge(cb_done, 2 * j - 3)
                            nc.vector.tensor_tensor(rc[0][:, :], rp[0][:, :], flat(p_cb), ALU.mult)\
                              .then_inc(rc_ready, 1)
                        if back:
                            dve.wait_ge(h_ready, 8 * j - 7)
                            dve.wait_ge(cb_done, 2 * j - 2)
                            nc.vector.tensor_tensor(rc[1][:, :], rp[1][:, :], flat(p_hl), ALU.mult)\
                              .then_inc(rc_ready, 1)
                        if first:
                            dve.wait_ge(root_done[0], j + 1)
                            nc.vector.tensor_tensor(dm[:, :], root[0][:, R:2 * R], maskt[:, bass.ds(R * j, R)],
                                                    ALU.mult)
                            nc.vector.tensor_tensor(rd[:, :], root[0][:, 0:R], root[0][:, R:2 * R], ALU.mult)\
                              .then_inc(rd_ready, 1)
                            dve.wait_ge(rd_ready, j + 1)
                            nc.vector.scalar_tensor_tensor(nb[0][:, :], mv[0][:, :, 0], -1.0, rd[:, :],
                                                           ALU.mult, ALU.mult).then_inc(nb_ready[0], 1)
                        if back:
                            dve.wait_ge(out_done, j - 1)
                            dve.wait_ge(stored[p], 8 * i - 15)
                            nc.vector.tensor_tensor(outx[p][:, :, :], xtok[:, bass.ds(R * (j - 2), R), :],
                                                    p_out[:, :, :], ALU.add).then_inc(out_ready, 1)

                    turns3(dve, NB, body)




def layout(x, adj, nodemask, L0_gnn_W1, L0_gnn_b1, L0_gnn_W2, L0_gnn_b2, L0_gnn_fusion_w, L0_ffn_Wg, L0_ffn_bg,
           L0_ffn_W1, L0_ffn_b1, L0_ffn_W2, L0_ffn_b2, L1_gnn_W, L1_gnn_b, L1_ffn_sW1, L1_ffn_sb1, L1_ffn_sW2,
           L1_ffn_sb2, L1_ffn_sW3, L1_ffn_sb3, L1_ffn_eW1, L1_ffn_eb1, L1_ffn_eW2, L1_ffn_eb2, L1_ffn_eW3,
           L1_ffn_eb3, L1_ffn_gW, L1_ffn_gb):
    f = np.float32
    every = lambda v, n=P: np.broadcast_to(v.reshape(1, -1), (n, v.size))
    x_grp = np.zeros((NGB, P, R, D), f)
    a_grp = np.zeros((NGB, P, R, P), f)
    w_grp = np.zeros((NGB, P, GWID), f)
    j = 0
    for g, nodes in enumerate(GROUPS):
        n, per = GN[g], GPT[g]
        for b in range(GB[g]):
            for k in range(R):
                first = (b * R + k) * per
                for s, graph in enumerate(range(first, min(first + per, B))):
                    r = slice(s * n, (s + 1) * n)
                    x_grp[j, r, k, :] = x[graph][nodes]
                    a_grp[j, r, k, r] = adj[graph][np.ix_(nodes, nodes)].T
            w_grp[j] = np.concatenate([
                L0_gnn_W1[g], L0_gnn_W2[g].reshape(2, P, D).transpose(1, 0, 2).reshape(P, 2 * D),
                L0_gnn_b1[g].reshape(2, P).T, every(L0_gnn_b2[g])], axis=1)
            j += 1
    w_exp = np.concatenate([
        L0_ffn_W1.transpose(2, 0, 1),
        L0_ffn_W2.reshape(E0, D, HC, P).transpose(3, 0, 2, 1).reshape(P, E0, HC * D),
        L0_ffn_b1.reshape(E0, HC, P).transpose(2, 0, 1),
        L0_ffn_b2.T.reshape(P, E0, 1),
        np.zeros((P, E0, 1), f)], axis=2)
    b_out = np.zeros((KV, R, D), f)
    for k in range(R):
        for c in range(3):
            b_out[(c * R + k) * E1:(c * R + k + 1) * E1, k, :] = L1_ffn_eb3
        b_out[2 * 32, k, :] = b_out[3 * 32, k, :] = L1_ffn_sb3
    cf, ch, sel, selp = consts()
    return {
        "x_tok": x.transpose(1, 0, 2), "x_grp": x_grp, "a_grp": a_grp, "w_grp": w_grp,
        "fus": every(L0_gnn_fusion_w), "wg": L0_ffn_Wg.T, "bg": every(L0_ffn_bg), "w_exp": w_exp,
        "a_t": adj.transpose(2, 0, 1), "w_gcn": L1_gnn_W.T, "b_gcn": every(L1_gnn_b), "mask_t": nodemask.T,
        "w_s": np.concatenate([L1_ffn_sW1, L1_ffn_sW2, L1_ffn_sW3], axis=1),
        "b_s": np.stack([L1_ffn_sb1, L1_ffn_sb2], axis=1),
        "e_w1": L1_ffn_eW1.transpose(1, 0, 2), "e_w2": L1_ffn_eW2.transpose(1, 0, 2),
        "e_w3": L1_ffn_eW3.reshape(2, P, D).transpose(1, 0, 2),
        "b_e": np.concatenate([L1_ffn_eb1.T, L1_ffn_eb2.reshape(2, P).T], axis=1),
        "b_out": b_out, "gw": L1_ffn_gW, "gb": every(L1_ffn_gb),
        "cf_d": cf, "ch_d": ch, "sel_d": sel, "selp_d": selp,
    }


def kernel(**inputs):
    import concourse.bacc as bacc
    from concourse.bass_utils import run_bass_kernel_spmd

    nc = bacc.Bacc("TRN2", target_bir_lowering=False, num_devices=1)
    arrays, args = {}, []
    for name, a in layout(**{k: np.asarray(v) for k, v in inputs.items()}).items():
        arrays["in_" + name] = np.ascontiguousarray(a)
        args.append(nc.dram_tensor("in_" + name, a.shape, mybir.dt.from_np(a.dtype), kind="ExternalInput").ap())
    out = nc.dram_tensor("out_0", (B, N, D), F32, kind="ExternalOutput").ap()
    build(nc, *args, out)
    r = run_bass_kernel_spmd(nc, [arrays], core_ids=[0])
    return r.results[0]["out_0"]
```
